# Optimizing a Trainium2 kernel written in Bass

```python
import numpy as np
import jax
import jax.numpy as jnp

def _softmax(x, axis=-1):
    return jax.nn.softmax(x, axis=axis)

def _gelu(x):
    return jax.nn.gelu(x, approximate=True)

def _silu(x):
    return jax.nn.silu(x)

def _sigmoid(x):
    return jax.nn.sigmoid(x)

def _layernorm(x, axis=-1, eps=1e-05):
    m = jnp.mean(x, axis=axis, keepdims=True)
    v = jnp.var(x, axis=axis, keepdims=True)
    return (x - m) / jnp.sqrt(v + eps)

def _scatter_add(tgt, idx, src, axis=0):
    return tgt.at[idx].add(src)

def _segment_sum(src, seg, n):
    return jax.ops.segment_sum(src, seg, n)
kernel_name = 'mk_conv_preact_d2_conv_nhwc768_r2_d5494c'

def setup_inputs(seed: int=0):
    np.random.seed(seed)
    _w = jnp.asarray

    def _rec_inputs():
        import jax
        import jax.numpy as jnp
        _gk = jax.random.key(seed)
        x = 7.572e-06 + 1 * jax.random.normal(jax.random.fold_in(_gk, 1), (32, 14, 14, 384), jnp.float32)
        return x
    x = _rec_inputs()

    def _L0_conv_setup():
        import jax, jax.numpy as jnp
        import numpy as np
        B, H, W, C = (32, 14, 14, 384)
        key = jax.random.key(seed)
        k = jax.random.split(key, 5)
        s = 0.02
        return {'x': jax.random.normal(k[0], (B, H, W, C), dtype=jnp.float32), 'Wx': jax.random.normal(k[1], (3 * C, C), dtype=jnp.float32) * s, 'bx': jnp.zeros((3 * C,), dtype=jnp.float32), 'Wh': jax.random.normal(k[2], (3 * C, C), dtype=jnp.float32) * s, 'bh': jnp.zeros((3 * C,), dtype=jnp.float32), 'Wp': jax.random.normal(k[3], (C, C), dtype=jnp.float32) * s}
    _L0_conv_all = _L0_conv_setup()
    _L0_conv_in = {k: v for k, v in _L0_conv_all.items() if k in ('Wx', 'bx', 'Wh', 'bh', 'Wp')}
    del _L0_conv_all

    def _L1_conv_setup():
        import jax, jax.numpy as jnp
        import numpy as np
        B_, H_, W_, DM = (4, 32, 32, 384)
        DI = int(0.5 * DM)
        N = 16
        R = -(-DM // 16)
        K = 4

        def selective_scan(xs, dts, As, Bs, Cs, Dsk):
            u = jnp.moveaxis(xs, -1, 0)
            d = jnp.moveaxis(dts, -1, 0)
            Bt = jnp.moveaxis(Bs, -1, 0)
            Ct = jnp.moveaxis(Cs, -1, 0)

            def step(h, inp):
                u_t, d_t, B_t, C_t = inp
                dA = jnp.exp(d_t[..., None] * As)
                h = h * dA + (d_t * u_t)[..., None] * B_t[:, :, None, :]
                y = jnp.einsum('bkcn,bkn->bkc', h, C_t)
                return (h, y)
            h0 = jnp.zeros(u.shape[1:] + (As.shape[-1],), u.dtype)
            _, ys = jax.lax.scan(step, h0, (u, d, Bt, Ct))
            ys = jnp.moveaxis(ys, 0, -1)
            return ys + Dsk[None, :, :, None] * xs
        key = jax.random.key(seed)
        ks = jax.random.split(key, 8)
        s = lambda i, shape, sc=0.02: jax.random.normal(ks[i], shape, jnp.float32) * sc
        return dict(x=jax.random.normal(ks[0], (B_, H_, W_, DM), jnp.float32), in_proj_w=s(1, (2 * DI, DM)), conv_w=s(2, (DI, 1, 3, 3)), conv_b=jnp.zeros((DI,), jnp.float32), x_proj_w=s(3, (K, R + 2 * N, DI)), dt_projs_w=s(4, (K, DI, R)), dt_projs_b=s(5, (K, DI)), A_logs=jnp.log(jnp.tile(jnp.arange(1, N + 1, dtype=jnp.float32)[None, :], (K * DI, 1))), Ds=jnp.ones((K * DI,), jnp.float32), out_norm_g=jnp.ones((DI,), jnp.float32), out_norm_b=jnp.zeros((DI,), jnp.float32), out_proj_w=s(6, (DM, DI)))
    _L1_conv_all = _L1_conv_setup()
    _L1_conv_in = {k: v for k, v in _L1_conv_all.items() if k in ('in_proj_w', 'conv_w', 'conv_b', 'x_proj_w', 'dt_projs_w', 'dt_projs_b', 'A_logs', 'Ds', 'out_norm_g', 'out_norm_b', 'out_proj_w')}
    del _L1_conv_all
    return {'x': x, 'L0_conv_Wx': _L0_conv_in['Wx'], 'L0_conv_bx': _L0_conv_in['bx'], 'L0_conv_Wh': _L0_conv_in['Wh'], 'L0_conv_bh': _L0_conv_in['bh'], 'L0_conv_Wp': _L0_conv_in['Wp'], 'L1_conv_in_proj_w': _L1_conv_in['in_proj_w'], 'L1_conv_conv_w': _L1_conv_in['conv_w'], 'L1_conv_conv_b': _L1_conv_in['conv_b'], 'L1_conv_x_proj_w': _L1_conv_in['x_proj_w'], 'L1_conv_dt_projs_w': _L1_conv_in['dt_projs_w'], 'L1_conv_dt_projs_b': _L1_conv_in['dt_projs_b'], 'L1_conv_A_logs': _L1_conv_in['A_logs'], 'L1_conv_Ds': _L1_conv_in['Ds'], 'L1_conv_out_norm_g': _L1_conv_in['out_norm_g'], 'L1_conv_out_norm_b': _L1_conv_in['out_norm_b'], 'L1_conv_out_proj_w': _L1_conv_in['out_proj_w']}

def reference(x, L0_conv_Wx, L0_conv_bx, L0_conv_Wh, L0_conv_bh, L0_conv_Wp, L1_conv_in_proj_w, L1_conv_conv_w, L1_conv_conv_b, L1_conv_x_proj_w, L1_conv_dt_projs_w, L1_conv_dt_projs_b, L1_conv_A_logs, L1_conv_Ds, L1_conv_out_norm_g, L1_conv_out_norm_b, L1_conv_out_proj_w):
    import jax
    import jax.numpy as jnp

    def _L0_conv_ref(x, Wx, bx, Wh, bh, Wp):
        import jax, jax.numpy as jnp
        import numpy as np
        B, H, W, C = (32, 14, 14, 384)
        b, h_, w_, c = x.shape
        n = h_ * w_
        seq = x.reshape(b, n, c)
        x_zrn = jnp.einsum('bnc,dc->bnd', seq, Wx) + bx
        x_zrn_t = jnp.transpose(x_zrn, (1, 0, 2))

        def step(h, xz):
            h_zrn = h @ Wh.T + bh
            x_z, x_r, x_n = jnp.split(xz, 3, axis=-1)
            h_z, h_r, h_n = jnp.split(h_zrn, 3, axis=-1)
            z = jax.nn.sigmoid(x_z + h_z)
            r = jax.nn.sigmoid(x_r + h_r)
            ncand = jnp.tanh(x_n + r * h_n)
            h_new = (1.0 - z) * ncand + z * h
            return (h_new, h_new)
        h0 = jnp.zeros((b, c), dtype=x.dtype)
        _, hs = jax.lax.scan(step, h0, x_zrn_t)
        y = jnp.transpose(hs, (1, 0, 2))
        y = jnp.einsum('bnc,dc->bnd', y, Wp)
        return y.reshape(b, h_, w_, c)

    def _L1_conv_ref(x, in_proj_w, conv_w, conv_b, x_proj_w, dt_projs_w, dt_projs_b, A_logs, Ds, out_norm_g, out_norm_b, out_proj_w):
        import jax, jax.numpy as jnp
        import numpy as np
        B_, H_, W_, DM = (4, 32, 32, 384)
        DI = int(0.5 * DM)
        N = 16
        R = -(-DM // 16)
        K = 4

        def selective_scan(xs, dts, As, Bs, Cs, Dsk):
            u = jnp.moveaxis(xs, -1, 0)
            d = jnp.moveaxis(dts, -1, 0)
            Bt = jnp.moveaxis(Bs, -1, 0)
            Ct = jnp.moveaxis(Cs, -1, 0)

            def step(h, inp):
                u_t, d_t, B_t, C_t = inp
                dA = jnp.exp(d_t[..., None] * As)
                h = h * dA + (d_t * u_t)[..., None] * B_t[:, :, None, :]
                y = jnp.einsum('bkcn,bkn->bkc', h, C_t)
                return (h, y)
            h0 = jnp.zeros(u.shape[1:] + (As.shape[-1],), u.dtype)
            _, ys = jax.lax.scan(step, h0, (u, d, Bt, Ct))
            ys = jnp.moveaxis(ys, 0, -1)
            return ys + Dsk[None, :, :, None] * xs
        B, H, W, _ = x.shape
        L = H * W
        xz = x @ in_proj_w.T
        xh, z = jnp.split(xz, 2, axis=-1)
        xc = jnp.transpose(xh, (0, 3, 1, 2))
        xc = jax.lax.conv_general_dilated(xc, conv_w, (1, 1), 'SAME', feature_group_count=DI)
        xc = jax.nn.silu(xc + conv_b[None, :, None, None])
        x_flat = xc.reshape(B, DI, L)
        x_t = jnp.transpose(xc, (0, 1, 3, 2)).reshape(B, DI, L)
        x_hwwh = jnp.stack([x_flat, x_t], 1)
        xs = jnp.concatenate([x_hwwh, jnp.flip(x_hwwh, -1)], 1)
        x_dbl = jnp.einsum('bkdl,kcd->bkcl', xs, x_proj_w)
        dts, Bs, Cs = jnp.split(x_dbl, [R, R + N], axis=2)
        dts = jnp.einsum('bkrl,kdr->bkdl', dts, dt_projs_w)
        dts = jax.nn.softplus(dts + dt_projs_b[None, :, :, None])
        As = -jnp.exp(A_logs).reshape(K, DI, N)
        out_y = selective_scan(xs, dts, As, Bs, Cs, Ds.reshape(K, DI))
        inv_y = jnp.flip(out_y[:, 2:4], -1)
        wh_y = jnp.transpose(out_y[:, 1].reshape(B, DI, W, H), (0, 1, 3, 2)).reshape(B, DI, L)
        invwh_y = jnp.transpose(inv_y[:, 1].reshape(B, DI, W, H), (0, 1, 3, 2)).reshape(B, DI, L)
        y = out_y[:, 0] + inv_y[:, 0] + wh_y + invwh_y
        y = jnp.transpose(y, (0, 2, 1)).reshape(B, H, W, DI)
        mu = y.mean(-1, keepdims=True)
        var = y.var(-1, keepdims=True)
        y = (y - mu) / jnp.sqrt(var + 1e-05) * out_norm_g + out_norm_b
        y = y * jax.nn.silu(z)
        return y @ out_proj_w.T

    def _gn(v, G=32, eps=1e-05):
        B_, H_, W_, C_ = v.shape
        g = v.reshape(B_, H_, W_, G, C_ // G)
        m = jnp.mean(g, axis=(1, 2, 4), keepdims=True)
        s = jnp.var(g, axis=(1, 2, 4), keepdims=True)
        return ((g - m) / jnp.sqrt(s + eps)).reshape(v.shape)

    def _ln_c(v, eps=1e-06):
        m = jnp.mean(v, axis=-1, keepdims=True)
        s = jnp.var(v, axis=-1, keepdims=True)
        return (v - m) / jnp.sqrt(s + eps)

    def _ln_t(v, eps=1e-05):
        m = jnp.mean(v, axis=-1, keepdims=True)
        s = jnp.var(v, axis=-1, keepdims=True)
        return (v - m) / jnp.sqrt(s + eps)

    def _to_tokens(v):
        B_, H_, W_, C_ = v.shape
        return v.reshape(B_, H_ * W_, C_)

    def _from_tokens(t, like):
        return t.reshape(like.shape)
    x = x + _L0_conv_ref(_gn(x), L0_conv_Wx, L0_conv_bx, L0_conv_Wh, L0_conv_bh, L0_conv_Wp)
    x = x + _L1_conv_ref(_gn(x), L1_conv_in_proj_w, L1_conv_conv_w, L1_conv_conv_b, L1_conv_x_proj_w, L1_conv_dt_projs_w, L1_conv_dt_projs_b, L1_conv_A_logs, L1_conv_Ds, L1_conv_out_norm_g, L1_conv_out_norm_b, L1_conv_out_proj_w)
    return x

_drawn_inputs = setup_inputs


def setup_inputs(seed=0):
    import zlib

    import numpy as np

    out = dict(_drawn_inputs(seed))
    spreads = {'L0_conv_bx': (0.0, 0.1),
     'L0_conv_bh': (0.0, 0.451),
     'L1_conv_conv_b': (0.0, 0.1),
     'L1_conv_Ds': (1.0, 0.6),
     'L1_conv_out_norm_g': (1.0, 0.6),
     'L1_conv_out_norm_b': (0.0, 0.8)}
    factors = {'L0_conv_Wh': 4.392,
     'L1_conv_conv_w': 3.714,
     'L1_conv_x_proj_w': 64.0,
     'L1_conv_dt_projs_w': 64.0,
     'L1_conv_dt_projs_b': 64.0,
     'L1_conv_A_logs': 64.0}
    for name, (base, spread) in spreads.items():
        noise = np.random.default_rng([zlib.crc32(name.encode()), seed]).standard_normal(out[name].shape)
        drawn = base * np.exp(spread * noise) if base else spread * noise
        out[name] = jnp.asarray(drawn.astype(out[name].dtype))
    for name, factor in factors.items():
        out[name] = (out[name] * factor).astype(out[name].dtype)
    return out
```

```python
from contextlib import ExitStack

import concourse.bass as bass
from concourse import mybir

F32 = mybir.dt.float32
BF16 = mybir.dt.bfloat16
ALU = mybir.AluOpType
ACT = mybir.ActivationFunctionType

B, H, W, C = 32, 14, 14, 384
T = H * W
KC = C // 128
NJ = 4
CJ = C // NJ
SEQ = KC * B
G3 = 3 * CJ
Z_BANK = 4
GN = 12
PAIRS = B // 2
DI = C // 2
N = 16
R = 24
K4 = 4
T2 = 2 * T
TC = 3 * T
GRP = 12
GC = 4 * T
RING = 4
EPS = 1e-5
UNROLL = 16
A_LOG_MAX = 88.72
SMALL = 0.022
P_CW, P_CB, P_DTB, P_AL, P_DS, P_G, P_B = 0, 9, 10, 14, 78, 82, 83
NP = 84


def build(nc, x_seq, x_pair, wx, wh, bx, bh, wp, win, par, xproj, dtproj, wout, out):
    x1_dram = nc.dram_tensor("x1_dram", [PAIRS, 128, KC * T2], F32)
    z_dram = nc.dram_tensor("z_dram", [PAIRS, 128, TC], F32)
    xc_dram = nc.dram_tensor("xc_dram", [PAIRS + 1, 128, TC], F32)

    with ExitStack() as ctx:
        def sb(name, shape, dt=F32):
            return ctx.enter_context(nc.sbuf_tensor(name, shape, dt))

        def sem(name):
            return ctx.enter_context(nc.semaphore(name))

        arena = sb("arena", [128, T * SEQ])
        wx_sb = sb("wx_sb", [128, KC, NJ, G3])
        wh_sb = sb("wh_sb", [128, KC, NJ, G3])
        wp_sb = sb("wp_sb", [128, KC, C])
        win_sb = sb("win_sb", [128, KC, C])
        par01 = sb("par01", [128, NP])
        par2 = sb("par2", [128, NP])
        gavg = sb("gavg", [128, KC, C])
        bias_parts = sb("bias_parts", [96, NJ, 4 * CJ], BF16)
        ones_bf = sb("ones_bf", [96, 32], BF16)
        ident = sb("ident", [128, 128])
        sel = sb("sel", [96, N, 3, 128], BF16)
        bc_w = sb("bc_w", [128, K4, 2, 3, 128])
        dt_w = sb("dt_w", [128, K4, 3, 128])
        wout01 = sb("wout01", [128, C])
        wout2 = sb("wout2", [128, 2, C])
        avg = sb("avg", [128, 6, 128])
        a01 = sb("a01", [128, K4 * N])
        a2 = sb("a2", [128, K4 * N])
        abias01 = sb("abias01", [128, K4 * N])
        abias2 = sb("abias2", [128, K4 * N])
        dsum01 = sb("dsum01", [128, 1])
        dsum2 = sb("dsum2", [128, 1])
        neg_half = sb("neg_half", [128, SEQ])
        series_bias = sb("series_bias", [128, 1])
        stats = sb("stats", [128, SEQ, 4, 3])
        gsum = sb("gsum", [128, SEQ])
        gmean = sb("gmean", [128, SEQ])
        grstd = sb("grstd", [128, SEQ])
        dev = sb("dev", [128, SEQ, 4])
        x_tmp = sb("x_tmp", [128, SEQ])
        x_cur = sb("x_cur", [128, 2, SEQ])
        h_nat = sb("h_nat", [128, CJ])
        h_t = sb("h_t", [128, 2, CJ])
        z_gate = sb("z_gate", [128, CJ])
        r_gate = sb("r_gate", [128, CJ])
        rh = sb("rh", [128, CJ])
        cand_pre = sb("cand_pre", [128, CJ])
        cand = sb("cand", [128, CJ])
        zh = sb("zh", [128, CJ])
        blend = sb("blend", [128, CJ])
        x_in = sb("x_in", [128, KC, T2])
        x1 = sb("x1", [128, KC, T2])
        xhat = sb("xhat", [128, KC, T2])
        pad01 = sb("pad01", [128, 2 * H + 3, W + 2])
        pad2 = sb("pad2", [128, H + 2, W + 2])
        conv01_out = sb("conv01_out", [128, 2 * H + 2, W])
        conv2_out = sb("conv2_out", [128, H, W])
        xc_out = sb("xc_out", [128, TC])
        z_out = sb("z_out", [128, TC])

        ps = ctx.enter_context(nc.psum_tensor("ps", [128, 8, 512], F32))

        bias_x = x_in[0:96, :, :].rearrange("p a b -> p (a b)")[:, 0:0 + 1152]
        seq = arena[:, :].rearrange("p (t c) -> p t c", c=SEQ)

        used = [0]

        def carve(cols, shape=None):
            a = arena[:, used[0]:used[0] + cols]
            used[0] += cols
            return a

        wx_cols = wx_sb[:, :, :, :].rearrange("p a b c -> p (a b c)")
        spare = [wx_cols[:, q * GC:(q + 1) * GC] for q in range(3)]
        da = [[carve(GC) for _ in range(RING - 1)] + [spare[d]] for d in range(2)]
        hb = [carve(GC) for _ in range(RING - 1)] + [spare[2]]
        delta = [carve(TC) for _ in range(2)]
        du = [carve(TC) for _ in range(2)]
        xc = carve(TC)
        xt = carve(TC)
        xdbl = carve(T2)
        resid = carve(T2)
        bcs = [carve(T2 // 2).bitcast(BF16) for _ in range(2)]
        midt = carve(T2 // 2).bitcast(BF16)
        soft = carve(TC)
        relu = carve(TC)
        lnp = carve(TC)
        poly = carve(TC)
        xc_fin = carve(TC)
        z_fin = carve(TC)
        ysb = carve(TC)
        yc = carve(TC)
        ysq = carve(TC)
        x1_fin = x1[:, :, :]
        o_sb = carve(KC * T2).rearrange("p (a b) -> p a b", a=KC)
        assert used[0] <= T * SEQ

        s = {n: sem(n) for n in (
            "params_in", "gru_weights_in", "late_weights_in", "dt_w_clear", "xload0", "xload1", "ident0", "ident_ready", "sel_step", "gavg_step", "const_ready", "staging_clear",
            "split_step", "a_exp", "a_capped",
            "bias_step", "bcw_step", "avg_ready", "a_step",
            "st_done", "a_gn", "a_g1", "a_g2", "a_std", "a_rstd",
            "xs_tmp", "x_ready", "xpart_done", "h_ready", "r_pre_ready", "z_pre_ready", "r_ready", "z_gate_ready", "rh_ready",
            "pre_ready", "tanh_ready", "mix_step", "hnat_ready", "hist_done",
            "xin_ready", "yproj_ready", "x1_ready", "x1_spilled", "stats_ready", "gn_step", "g1_ready",
            "g2_ready", "rstd_ready", "xhat_ready", "inproj_ready", "inproj_whole", "pad_ready", "z_ready", "conv01_step",
            "conv2_step", "xc_ready", "z_spilled", "xc_spilled", "xc_dup", "pad_zero",
            "d_zero", "xc_loaded", "xt_ready", "bc_ready", "xdbl_ready", "resid_ready", "mid_ready",
            "parts_ready", "dt_ready", "dt_read", "soft_step", "series_step", "choice_ready", "log_ready", "delta_ready", "du_ready", "bb_ready",
            "cb_ready", "da_ready", "m1_done", "scan_done", "m3_done", "red_done", "y_drained",
            "mean_ready", "yc_ready", "ysq_ready", "var_ready", "rstd2_step", "norm_step", "gated",
            "oproj_ready", "o_ready", "out_stored", "fin_x", "fin_z", "fin_x1")}

        convs = ((pad01, conv01_out, 2 * H + 1, par01, s["conv01_step"]), (pad2, conv2_out, H, par2, s["conv2_step"]))

        def conv_taps(eng, i, taps):
            for tap in taps:
                for pad, conv, rows, table, step in convs:
                    win_ = pad[:, tap // 3:tap // 3 + rows, tap % 3:tap % 3 + W]
                    dst = conv[:, 0:rows, :]
                    wv = table[:, P_CW + tap:P_CW + tap + 1]
                    if tap == 0:
                        ins = eng.tensor_scalar(dst, win_, wv, table[:, P_CB:P_CB + 1], ALU.mult, ALU.add)
                    else:
                        eng.wait_ge(step, i * 9 + tap)
                        ins = eng.scalar_tensor_tensor(dst, win_, wv, dst, ALU.mult, ALU.add)
                    ins.then_inc(step, 1)

        def two_images(rows):
            return rows.rearrange("p (b r) w -> p b r w", b=2)[:, :, 0:H, :]

        def group_aps(g):
            if g < 8:
                return (lambda a: a[:, 0:T2].unsqueeze(1).broadcast_to([128, 2, T2]),
                        lambda bank: ps[:, bank:bank + 2, 0:T2],
                        lambda a: a.rearrange("p (m c) -> p m c", m=2))
            return (lambda a: a[:, T2:TC].unsqueeze(1).unsqueeze(1).broadcast_to([128, 2, 2, T]),
                    lambda bank: ps[:, bank:bank + 2, 0:T2].rearrange("p m (q t) -> p m q t", q=2),
                    lambda a: a.rearrange("p (m q t) -> p m q t", m=2, q=2))

        def ring_of(k, g):
            return (k * GRP + g) % RING, da[k // 2][(k % 2 * GRP + g) % RING]

        block = ctx.enter_context(nc.Block())

        PARAM_LOADS, LATE_LOADS = 12, 8
        HALF = T // 2

        @block.sync
        def _(sp):
            stage = x1[:, :, :].rearrange("p a b -> p (a b)")
            n56 = K4 * (R + 2 * N)
            for dst, src in (
                    (par01[:, :], par[0:128, :]), (par2[0:64, :], par[128:DI, :]), (par2[64:128, :], par[128:DI, :]),
                    (stage[:, 0:n56], xproj[0:128, :]), (stage[0:64, n56:2 * n56], xproj[128:DI, :]),
                    (stage[64:128, n56:2 * n56], xproj[128:DI, :])):
                sp.dma_start(dst, src).then_inc(s["params_in"], 16)
            sp.wait_ge(s["staging_clear"], 2)
            for q in range(3):
                sp.dma_start(x_in[32 * q:32 * q + 1, :, :].rearrange("p a b -> p (a b)")[:, 0:NJ * G3],
                             bx).then_inc(s["params_in"], 16)
                sp.dma_start(xhat[32 * q:32 * q + 1, :, :].rearrange("p a b -> p (a b)")[:, 0:NJ * G3],
                             bh).then_inc(s["params_in"], 16)
            for h in range(2):
                sp.dma_start(seq[:, h * HALF:(h + 1) * HALF, :],
                             x_seq[:, h * HALF:(h + 1) * HALF, :]).then_inc(s[f"xload{h}"], 16)
            sp.dma_start(wx_sb[:, :, :, :], wx).then_inc(s["gru_weights_in"], 16)
            sp.dma_start(wh_sb[:, :, :, :], wh).then_inc(s["gru_weights_in"], 16)
            sp.wait_ge(s["dt_w_clear"], 1)
            for dst, src in (
                    (wp_sb[:, :, :], wp), (win_sb[:, :, :], win),
                    (wout01[:, :], wout[0:128, :]), (wout2[0:64, 0, :], wout[128:DI, :]), (wout2[64:128, 1, :], wout[128:DI, :]),
                    (dt_w[96:96 + R, :, 0, :], dtproj[:, :, 0:128]), (dt_w[96:96 + R, :, 1, 0:64], dtproj[:, :, 128:DI]),
                    (dt_w[96:96 + R, :, 2, 64:128], dtproj[:, :, 128:DI])):
                sp.dma_start(dst, src).then_inc(s["late_weights_in"], 16)

            sp.wait_ge(s["bias_step"], 8)
            sp.dma_start(x_in[:, :, :], x_pair[0]).then_inc(s["xin_ready"], 16)

            def load_x(i):
                sp.wait_ge(s["xin_ready"], i * 16)
                sp.dma_start(flat(x_in), dram(x_pair, i)).then_inc(s["xin_ready"], 16)

            def spill_z(i):
                sp.wait_ge(s["z_ready"], i * 2 + 2)
                sp.dma_start(dram(z_dram, i), z_out[:, :]).then_inc(s["z_spilled"], 16)

            def spill_xc(i):
                sp.wait_ge(s["xc_ready"], i * 2 + 2)
                sp.dma_start(dram(xc_dram, i), xc_out[:, :]).then_inc(s["xc_spilled"], 16)

            def spill_a(i):
                sp.wait_ge(s["x1_ready"], i + 1)
                sp.wait_ge(s["x1_spilled"], i * 16)
                sp.dma_start(dram(x1_dram, i), flat(x1)).then_inc(s["x1_spilled"], 16)

            sp.wait_ge(s["x1_ready"], 1)
            sp.dma_start(dram(x1_dram, 0), flat(x1)).then_inc(s["x1_spilled"], 16)
            load_x(1)
            spill_a(1)
            spill_z(0)
            with sp.Fori(2, PAIRS) as i:
                load_x(i)
                spill_a(i)
                spill_xc(i - 2)
                spill_z(i - 1)
            spill_xc(PAIRS - 2)
            spill_z(PAIRS - 1)
            spill_xc(PAIRS - 1)
            sp.dma_start(dram(xc_dram, PAIRS), xc_out[:, :]).then_inc(s["xc_dup"], 16)
            sp.wait_ge(s["xc_dup"], 16)

            sp.wait_ge(s["xc_spilled"], 16 * PAIRS)
            sp.wait_ge(s["z_spilled"], 16 * PAIRS)
            sp.wait_ge(s["x1_spilled"], 16 * PAIRS)
            sp.wait_ge(s["inproj_ready"], PAIRS)
            sp.dma_start(xc, dram(xc_dram, 0)).then_inc(s["xc_loaded"], 16)

            def fin_loads(i):
                sp.dma_start(xc_fin, dram(xc_dram, i)).then_inc(s["fin_x"], 16)
                sp.dma_start(z_fin, dram(z_dram, i)).then_inc(s["fin_z"], 16)
                sp.dma_start(flat(x1), dram(x1_dram, i)).then_inc(s["fin_x1"], 16)

            def next_x(i):
                sp.wait_ge(s["du_ready"], i * 4 + 4)
                sp.dma_start(xc, dram(xc_dram, i + 1)).then_inc(s["xc_loaded"], 16)

            def store(i):
                sp.wait_ge(s["o_ready"], i * 3 + 3)
                sp.dma_start(dram(out, i), o_sb.rearrange("p a b -> p (a b)")).then_inc(s["out_stored"], 16)

            fin_loads(0)
            next_x(0)
            with sp.Fori(1, PAIRS) as i:
                store(i - 1)
                sp.wait_ge(s["out_stored"], i * 16)
                sp.wait_ge(s["fin_x"], i * 16)
                sp.wait_ge(s["fin_z"], i * 16)
                sp.wait_ge(s["fin_x1"], i * 16)
                fin_loads(i)
                next_x(i)
            store(PAIRS - 1)
            sp.wait_ge(s["out_stored"], 16 * PAIRS)

        @block.gpsimd
        def _(pool):
            pool.memset(x_in[:, :, :], 0.0).then_inc(s["staging_clear"], 1)
            pool.memset(xhat[:, :, :], 0.0).then_inc(s["staging_clear"], 1)
            pool.memset(dt_w[:, :, :, :], 0.0).then_inc(s["dt_w_clear"], 1)
            pool.memset(ident[:, :], 0.0).then_inc(s["ident0"], 1)
            pool.wait_ge(s["ident0"], 1)
            pool.affine_select(out=ident[:, :], in_=ident[:, :], compare_op=ALU.not_equal, fill=1.0, base=0,
                               pattern=[[-1, 128]], channel_multiplier=1).then_inc(s["ident_ready"], 1)
            g = gavg[:, :, :].rearrange("p k (g i) -> p k g i", i=GN)
            pool.memset(gavg[:, :, :], 1.0 / GN).then_inc(s["gavg_step"], 1)
            pool.wait_ge(s["gavg_step"], 1)
            pool.affine_select(out=g, in_=g, compare_op=ALU.is_ge, fill=0.0, base=0,
                               pattern=[[128, KC], [-GN, C // GN], [0, GN]], channel_multiplier=1
                               ).then_inc(s["gavg_step"], 1)
            pool.wait_ge(s["gavg_step"], 2)
            pool.affine_select(out=g, in_=g, compare_op=ALU.is_ge, fill=0.0, base=GN - 1,
                               pattern=[[-128, KC], [GN, C // GN], [0, GN]], channel_multiplier=-1
                               ).then_inc(s["gavg_step"], 1)
            pool.memset(neg_half[:, :], -0.5).then_inc(s["gavg_step"], 1)
            pool.memset(sel[:, :, :, :], 0.0).then_inc(s["sel_step"], 1)
            step = 1
            for part in range(3):
                for kind, lo, hi, img in ((0, 0, 128, 0), (1, 0, 128, 1), (2, 0, 64, 0), (2, 64, 128, 1)):
                    v = sel[:, :, kind, lo:hi]
                    pool.wait_ge(s["sel_step"], step)
                    pool.affine_select(out=v, in_=v, compare_op=ALU.not_equal, fill=1.0,
                                       base=-(32 * part + N * img), pattern=[[-1, N], [0, hi - lo]],
                                       channel_multiplier=1).then_inc(s["sel_step"], 1)
                    step += 1
            pool.memset(pad01[:, :, :], 0.0).then_inc(s["pad_zero"], 1)
            pool.memset(pad2[:, :, :], 0.0).then_inc(s["pad_zero"], 1)

            pool.wait_ge(s["a_rstd"], 1)

            def norm(t, p, first=False):
                if not first:
                    pool.wait_ge(s["x_ready"], t + 0)
                pool.tensor_tensor(x_tmp[:, :], tok(t), gmean[:, :], ALU.subtract).then_inc(s["xs_tmp"], 1)
                pool.wait_ge(s["xs_tmp"], t + 1)
                if not first:
                    pool.wait_ge(s["xpart_done"], t - 1)
                pool.tensor_tensor(x_cur[:, p, :], x_tmp[:, :], grstd[:, :], ALU.mult).then_inc(s["x_ready"], 1)

            def tok(t):
                return arena[:, bass.ds(t * SEQ, SEQ)] if not isinstance(t, int) else arena[:, t * SEQ:(t + 1) * SEQ]

            def keep(t, p):
                pool.wait_ge(s["h_ready"], t + 2)
                pool.tensor_copy(tok(t), h_t[:, p, :]).then_inc(s["hist_done"], 1)

            norm(0, 0, True)
            pool.wait_ge(s["x_ready"], 1)
            norm(1, 1, True)
            with pool.Fori(0, T // 2 - 1) as i:
                for p in range(2):
                    norm(i * 2 + (p + 2), p)
                    keep(i * 2 + p, p)
            keep(T - 2, 0)
            keep(T - 1, 1)

            pool.wait_ge(s["gavg_step"], 4)

            def rstd_c(i):
                pool.wait_ge(s["gn_step"], i * 8 + 7)
                pool.tensor_tensor(grstd[:, 0:6], gsum[:, 0:6], neg_half[:, 0:6], ALU.pow).then_inc(s["rstd_ready"], 1)

            pool.wait_ge(s["hist_done"], T)
            rstd_c(0)
            with pool.Fori(1, PAIRS) as i:
                rstd_c(i)

            def small_parts(st, b):
                pool.wait_ge(s["xdbl_ready"], 2 * st + 2)
                pool.tensor_tensor(resid[0:96, :], xdbl[0:96, :], bcs[b][0:96, :], ALU.subtract).then_inc(s["resid_ready"], 1)
                pool.wait_ge(s["mid_ready"], 2 * st + 2)
                pool.tensor_tensor(bcs[b][64:96, :], resid[64:96, :], midt[64:96, :], ALU.subtract).then_inc(s["parts_ready"], 1)

            def deltas(st, k, b, first=False):
                pool.wait_ge(s["parts_ready"], st + 1)
                pool.wait_ge(s["soft_step"], 4 * st + 4)
                pool.tensor_tensor(poly, poly, soft, ALU.mult).then_inc(s["series_step"], 1)
                pool.wait_ge(s["series_step"], 2 * st + 1)
                pool.tensor_tensor(poly, poly, lnp, ALU.subtract).then_inc(s["series_step"], 1)
                pool.wait_ge(s["series_step"], 2 * st + 2)
                pool.tensor_tensor(lnp, lnp, relu, ALU.add).then_inc(s["log_ready"], 1)
                pool.wait_ge(s["choice_ready"], st + 1)
                pool.wait_ge(s["log_ready"], st + 1)
                if not first:
                    pool.wait_ge(s["da_ready"], (st - 1) * GRP)
                pool.tensor_tensor(delta[b], lnp, poly, ALU.add).then_inc(s["delta_ready"], 1)
                pool.wait_ge(s["delta_ready"], st + 1)
                if not first:
                    pool.wait_ge(s["m1_done"], (st - 1) * GRP)
                pool.tensor_tensor(du[b], delta[b], xt if k % 2 else xc, ALU.mult).then_inc(s["du_ready"], 1)

            pool.wait_ge(s["xc_loaded"], 16)
            small_parts(0, 0)
            deltas(0, 0, 0, True)

            def pair(i):
                for k in range(K4):
                    st = i * K4 + (k + 1)
                    small_parts(st, (k + 1) % 2)
                    deltas(st, (k + 1) % K4, (k + 1) % 2)

            pair(0)
            with pool.Fori(1, PAIRS) as i:
                pair(i)

        @block.vector
        def _(dve):
            dve.memset(series_bias[:, :], -(3.0 ** 0.5) / 4.0).then_inc(s["const_ready"], 1)
            dve.memset(ones_bf[:, :], 1.0).then_inc(s["const_ready"], 1)
            dve.memset(h_nat[:, :], 0.0).then_inc(s["const_ready"], 1)
            dve.memset(h_t[:, 1, :], 0.0).then_inc(s["h_ready"], 1)
            dve.memset(bc_w[:, :, :, :, :], 0.0).then_inc(s["bcw_step"], 1)
            dve.memset(avg[:, :, :], 0.0).then_inc(s["avg_ready"], 1)
            dve.wait_ge(s["avg_ready"], 1)
            dve.memset(avg[:, 0, :], 1.0 / DI).then_inc(s["avg_ready"], 1)
            dve.memset(avg[0:64, 1, :], 1.0 / DI).then_inc(s["avg_ready"], 1)
            dve.memset(avg[64:128, 2, :], 1.0 / DI).then_inc(s["avg_ready"], 1)
            dve.memset(avg[0:64, 3, 0:64], 1.0 / DI).then_inc(s["avg_ready"], 1)
            dve.memset(avg[64:128, 3, 64:128], 1.0 / DI).then_inc(s["avg_ready"], 1)
            dve.memset(wout2[64:128, 0, :], 0.0).then_inc(s["avg_ready"], 1)
            dve.memset(wout2[0:64, 1, :], 0.0).then_inc(s["avg_ready"], 1)
            dve.memset(avg[:, 4, 0:64], 1.0 / DI).then_inc(s["avg_ready"], 1)
            dve.memset(avg[:, 5, 64:128], 1.0 / DI).then_inc(s["avg_ready"], 1)
            dve.wait_ge(s["params_in"], 16 * PARAM_LOADS)
            dve.wait_ge(s["bcw_step"], 1)
            stage = x1[:, :, :].rearrange("p a b -> p (a b)")
            n56 = K4 * (R + 2 * N)
            for rows, tile, img, col in ((slice(0, 128), 0, 0, 0), (slice(0, 128), 1, 1, 0),
                                         (slice(0, 64), 2, 0, n56), (slice(64, 128), 2, 1, n56)):
                src = stage[rows, col:col + n56].rearrange("p (k m) -> p k m", k=K4)
                rn = rows.stop - rows.start
                for bc in range(2):
                    dst = bc_w[rows, :, bc, tile, 0:96].rearrange("p k (q m) -> p k q m", q=3)[:, :, :, N * img:N * img + N]
                    dve.tensor_copy(dst, src[:, :, R + N * bc:R + N * bc + N].unsqueeze(2).broadcast_to([rn, K4, 3, N])
                                    ).then_inc(s["bcw_step"], 1)
                dve.tensor_copy(bc_w[rows, :, img, tile, 96:96 + R], src[:, :, 0:R]).then_inc(s["bcw_step"], 1)
            bxv = x_in[0:96, :, :].rearrange("p a b -> p (a b)")[:, 0:NJ * G3].rearrange("p (j c) -> p j c", j=NJ)
            bhv = xhat[0:96, :, :].rearrange("p a b -> p (a b)")[:, 0:NJ * G3].rearrange("p (j c) -> p j c", j=NJ)
            for lo, lo_h in ((CJ, 0), (2 * CJ, 2 * CJ)):
                dve.tensor_tensor(bxv[:, :, lo:lo + CJ], bxv[:, :, lo:lo + CJ], bhv[:, :, lo_h:lo_h + CJ], ALU.add
                                  ).then_inc(s["bias_step"], 1)
            dve.wait_ge(s["bias_step"], 2)
            pieces = ((bxv[:, :, 0:2 * CJ], 0), (bhv[:, :, CJ:2 * CJ], 2 * CJ), (bxv[:, :, 2 * CJ:G3], G3))

            def part_of(piece, lo, hi):
                bias, at = pieces[piece]
                return bias[lo:hi], bias_parts[lo:hi, :, at:at + bias.shape[2]]

            for piece in range(3):
                bias, part = part_of(piece, 0, 96)
                dve.tensor_copy(part, bias).then_inc(s["bias_step"], 1)
            dve.wait_ge(s["bias_step"], 5)
            for piece in range(3):
                bias, part = part_of(piece, 0, 96)
                dve.tensor_tensor(bias, bias, part, ALU.subtract).then_inc(s["split_step"], 1)
            dve.wait_ge(s["split_step"], 3)
            for lo in (32, 64):
                for piece in range(3):
                    bias, part = part_of(piece, lo, lo + 32)
                    dve.tensor_copy(part, bias).then_inc(s["split_step"], 1)
            dve.wait_ge(s["split_step"], 9)
            for piece in range(3):
                bias, part = part_of(piece, 64, 96)
                dve.tensor_tensor(bias, bias, part, ALU.subtract).then_inc(s["split_step"], 1)
            dve.wait_ge(s["split_step"], 12)
            for piece in range(3):
                bias, part = part_of(piece, 64, 96)
                dve.tensor_copy(part, bias).then_inc(s["bias_step"], 1)
            for src, dst, bias in ((par01, a01, abias01), (par2, a2, abias2)):
                src = src[:, P_AL:P_AL + K4 * N]
                dve.tensor_scalar(dst[:, :], src, A_LOG_MAX, None, ALU.min).then_inc(s["a_capped"], 1)
                dve.tensor_scalar(bias[:, :], src, A_LOG_MAX, -1e30, ALU.is_gt, ALU.mult).then_inc(s["a_capped"], 1)
            dve.tensor_reduce(dsum01[:, :], par01[:, P_DS:P_DS + K4], mybir.AxisListType.X, ALU.add).then_inc(s["avg_ready"], 1)
            dve.tensor_reduce(dsum2[:, :], par2[:, P_DS:P_DS + K4], mybir.AxisListType.X, ALU.add).then_inc(s["avg_ready"], 1)
            dve.wait_ge(s["a_exp"], 2)
            dve.tensor_scalar(a01[:, :], a01[:, :], -1.0, None, ALU.mult).then_inc(s["a_capped"], 1)
            dve.tensor_scalar(a2[:, :], a2[:, :], -1.0, None, ALU.mult).then_inc(s["a_capped"], 1)
            dve.wait_ge(s["a_capped"], 6)
            for dst, bias in ((a01, abias01), (a2, abias2)):
                dve.scalar_tensor_tensor(dst[:, :], bias[:, :], 0.0, dst[:, :], ALU.is_equal, ALU.mult).then_inc(s["avg_ready"], 1)

            for h in range(2):
                dve.wait_ge(s[f"xload{h}"], 16)
                tokens = seq[:, h * HALF:(h + 1) * HALF, :].rearrange("p t (c u) -> p t c u", u=UNROLL)
                halves = stats[:, :, 2 * h:2 * h + 2, :].rearrange("p (c u) a b -> p c u (a b)", u=UNROLL)
                with dve.Fori(0, SEQ // UNROLL) as c:
                    for u in range(UNROLL):
                        dve.bn_stats(halves[:, bass.ds(c, 1), u, :].rearrange("p c x -> p (c x)"),
                                     tokens[:, :, bass.ds(c, 1), u].rearrange("p t c -> p (t c)")
                                     ).then_inc(s["st_done"], 1)
            dve.wait_ge(s["st_done"], 2 * SEQ)
            dve.tensor_reduce(gsum[:, :], stats[:, :, :, 1], mybir.AxisListType.X, ALU.add).then_inc(s["a_gn"], 1)
            dve.wait_ge(s["a_g1"], 1)
            dve.tensor_scalar(gmean[:, :], ps[:, 2, 0:SEQ], 0.25, None, ALU.mult).then_inc(s["a_gn"], 1)
            dve.wait_ge(s["a_gn"], 2)
            dve.tensor_tensor(dev[:, :, :], stats[:, :, :, 1], gmean[:, :].unsqueeze(2).broadcast_to([128, SEQ, 4]),
                              ALU.subtract).then_inc(s["a_gn"], 1)
            dve.wait_ge(s["a_gn"], 3)
            dve.tensor_tensor(dev[:, :, :], dev[:, :, :], dev[:, :, :], ALU.mult).then_inc(s["a_gn"], 1)
            dve.wait_ge(s["a_gn"], 4)
            dve.scalar_tensor_tensor(dev[:, :, :], dev[:, :, :], float(T // 4), stats[:, :, :, 2], ALU.mult, ALU.add
                                     ).then_inc(s["a_gn"], 1)
            dve.wait_ge(s["a_gn"], 5)
            dve.tensor_reduce(gsum[:, :], dev[:, :, :], mybir.AxisListType.X, ALU.add).then_inc(s["a_gn"], 1)
            dve.wait_ge(s["a_g2"], 1)
            dve.tensor_scalar(gsum[:, :], ps[:, 3, 0:SEQ], 1.0 / T, EPS, ALU.mult, ALU.add).then_inc(s["a_gn"], 1)

            dve.wait_ge(s["a_std"], 1)
            dve.reciprocal(grstd[:, :], gsum[:, :]).then_inc(s["a_rstd"], 1)

            def step(t, p, first=False):
                dve.wait_ge(s["r_ready"], t + 1)
                dve.tensor_tensor(rh[:, :], r_gate[:, :], ps[:, p, 2 * CJ:G3], ALU.mult).then_inc(s["rh_ready"], 1)
                dve.wait_ge(s["rh_ready"], t + 1)
                dve.tensor_tensor(cand_pre[:, :], rh[:, :], ps[:, p, 0:CJ], ALU.add).then_inc(s["pre_ready"], 1)
                dve.wait_ge(s["z_gate_ready"], t + 1)
                if not first:
                    dve.wait_ge(s["hist_done"], t - 1)
                dve.tensor_tensor(zh[:, :], z_gate[:, :], h_nat[:, :], ALU.mult).then_inc(s["mix_step"], 1)
                dve.wait_ge(s["tanh_ready"], t + 1)
                dve.scalar_tensor_tensor(blend[:, :], z_gate[:, :], -1.0, cand[:, :], ALU.add, ALU.mult).then_inc(s["mix_step"], 1)
                dve.wait_ge(s["mix_step"], t * 2 + 2)
                dve.tensor_tensor(h_nat[:, :], zh[:, :], blend[:, :], ALU.subtract).then_inc(s["hnat_ready"], 1)
                dve.wait_ge(s["hnat_ready"], t + 1)
                dve.transpose(h_t[:, p, :], h_nat[:, :]).then_inc(s["h_ready"], 1)

            dve.wait_ge(s["const_ready"], 3)
            step(0, 0, True)
            step(1, 1, True)
            with dve.Fori(1, T // 2) as i:
                for p in range(2):
                    step(i * 2 + p, p)

            st6 = stats[:, 0:KC * 2, 0:2, :]
            mean2 = st6[:, :, :, 1]
            dv = dev[:, 0:6, 0:2]

            def add_and_stats(i, first=False):
                dve.wait_ge(s["yproj_ready"], i + 1)
                dve.wait_ge(s["xin_ready"], i * 16 + 16)
                if not first:
                    dve.wait_ge(s["x1_spilled"], i * 16)
                    dve.wait_ge(s["xhat_ready"], i * 6)
                dve.tensor_tensor(x1[:, :, :], x_in[:, :, :], ps[:, 0:3, 0:T2], ALU.add).then_inc(s["x1_ready"], 1)
                dve.wait_ge(s["x1_ready"], i + 1)
                for kc in range(KC):
                    for b in range(2):
                        dve.bn_stats(st6[:, 2 * kc + b, :, :].rearrange("p a b -> p (a b)"),
                                     x1[:, kc, b * T:(b + 1) * T]).then_inc(s["stats_ready"], 1)
                dve.wait_ge(s["stats_ready"], i * 6 + 6)
                dve.tensor_tensor(gsum[:, 0:6], mean2[:, :, 0], mean2[:, :, 1], ALU.add).then_inc(s["gn_step"], 1)

            def deviations(i):
                dve.wait_ge(s["g1_ready"], i + 1)
                dve.tensor_scalar(gmean[:, 0:6], ps[:, 6, 0:6], 0.5, None, ALU.mult).then_inc(s["gn_step"], 1)
                dve.wait_ge(s["gn_step"], i * 8 + 2)
                dve.tensor_tensor(dv, mean2, gmean[:, 0:6].unsqueeze(2).broadcast_to([128, 6, 2]), ALU.subtract
                                  ).then_inc(s["gn_step"], 1)
                dve.wait_ge(s["gn_step"], i * 8 + 3)
                dve.tensor_tensor(dv, dv, dv, ALU.mult).then_inc(s["gn_step"], 1)
                dve.wait_ge(s["gn_step"], i * 8 + 4)
                dve.scalar_tensor_tensor(dv, dv, float(T // 2), st6[:, :, :, 2], ALU.mult, ALU.add).then_inc(s["gn_step"], 1)
                dve.wait_ge(s["gn_step"], i * 8 + 5)
                dve.tensor_tensor(gsum[:, 0:6], dv[:, :, 0], dv[:, :, 1], ALU.add).then_inc(s["gn_step"], 1)

            def variance(i):
                dve.wait_ge(s["g2_ready"], i + 1)
                dve.tensor_scalar(gsum[:, 0:6], ps[:, 7, 0:6], 1.0 / T, EPS, ALU.mult, ALU.add).then_inc(s["gn_step"], 1)

            def normalise(i, first=False):
                dve.wait_ge(s["rstd_ready"], i + 1)
                dve.scalar_tensor_tensor(gmean[:, 0:6], gmean[:, 0:6], -1.0, grstd[:, 0:6], ALU.mult, ALU.mult
                                         ).then_inc(s["gn_step"], 1)
                dve.wait_ge(s["gn_step"], i * 8 + 8)
                if not first:
                    dve.wait_ge(s["inproj_ready"], i + 0)
                for c in range(6):
                    v = (slice(None), c // 2, slice(c % 2 * T, c % 2 * T + T))
                    dve.tensor_scalar(xhat[v], x1[v], grstd[:, c:c + 1], gmean[:, c:c + 1], ALU.mult, ALU.add
                                      ).then_inc(s["xhat_ready"], 1)

            def convolve(i, taps, first=False):
                if taps[0] == 0:
                    dve.wait_ge(s["pad_ready"], i * 2 + 2)
                    if not first:
                        dve.wait_ge(s["xc_ready"], i * 2)
                conv_taps(dve, i, taps)

            add_and_stats(0, True)
            deviations(0)
            variance(0)
            normalise(0, True)

            def norm_and_convolve(i, first=False):
                add_and_stats(i)
                if not first:
                    convolve(i - 2, range(4, 6))
                deviations(i)
                if not first:
                    convolve(i - 2, range(6, 9))
                variance(i)
                convolve(i - 1, range(0, 2), first)
                normalise(i)
                convolve(i - 1, range(2, 4))

            norm_and_convolve(1, True)
            with dve.Fori(2, PAIRS) as i:
                norm_and_convolve(i)
            convolve(PAIRS - 2, range(4, 9))
            convolve(PAIRS - 1, range(9))

            dve.wait_ge(s["inproj_ready"], PAIRS)
            for q in range(RING):
                for d in range(2):
                    z0 = da[d][q].rearrange("p (r t) -> p r t", t=T)
                    dve.memset(z0[:, :, 0:1] if d == 0 else z0[:, :, T - 1:T], 0.0).then_inc(s["d_zero"], 1)
            dve.wait_ge(s["d_zero"], 2 * RING)

            def m1(i, k, g, G, b, first=False):
                dux, bank, view = group_aps(g)
                q, _ = ring_of(k, g)
                if g == 0:
                    dve.wait_ge(s["du_ready"], i * K4 + (k + 1))
                dve.wait_ge(s["bb_ready"], G + 1)
                if not first:
                    dve.wait_ge(s["red_done"], G - (RING - 1))
                dve.tensor_tensor(view(hb[q]), dux(du[b]), bank(0), ALU.mult).then_inc(s["m1_done"], 1)

            def scan(k, g, G):
                q, dec = ring_of(k, g)
                dve.wait_ge(s["m1_done"], G + 1)
                dve.wait_ge(s["da_ready"], G + 1)
                st = hb[q]
                if k < 2:
                    dve.tensor_tensor_scan(st, dec, st, 0.0, ALU.mult, ALU.add).then_inc(s["scan_done"], 1)
                else:
                    dve.tensor_tensor_scan(st[:, ::-1], dec[:, ::-1], st[:, ::-1], 0.0, ALU.mult, ALU.add
                                           ).then_inc(s["scan_done"], 1)

            def m3(k, g, G):
                _, bank, view = group_aps(g)
                q, _ = ring_of(k, g)
                dve.wait_ge(s["scan_done"], G + 1)
                dve.wait_ge(s["cb_ready"], G + 1)
                dve.tensor_tensor(view(hb[q]), view(hb[q]), bank(2), ALU.mult).then_inc(s["m3_done"], 1)

            def drain(i):
                dve.wait_ge(s["red_done"], (i + 1) * (K4 * GRP))
                dve.wait_ge(s["fin_x"], i * 16 + 16)
                dve.scalar_tensor_tensor(ysb[:, 0:T2], xc_fin[:, 0:T2], dsum01[:, 0:1], ps[:, 4, 0:T2], ALU.mult, ALU.add
                                         ).then_inc(s["y_drained"], 1)
                dve.scalar_tensor_tensor(ysb[:, T2:TC], xc_fin[:, T2:TC], dsum2[:, 0:1], ps[:, 5, 0:T], ALU.mult, ALU.add
                                         ).then_inc(s["y_drained"], 1)

            def centre(i):
                dve.wait_ge(s["mean_ready"], i * 2 + 2)
                dve.tensor_tensor(yc[:, 0:T2], ysb[:, 0:T2], ps[:, 6, 0:T2], ALU.subtract).then_inc(s["yc_ready"], 1)
                dve.tensor_tensor(yc[:, T2:TC], ysb[:, T2:TC], ps[:, 7, 0:T], ALU.subtract).then_inc(s["yc_ready"], 1)

            def gate(i):
                dve.wait_ge(s["rstd2_step"], i * 3 + 3)
                dve.wait_ge(s["fin_z"], i * 16 + 16)
                for lo, hi, table in ((0, T2, par01), (T2, TC, par2)):
                    dve.scalar_tensor_tensor(yc[:, lo:hi], yc[:, lo:hi], table[:, P_G:P_G + 1], ysq[:, lo:hi],
                                             ALU.mult, ALU.mult).then_inc(s["norm_step"], 1)
                dve.wait_ge(s["norm_step"], i * 2 + 2)
                for lo, hi, table in ((0, T2, par01), (T2, TC, par2)):
                    dve.scalar_tensor_tensor(yc[:, lo:hi], yc[:, lo:hi], table[:, P_B:P_B + 1], z_fin[:, lo:hi],
                                             ALU.add, ALU.mult).then_inc(s["gated"], 1)

            def residual(i, oc):
                dve.wait_ge(s["oproj_ready"], i * 3 + (oc + 1))
                dve.wait_ge(s["fin_x1"], i * 16 + 16)
                dve.tensor_tensor(o_sb[:, oc, :], x1[:, oc, :], ps[:, 6 + oc % 2, 0:T2], ALU.add).then_inc(s["o_ready"], 1)

            def choose(st):
                dve.wait_ge(s["series_step"], 2 * st + 2)
                dve.scalar_tensor_tensor(poly, soft, SMALL, poly, ALU.is_lt, ALU.mult).then_inc(s["choice_ready"], 1)

            def pair(i, head):
                for k in range(K4):
                    for g in range(GRP):
                        G = i * (K4 * GRP) + (k * GRP + g)
                        scan(k, g, G)
                        k2, g2 = (k, g + 1) if g + 1 < GRP else (k + 1, 0)
                        if k2 < K4:
                            m1(i, k2, g2, G + 1, k2 % 2, head and k2 * GRP + g2 < RING)
                        else:
                            m1_next(i, G + 1)
                        m3(k, g, G)
                        if g == (8 if k != 1 else 9):
                            choose(i * K4 + (k + 1))
                        if not head:
                            if (k, g) == (0, 0):
                                drain(i - 1)
                            if (k, g) == (0, 7):
                                centre(i - 1)
                            if (k, g) == (1, 1):
                                gate(i - 1)
                            if k == 1 and 7 <= g < 7 + KC:
                                residual(i - 1, g - 7)

            def m1_next(i, G):
                dux, bank, view = group_aps(0)
                dve.wait_ge(s["du_ready"], i * K4 + (K4 + 1))
                dve.wait_ge(s["bb_ready"], G + 1)
                dve.wait_ge(s["red_done"], G - (RING - 1))
                dve.tensor_tensor(view(hb[0]), dux(du[0]), bank(0), ALU.mult).then_inc(s["m1_done"], 1)

            choose(0)
            m1(0, 0, 0, 0, 0, True)
            pair(0, True)
            with dve.Fori(1, PAIRS) as i:
                pair(i, False)
            drain(PAIRS - 1)
            centre(PAIRS - 1)
            gate(PAIRS - 1)
            for oc in range(KC):
                residual(PAIRS - 1, oc)

        @block.scalar
        def _(act):
            act.wait_ge(s["a_capped"], 4)
            act.activation(a01[:, :], a01[:, :], ACT.Exp).then_inc(s["a_exp"], 1)
            act.activation(a2[:, :], a2[:, :], ACT.Exp).then_inc(s["a_exp"], 1)

            act.preload_act_table_set("sqrt_and_others")
            act.wait_ge(s["a_gn"], 7)
            act.activation(gsum[:, :], gsum[:, :], ACT.Sqrt).then_inc(s["a_std"], 1)

            act.preload_act_table_set("sigmoid_and_others")

            def step(t, p):
                act.wait_ge(s["r_pre_ready"], t + 1)
                act.activation(r_gate[:, :], ps[:, p, CJ:2 * CJ], ACT.Sigmoid).then_inc(s["r_ready"], 1)
                act.wait_ge(s["z_pre_ready"], t + 1)
                act.activation(z_gate[:, :], ps[:, Z_BANK + p, 0:CJ], ACT.Sigmoid).then_inc(s["z_gate_ready"], 1)
                act.wait_ge(s["pre_ready"], t + 1)
                act.activation(cand[:, :], cand_pre[:, :], ACT.Tanh).then_inc(s["tanh_ready"], 1)

            with act.Fori(0, T // 2) as i:
                for p in range(2):
                    step(i * 2 + p, p)

            def xh_and_z(i, first=False):
                act.wait_ge(s["inproj_whole"], i + 1)
                if not first:
                    act.wait_ge(s["conv01_step"], i * 9)
                    act.wait_ge(s["conv2_step"], i * 9)
                    act.wait_ge(s["z_spilled"], i * 16)
                act.activation(two_images(pad01[:, 1:2 * H + 3, :])[:, :, :, 1:W + 1],
                               ps[:, 3, 0:T2].rearrange("p (b h w) -> p b h w", b=2, h=H), ACT.Copy
                               ).then_inc(s["pad_ready"], 1)
                act.activation(z_out[:, 0:T2], ps[:, 5, 0:T2], ACT.Silu).then_inc(s["z_ready"], 1)
                act.wait_ge(s["inproj_ready"], i + 1)
                act.activation(pad2[:, 1:H + 1, 1:W + 1],
                               ps[:, 4, 0:T].rearrange("p (h w) -> p h w", h=H), ACT.Copy).then_inc(s["pad_ready"], 1)
                act.activation(z_out[:, T2:TC], ps[:, 4, T:T2], ACT.Silu).then_inc(s["z_ready"], 1)

            def conv_silu(i, first=False):
                if not first:
                    act.wait_ge(s["xc_spilled"], i * 16)
                act.wait_ge(s["conv2_step"], i * 9 + 9)
                act.activation(xc_out[:, T2:TC], conv2_out[:, :, :].rearrange("p h w -> p (h w)"), ACT.Silu).then_inc(s["xc_ready"], 1)
                act.wait_ge(s["conv01_step"], i * 9 + 9)
                act.activation(xc_out[:, 0:T2].rearrange("p (b h w) -> p b h w", b=2, h=H), two_images(conv01_out[:, :, :]), ACT.Silu).then_inc(s["xc_ready"], 1)

            act.wait_ge(s["pad_zero"], 2)
            act.preload_act_table_set("silu_and_others")
            xh_and_z(0, True)
            conv_silu(0, True)
            with act.Fori(1, PAIRS) as i:
                xh_and_z(i)
                conv_silu(i)

            act.preload_act_table_set("natural_log_exp_and_others")
            act.wait_ge(s["inproj_ready"], PAIRS)

            def turn(i):
                act.wait_ge(s["xc_loaded"], i * 16 + 16)
                act.activation(xt.rearrange("p (r w h) -> p r h w", r=3, w=W),
                               xc.rearrange("p (r h w) -> p r h w", r=3, h=H), ACT.Copy).then_inc(s["xt_ready"], 1)

            def read_bc(st, b, first=False):
                act.wait_ge(s["bc_ready"], 2 * st + 2)
                if not first:
                    act.wait_ge(s["dt_ready"], 2 * st)
                    act.wait_ge(s["parts_ready"], st + 0)
                    act.wait_ge(s["cb_ready"], (st - 1) * GRP)
                act.activation(xdbl[:, :], ps[:, 6, 0:T2], ACT.Copy).then_inc(s["xdbl_ready"], 1)
                act.activation(bcs[b][0:96, :], ps[0:96, 6, 0:T2], ACT.Copy).then_inc(s["xdbl_ready"], 1)

            def mid_parts(st, b):
                act.wait_ge(s["resid_ready"], st + 1)
                act.activation(bcs[b][32:64, :], resid[32:64, :], ACT.Copy).then_inc(s["mid_ready"], 1)
                act.activation(midt[64:96, :], resid[64:96, :], ACT.Copy).then_inc(s["mid_ready"], 1)

            def softplus(st, k, first=False):
                act.wait_ge(s["dt_ready"], 2 * st + 2)
                if not first:
                    act.wait_ge(s["delta_ready"], st + 0)
                for lo, hi, bank, table in ((0, T2, 7, par01), (T2, TC, 6, par2)):
                    bias = table[:, P_DTB + k:P_DTB + k + 1]
                    act.activation(soft[:, lo:hi], ps[:, bank, 0:hi - lo], ACT.Abs, bias=bias).then_inc(s["dt_read"], 1)
                    act.activation(relu[:, lo:hi], ps[:, bank, 0:hi - lo], ACT.Relu, bias=bias).then_inc(s["dt_read"], 1)

            def series(st):
                act.wait_ge(s["dt_read"], 4 * st + 4)
                act.activation(soft, soft, ACT.Exp, scale=-1.0).then_inc(s["soft_step"], 1)
                act.wait_ge(s["soft_step"], 4 * st + 1)
                act.activation(lnp, soft, ACT.Ln, bias=1.0).then_inc(s["soft_step"], 1)
                act.activation(poly, soft, ACT.Square, scale=3.0 ** -0.5, bias=series_bias[:, 0:1]).then_inc(s["soft_step"], 1)
                act.wait_ge(s["soft_step"], 4 * st + 3)
                act.activation(poly, poly, ACT.Copy, bias=13.0 / 16.0).then_inc(s["soft_step"], 1)

            def decays(i, k, g, G, b, first=False):
                _, dec = ring_of(k, g)
                r = dec.rearrange("p (r t) -> p r t", t=T)
                lo = 1 if k < 2 else 0
                if g == 0:
                    act.wait_ge(s["delta_ready"], i * K4 + (k + 1))
                if not first:
                    act.wait_ge(s["scan_done"], G - (RING - 1))
                if g < 8:
                    src = delta[b][:, 0:T2].rearrange("p (r t) -> p r t", r=2)[:, :, lo:lo + T - 1]
                    for m in range(2):
                        n = 2 * g + m
                        ins = act.activation(r[:, 2 * m:2 * m + 2, lo:lo + T - 1], src, ACT.Exp,
                                             scale=a01[:, k * N + n:k * N + n + 1], bias=abias01[:, k * N + n:k * N + n + 1])
                else:
                    for m in range(4):
                        n = 4 * (g - 8) + m
                        ins = act.activation(r[:, m, lo:lo + T - 1], delta[b][:, T2 + lo:T2 + lo + T - 1], ACT.Exp,
                                             scale=a2[:, k * N + n:k * N + n + 1], bias=abias2[:, k * N + n:k * N + n + 1])
                ins.then_inc(s["da_ready"], 1)

            def square(i):
                act.wait_ge(s["yc_ready"], i * 2 + 2)
                act.activation(ysq, yc, ACT.Square).then_inc(s["ysq_ready"], 1)

            def rstd(i):
                act.wait_ge(s["var_ready"], i * 2 + 2)
                act.activation(ysq[:, 0:T2], ps[:, 6, 0:T2], ACT.Ln, bias=EPS
                               ).then_inc(s["rstd2_step"], 1)
                act.activation(ysq[:, T2:TC], ps[:, 7, 0:T], ACT.Ln, bias=EPS).then_inc(s["rstd2_step"], 1)
                act.wait_ge(s["rstd2_step"], i * 3 + 2)
                act.activation(ysq, ysq, ACT.Exp, scale=-0.5).then_inc(s["rstd2_step"], 1)

            def pair(i, head):
                for k in range(K4):
                    st = i * K4 + (k + 1)
                    kn, b = (k + 1) % K4, (k + 1) % 2
                    g0 = 1 if k == 1 else 0
                    for g in range(GRP):
                        decays(i, k, g, i * (K4 * GRP) + (k * GRP + g), k % 2, head and k * GRP + g < RING)
                        if g == g0 + 3:
                            read_bc(st, b)
                        if g == g0 + 4:
                            mid_parts(st, b)
                        if g == g0 + 6:
                            softplus(st, kn)
                        if g == g0 + 7:
                            series(st)
                        if not head:
                            if (k, g) == (0, 10):
                                square(i - 1)
                            if (k, g) == (1, 1):
                                rstd(i - 1)
                        if k == 3 and g == 9:
                            turn(i + 1)

            turn(0)
            read_bc(0, 0, True)
            mid_parts(0, 0)
            softplus(0, 0, True)
            series(0)
            act.wait_ge(s["avg_ready"], 14)
            act.wait_ge(s["d_zero"], 2 * RING)
            pair(0, True)
            with act.Fori(1, PAIRS) as i:
                pair(i, False)
            square(PAIRS - 1)
            rstd(PAIRS - 1)

        @block.tensor
        def _(pe):
            def group_average(src, bank, cols, done):
                for oc in range(KC):
                    ks = [k for k in range(KC) if abs(k - oc) < 2]
                    for k in ks:
                        mm = pe.matmul(ps[:, bank, oc * cols:(oc + 1) * cols], gavg[:, k, oc * 128:(oc + 1) * 128],
                                       src[:, k * cols:(k + 1) * cols], start=(k == ks[0]), stop=(k == ks[-1]))
                mm.then_inc(done, 1)

            pe.wait_ge(s["gavg_step"], 3)
            pe.wait_ge(s["a_gn"], 1)
            group_average(gsum, 2, B, s["a_g1"])
            pe.wait_ge(s["a_gn"], 6)
            group_average(gsum, 3, B, s["a_g2"])

            def x_part(p):
                for bank, lo, cols in ((p, 0, G3), (Z_BANK + p, G3, CJ)):
                    for j in range(NJ):
                        pe.matmul(ps[32 * j:32 * j + 32, bank, 0:cols], ones_bf[:, :], bias_parts[:, j, lo:lo + cols],
                                  start=True, stop=False)
                for bank, lo, hi in ((p, 0, 2 * CJ), (Z_BANK + p, 2 * CJ, G3)):
                    for k in range(KC):
                        for j in range(NJ):
                            mm = pe.matmul(ps[32 * j:32 * j + 32, bank, 0:hi - lo], x_cur[:, p, 32 * k:32 * k + 32],
                                           wx_sb[:, k, j, lo:hi], start=False, stop=False)
                mm.then_inc(s["xpart_done"], 1)

            def h_part(p):
                for bank, at, lo, hi, done in ((p, CJ, 0, 2 * CJ, s["r_pre_ready"]), (Z_BANK + p, 0, 2 * CJ, G3, s["z_pre_ready"])):
                    for k in range(KC):
                        for j in range(NJ):
                            mm = pe.matmul(ps[32 * j:32 * j + 32, bank, at:at + hi - lo], h_t[:, 1 - p, 32 * k:32 * k + 32],
                                           wh_sb[:, k, j, lo:hi], start=False, stop=(k == KC - 1))
                    mm.then_inc(done, 1)

            pe.wait_ge(s["gru_weights_in"], 32)
            pe.wait_ge(s["bias_step"], 8)
            pe.wait_ge(s["const_ready"], 3)
            pe.wait_ge(s["x_ready"], 1)
            x_part(0)

            def step(t, p, last=False):
                pe.wait_ge(s["h_ready"], t + 1)
                h_part(p)
                if not last:
                    pe.wait_ge(s["x_ready"], t + 2)
                    x_part(1 - p)

            with pe.Fori(0, T // 2 - 1) as i:
                for p in range(2):
                    step(i * 2 + p, p)
            step(T - 2, 0)
            step(T - 1, 1, True)

            def y_proj(i, first=False):
                if not first:
                    pe.wait_ge(s["x1_ready"], i + 0)
                for oc in range(KC):
                    for k in range(KC):
                        col = i * 2 + k * 32
                        rhs = seq[:, :, col:col + 2] if isinstance(i, int) else seq[:, :, bass.ds(col, 2)]
                        mm = pe.matmul(ps[:, oc, 0:T2].rearrange("p (b t) -> p b t", b=2), wp_sb[:, k, oc * 128:(oc + 1) * 128],
                                       rhs.rearrange("p t b -> p b t"), start=(k == 0), stop=(k == KC - 1))
                mm.then_inc(s["yproj_ready"], 1)

            def in_proj_whole(i, first=False):
                pe.wait_ge(s["xhat_ready"], i * 6 + 6)
                if not first:
                    pe.wait_ge(s["z_ready"], i * 2)
                    pe.wait_ge(s["pad_ready"], i * 2)
                for bank, lo in ((3, 0), (5, DI)):
                    for k in range(KC):
                        mm = pe.matmul(ps[:, bank, 0:T2], win_sb[:, k, lo:lo + 128], xhat[:, k, :], start=(k == 0), stop=(k == KC - 1))
                mm.then_inc(s["inproj_whole"], 1)

            def in_proj_halves(i):
                for col, lo in ((0, 128), (T, DI + 128)):
                    for k in range(KC):
                        for b in range(2):
                            mm = pe.matmul(ps[64 * b:64 * b + 64, 4, col:col + T], win_sb[:, k, lo:lo + 64],
                                           xhat[:, k, b * T:(b + 1) * T], start=(k == 0), stop=(k == KC - 1))
                mm.then_inc(s["inproj_ready"], 1)

            def mean_sums(i):
                pe.wait_ge(s["gn_step"], i * 8 + 1)
                group_average(gsum, 6, 2, s["g1_ready"])

            def var_sums(i):
                pe.wait_ge(s["gn_step"], i * 8 + 6)
                group_average(gsum, 7, 2, s["g2_ready"])

            pe.wait_ge(s["hist_done"], T)
            def project(i, first=False):
                y_proj(i)
                in_proj_whole(i - 1, first)
                mean_sums(i)
                in_proj_halves(i - 1)
                var_sums(i)

            pe.wait_ge(s["late_weights_in"], 16 * LATE_LOADS)
            y_proj(0, True)
            mean_sums(0)
            var_sums(0)
            project(1, True)
            with pe.Fori(2, PAIRS) as i:
                project(i)
            in_proj_whole(PAIRS - 1)
            in_proj_halves(PAIRS - 1)

            def bc_proj(i, k, st, bc, first=False):
                x = xt if k % 2 else xc
                if bc == 0:
                    pe.wait_ge(s["xc_loaded"], i * 16 + 16)
                    if k % 2:
                        pe.wait_ge(s["xt_ready"], i + 1)
                    if not first:
                        pe.wait_ge(s["dt_read"], 4 * st)
                for tile in range(3):
                    mm = pe.matmul(ps[:, 6, bc * T:(bc + 1) * T], bc_w[:, k, bc, tile, :], x[:, tile * T:(tile + 1) * T],
                                   start=(tile == 0), stop=(tile == 2))
                mm.then_inc(s["bc_ready"], 1)

            def dt_proj(k, st, part):
                if part == 0:
                    pe.wait_ge(s["xdbl_ready"], 2 * st + 2)
                    pe.matmul(ps[:, 7, 0:T2], dt_w[:, k, 0, :], xdbl[:, :], start=True, stop=True).then_inc(s["dt_ready"], 1)
                else:
                    pe.matmul(ps[:, 6, 0:T], dt_w[:, k, 1, :], xdbl[:, 0:T], start=True, stop=False)
                    pe.matmul(ps[:, 6, 0:T], dt_w[:, k, 2, :], xdbl[:, T:T2], start=False, stop=True).then_inc(s["dt_ready"], 1)

            def spread(g, part, bank, b, done):
                rhs = bcs[b][0:96, part * T:(part + 1) * T]
                for m in range(4):
                    n, kind = (2 * g + m // 2, m % 2) if g < 8 else (4 * (g - 8) + m, 2)
                    mm = pe.matmul(ps[:, bank + m // 2, m % 2 * T:m % 2 * T + T], sel[:, n, kind, :], rhs, start=True, stop=True)
                mm.then_inc(done, 1)

            def reduce(k, g, G, start, stop):
                q, _ = ring_of(k, g)
                runs = 2 if g < 8 else 4
                pe.wait_ge(s["m3_done"], G + 1)
                for m in range(runs):
                    cols = GC // runs
                    bank = 4 if g < 8 else 5
                    src = hb[q][:, m * cols:(m + 1) * cols]
                    dst = ps[:, bank, 0:cols]
                    if k % 2:
                        src = src.rearrange("p (r w h) -> p r h w", w=W, h=H)
                        dst = dst.rearrange("p (r h w) -> p r h w", h=H, w=W)
                    mm = pe.matmul(dst, ident[:, :], src, start=(start and m == 0), stop=(stop and m == runs - 1))
                mm.then_inc(s["red_done"], 1)

            def first_of_pair(k, g):
                return k == 0 and g in (0, 8)

            def last_of_pair(k, g):
                return k == K4 - 1 and g in (7, GRP - 1)

            def averages(src, part, done):
                if part == 0:
                    pe.matmul(ps[:, 6, 0:T2], avg[:, 0, :], src[:, 0:T2], start=True, stop=False)
                    pe.matmul(ps[:, 6, 0:T], avg[:, 1, :], src[:, T2:TC], start=False, stop=False)
                    pe.matmul(ps[:, 6, T:T2], avg[:, 2, :], src[:, T2:TC], start=False, stop=True).then_inc(done, 1)
                else:
                    pe.matmul(ps[:, 7, 0:T], avg[:, 3, :], src[:, T2:TC], start=True, stop=False)
                    pe.matmul(ps[:, 7, 0:T], avg[:, 4, :], src[:, 0:T], start=False, stop=False)
                    pe.matmul(ps[:, 7, 0:T], avg[:, 5, :], src[:, T:T2], start=False, stop=True).then_inc(done, 1)

            def mean(i, part, dt_reads):
                if part == 0:
                    pe.wait_ge(s["y_drained"], i * 2 + 2)
                    pe.wait_ge(s["dt_read"], dt_reads)
                averages(ysb, part, s["mean_ready"])

            def var(i, part):
                if part == 0:
                    pe.wait_ge(s["ysq_ready"], i + 1)
                averages(ysq, part, s["var_ready"])

            def out_proj(i, oc):
                bank = 6 + oc % 2
                pe.wait_ge(s["gated"], i * 2 + 2)
                if oc == 2:
                    pe.wait_ge(s["o_ready"], i * 3 + 1)
                c = slice(oc * 128, (oc + 1) * 128)
                pe.matmul(ps[:, bank, 0:T2], wout01[:, c], yc[:, 0:T2], start=True, stop=False)
                for b in range(2):
                    mm = pe.matmul(ps[:, bank, b * T:(b + 1) * T], wout2[:, b, c],
                                   yc[:, T2:TC], start=False, stop=(b == 1))
                mm.then_inc(s["oproj_ready"], 1)

            def pair(i, head):
                for k in range(K4):
                    st = i * K4 + (k + 1)
                    inext, kn = (i, k + 1) if k + 1 < K4 else (i + 1, 0)
                    g0 = 1 if k == 1 else 0
                    for g in range(GRP):
                        G = i * (K4 * GRP) + (k * GRP + g)
                        if g == GRP - 1:
                            pe.wait_ge(s["parts_ready"], st + 1)
                        pe.wait_ge(s["m1_done"], G + 1)
                        spread((g + 1) % GRP, 0, 0, (k if g < GRP - 1 else k + 1) % 2, s["bb_ready"])
                        if not (head and k == 0 and g == 0):
                            pe.wait_ge(s["m3_done"], G + 0)
                        spread(g, 1, 2, k % 2, s["cb_ready"])
                        if (k, g) != (0, 0):
                            kp, gp = (k, g - 1) if g else (k - 1, GRP - 1)
                            if (kp, gp) == (0, 0) and not head:
                                pe.wait_ge(s["y_drained"], i * 2)
                            reduce(kp, gp, G - 1, first_of_pair(kp, gp), last_of_pair(kp, gp))
                        elif not head:
                            reduce(K4 - 1, GRP - 1, G - 1, False, True)
                        if g in (g0, g0 + 1):
                            if g == g0 and not head:
                                if k == 1:
                                    pe.wait_ge(s["rstd2_step"], i * 3)
                                if k == 2:
                                    pe.wait_ge(s["o_ready"], i * 3)
                            bc_proj(inext, kn, st, g - g0)
                        if g in (g0 + 3, g0 + 4):
                            dt_proj(kn, st, g - g0 - 3)
                        if not head:
                            if k == 0 and g in (5, 6):
                                mean(i - 1, g - 5, 4 * st + 4)
                            if k == 0 and g in (9, 10):
                                var(i - 1, g - 9)
                            if k == 1 and 6 <= g < 6 + KC:
                                if g == 6:
                                    pe.wait_ge(s["dt_read"], 4 * st + 4)
                                out_proj(i - 1, g - 6)

            pe.wait_ge(s["bcw_step"], 13)
            pe.wait_ge(s["sel_step"], 13)
            pe.wait_ge(s["ident_ready"], 1)
            pe.wait_ge(s["z_ready"], 2 * PAIRS)
            pe.wait_ge(s["pad_ready"], 2 * PAIRS)
            pe.wait_ge(s["gn_step"], 8 * PAIRS)
            pe.wait_ge(s["avg_ready"], 14)
            for part in range(2):
                bc_proj(0, 0, 0, part, True)
            for part in range(2):
                dt_proj(0, 0, part)
            pe.wait_ge(s["parts_ready"], 1)
            spread(0, 0, 0, 0, s["bb_ready"])
            pair(0, True)
            with pe.Fori(1, PAIRS) as i:
                pair(i, False)
            reduce(K4 - 1, GRP - 1, PAIRS * K4 * GRP - 1, False, True)
            for part in range(2):
                mean(PAIRS - 1, part, 4 * (K4 * PAIRS + 1))
            for part in range(2):
                var(PAIRS - 1, part)
            for oc in range(KC):
                if oc == 0:
                    pe.wait_ge(s["rstd2_step"], 3 * PAIRS)
                out_proj(PAIRS - 1, oc)


def dram(t, i):
    return t[i] if isinstance(i, int) else t[bass.ds(i, 1), :, :].rearrange("o p c -> (o p) c")


def flat(t):
    return t[:, :, :].rearrange("p a b -> p (a b)")


def kernel(**inputs):
    import numpy as np
    import concourse.bacc as bacc
    from concourse.bass_utils import run_bass_kernel_spmd as run

    a = {k: np.asarray(v) for k, v in inputs.items()}
    x = a["x"]
    lay = {
        "x_seq": x.reshape(B, T, KC, 128).transpose(3, 1, 2, 0).reshape(128, T, SEQ),
        "x_pair": x.reshape(PAIRS, 2, T, KC, 128).transpose(0, 4, 3, 1, 2).reshape(PAIRS, 128, KC * T2),
        "wx": a["L0_conv_Wx"].reshape(3, NJ, CJ, KC, 128)[[2, 1, 0]].transpose(4, 3, 1, 0, 2).reshape(128, KC, NJ, G3),
        "wh": a["L0_conv_Wh"].reshape(3, NJ, CJ, NJ, KC, 32)[[1, 2, 0]].transpose(3, 5, 4, 1, 0, 2).reshape(128, KC, NJ, G3),
        "bx": a["L0_conv_bx"].reshape(3, NJ, CJ)[[2, 1, 0]].transpose(1, 0, 2).reshape(1, NJ * G3),
        "bh": a["L0_conv_bh"].reshape(3, NJ, CJ)[[1, 2, 0]].transpose(1, 0, 2).reshape(1, NJ * G3),
        "wp": a["L0_conv_Wp"].reshape(C, NJ, KC, 32).transpose(1, 3, 2, 0).reshape(128, KC, C),
        "win": a["L1_conv_in_proj_w"].reshape(C, KC, 128).transpose(2, 1, 0),
        "par": np.concatenate([
            a["L1_conv_conv_w"].reshape(DI, 9), a["L1_conv_conv_b"].reshape(DI, 1), a["L1_conv_dt_projs_b"].T,
            a["L1_conv_A_logs"].reshape(K4, DI, N).transpose(1, 0, 2).reshape(DI, K4 * N),
            a["L1_conv_Ds"].reshape(K4, DI).T, a["L1_conv_out_norm_g"].reshape(DI, 1),
            a["L1_conv_out_norm_b"].reshape(DI, 1)], axis=1),
        "xproj": a["L1_conv_x_proj_w"].transpose(2, 0, 1).reshape(DI, K4 * (R + 2 * N)),
        "dtproj": a["L1_conv_dt_projs_w"].transpose(2, 0, 1),
        "wout": a["L1_conv_out_proj_w"].T,
    }
    nc = bacc.Bacc("TRN2", target_bir_lowering=False, num_devices=1)
    arrays, args = {}, []
    for name, v in lay.items():
        v = np.ascontiguousarray(v)
        arrays[name] = v
        args.append(nc.dram_tensor(name, v.shape, mybir.dt.from_np(v.dtype), kind="ExternalInput").ap())
    args.append(nc.dram_tensor("out_0", (PAIRS, 128, KC * T2), F32, kind="ExternalOutput").ap())
    build(nc, *args)
    r = run(nc, [arrays], core_ids=[0])
    o = r.results[0]["out_0"].reshape(PAIRS, 128, KC, 2, T)
    return o.transpose(0, 3, 4, 2, 1).reshape(B, H, W, C)
```

```python
from contextlib import ExitStack

import concourse.bass as bass
from concourse import mybir

F32 = mybir.dt.float32
BF16 = mybir.dt.bfloat16
ALU = mybir.AluOpType
ACT = mybir.ActivationFunctionType

B, H, W, C = 32, 14, 14, 384
T = H * W
KC = C // 128
NJ = 4
CJ = C // NJ
SEQ = KC * B
G3 = 3 * CJ
Z_BANK = 4
GN = 12
PAIRS = B // 2
DI = C // 2
N = 16
R = 24
K4 = 4
T2 = 2 * T
TC = 3 * T
GRP = 12
GC = 4 * T
RING = 4
EPS = 1e-5
UNROLL = 16
A_LOG_MAX = 88.72
SMALL = 0.022
P_CW, P_CB, P_DTB, P_AL, P_DS, P_G, P_B = 0, 9, 10, 14, 78, 82, 83
NP = 84


def build(nc, x_seq, x_pair, wx, wh, bx, bh, wp, win, par, xproj, dtproj, wout, out):
    x1_dram = nc.dram_tensor("x1_dram", [PAIRS, 128, KC * T2], F32)
    z_dram = nc.dram_tensor("z_dram", [PAIRS, 128, TC], F32)
    xc_dram = nc.dram_tensor("xc_dram", [PAIRS + 1, 128, TC], F32)

    with ExitStack() as ctx:
        def sb(name, shape, dt=F32):
            return ctx.enter_context(nc.sbuf_tensor(name, shape, dt))

        def sem(name):
            return ctx.enter_context(nc.semaphore(name))

        arena = sb("arena", [128, T * SEQ])
        wx_sb = sb("wx_sb", [128, KC, NJ, G3])
        wh_sb = sb("wh_sb", [128, KC, NJ, G3])
        wp_sb = sb("wp_sb", [128, KC, C])
        win_sb = sb("win_sb", [128, KC, C])
        par01 = sb("par01", [128, NP])
        par2 = sb("par2", [128, NP])
        gavg = sb("gavg", [128, KC, C])
        gru_bias = sb("gru_bias", [128, 4 * CJ])
        bias_x = sb("bias_x", [128, G3])
        bias_h = sb("bias_h", [128, G3])
        ident = sb("ident", [128, 128])
        sel = sb("sel", [96, N, 3, 128], BF16)
        bc_w = sb("bc_w", [128, K4, 2, 3, 128])
        dt_w = sb("dt_w", [128, K4, 3, 128])
        wout01 = sb("wout01", [128, C])
        wout2 = sb("wout2", [128, 2, C])
        avg = sb("avg", [128, 6, 128])
        centring = sb("centring", [128, 6, 128])
        a01 = sb("a01", [128, K4 * N])
        a2 = sb("a2", [128, K4 * N])
        abias01 = sb("abias01", [128, K4 * N])
        abias2 = sb("abias2", [128, K4 * N])
        dsum01 = sb("dsum01", [128, 1])
        dsum2 = sb("dsum2", [128, 1])
        neg_half = sb("neg_half", [128, SEQ])
        series_bias = sb("series_bias", [128, 1])
        stats = sb("stats", [128, SEQ, 4, 3])
        gsum = sb("gsum", [128, SEQ])
        gmean = sb("gmean", [128, SEQ])
        grstd = sb("grstd", [128, SEQ])
        dev = sb("dev", [128, SEQ, 4])
        x_tmp = sb("x_tmp", [128, SEQ])
        x_cur = sb("x_cur", [128, 2, SEQ])
        h_nat = sb("h_nat", [128, CJ])
        h_t = sb("h_t", [128, 2, CJ])
        z_gate = sb("z_gate", [128, CJ])
        r_gate = sb("r_gate", [128, CJ])
        rh = sb("rh", [128, CJ])
        r_pre = sb("r_pre", [128, CJ])
        z_pre = sb("z_pre", [128, CJ])
        n_parts = sb("n_parts", [128, 2, CJ])
        cand_pre = sb("cand_pre", [128, CJ])
        cand = sb("cand", [128, CJ])
        zh = sb("zh", [128, CJ])
        blend = sb("blend", [128, CJ])
        x_in = sb("x_in", [128, KC, T2])
        x1 = sb("x1", [128, KC, T2])
        xhat = sb("xhat", [128, KC, T2])
        pad01 = sb("pad01", [128, 2 * H + 3, W + 2])
        pad2 = sb("pad2", [128, H + 2, W + 2])
        conv01_out = sb("conv01_out", [128, 2 * H + 2, W])
        conv2_out = sb("conv2_out", [128, H, W])
        xc_out = sb("xc_out", [128, TC])
        z_out = sb("z_out", [128, TC])

        ps = ctx.enter_context(nc.psum_tensor("ps", [128, 8, 512], F32))

        seq = arena[:, :].rearrange("p (t c) -> p t c", c=SEQ)

        used = [0]

        def carve(cols, shape=None):
            a = arena[:, used[0]:used[0] + cols]
            used[0] += cols
            return a

        wx_cols = wx_sb[:, :, :, :].rearrange("p a b c -> p (a b c)")
        spare = [wx_cols[:, q * GC:(q + 1) * GC] for q in range(3)]
        da = [[carve(GC) for _ in range(RING - 1)] + [spare[d]] for d in range(2)]
        hb = [carve(GC) for _ in range(RING - 1)] + [spare[2]]
        delta = [carve(TC) for _ in range(2)]
        du = [carve(TC) for _ in range(2)]
        xc = carve(TC)
        xt = carve(TC)
        xdbl = carve(T2)
        resid = carve(T2)
        bcs = [carve(T2 // 2).bitcast(BF16) for _ in range(2)]
        midt = carve(T2 // 2).bitcast(BF16)
        soft = carve(TC)
        relu = carve(TC)
        lnp = carve(TC)
        poly = carve(TC)
        xc_fin = carve(TC)
        z_fin = carve(TC)
        ysb = carve(TC)
        yc = carve(TC)
        ysq = carve(TC)
        x1_fin = x1[:, :, :]
        o_sb = carve(KC * T2).rearrange("p (a b) -> p a b", a=KC)
        assert used[0] <= T * SEQ

        s = {n: sem(n) for n in (
            "params_in", "gru_weights_in", "late_weights_in", "dt_w_clear", "xload0", "xload1", "ident0", "ident_ready", "sel_step", "gavg_step", "const_ready", "staging_clear",
            "split_step", "a_exp", "a_capped",
            "bias_step", "bcw_step", "avg_ready", "a_step",
            "st_done", "a_gn", "a_g1", "a_g2", "a_std", "a_rstd",
            "xs_tmp", "x_ready", "xpart_done", "h_ready", "r_pre_ready", "z_pre_ready", "r_ready", "z_gate_ready", "rh_ready", "r_biased", "n_biased", "z_biased",
            "pre_ready", "tanh_ready", "mix_step", "hnat_ready", "hist_done",
            "xin_ready", "yproj_ready", "x1_ready", "x1_spilled", "stats_ready", "gn_step", "g1_ready",
            "g2_ready", "rstd_ready", "xhat_ready", "inproj_ready", "inproj_whole", "pad_ready", "z_ready", "conv01_step",
            "conv2_step", "xc_ready", "z_spilled", "xc_spilled", "xc_dup", "pad_zero",
            "d_zero", "xc_loaded", "xt_ready", "bc_ready", "xdbl_ready", "resid_ready", "mid_ready",
            "parts_ready", "dt_ready", "dt_read", "soft_step", "series_step", "choice_ready", "log_ready", "delta_ready", "du_ready", "bb_ready",
            "cb_ready", "da_ready", "m1_done", "scan_done", "m3_done", "red_done", "y_drained",
            "centred", "centre_ready", "yc_ready", "ysq_ready", "var_ready", "rstd2_step", "norm_step", "gated",
            "oproj_ready", "o_ready", "out_stored", "fin_x", "fin_z", "fin_x1")}

        convs = ((pad01, conv01_out, 2 * H + 1, par01, s["conv01_step"]), (pad2, conv2_out, H, par2, s["conv2_step"]))

        def conv_taps(eng, i, taps):
            for tap in taps:
                for pad, conv, rows, table, step in convs:
                    win_ = pad[:, tap // 3:tap // 3 + rows, tap % 3:tap % 3 + W]
                    dst = conv[:, 0:rows, :]
                    wv = table[:, P_CW + tap:P_CW + tap + 1]
                    if tap == 0:
                        ins = eng.tensor_scalar(dst, win_, wv, table[:, P_CB:P_CB + 1], ALU.mult, ALU.add)
                    else:
                        eng.wait_ge(step, i * 9 + tap)
                        ins = eng.scalar_tensor_tensor(dst, win_, wv, dst, ALU.mult, ALU.add)
                    ins.then_inc(step, 1)

        def two_images(rows):
            return rows.rearrange("p (b r) w -> p b r w", b=2)[:, :, 0:H, :]

        def group_aps(g):
            if g < 8:
                return (lambda a: a[:, 0:T2].unsqueeze(1).broadcast_to([128, 2, T2]),
                        lambda bank: ps[:, bank:bank + 2, 0:T2],
                        lambda a: a.rearrange("p (m c) -> p m c", m=2))
            return (lambda a: a[:, T2:TC].unsqueeze(1).unsqueeze(1).broadcast_to([128, 2, 2, T]),
                    lambda bank: ps[:, bank:bank + 2, 0:T2].rearrange("p m (q t) -> p m q t", q=2),
                    lambda a: a.rearrange("p (m q t) -> p m q t", m=2, q=2))

        def ring_of(k, g):
            return (k * GRP + g) % RING, da[k // 2][(k % 2 * GRP + g) % RING]

        block = ctx.enter_context(nc.Block())

        PARAM_LOADS, LATE_LOADS = 6 + 2 * NJ, 8
        HALF = T // 2

        @block.sync
        def _(sp):
            stage = x1[:, :, :].rearrange("p a b -> p (a b)")
            n56 = K4 * (R + 2 * N)
            for dst, src in (
                    (par01[:, :], par[0:128, :]), (par2[0:64, :], par[128:DI, :]), (par2[64:128, :], par[128:DI, :]),
                    (stage[:, 0:n56], xproj[0:128, :]), (stage[0:64, n56:2 * n56], xproj[128:DI, :]),
                    (stage[64:128, n56:2 * n56], xproj[128:DI, :])):
                sp.dma_start(dst, src).then_inc(s["params_in"], 16)
            for j in range(NJ):
                sp.dma_start(bias_x[32 * j:32 * j + 32, :], bx[j:j + 1, :].broadcast_to([32, G3])).then_inc(s["params_in"], 16)
                sp.dma_start(bias_h[32 * j:32 * j + 32, :], bh[j:j + 1, :].broadcast_to([32, G3])).then_inc(s["params_in"], 16)
            for h in range(2):
                sp.dma_start(seq[:, h * HALF:(h + 1) * HALF, :],
                             x_seq[:, h * HALF:(h + 1) * HALF, :]).then_inc(s[f"xload{h}"], 16)
            sp.dma_start(wx_sb[:, :, :, :], wx).then_inc(s["gru_weights_in"], 16)
            sp.dma_start(wh_sb[:, :, :, :], wh).then_inc(s["gru_weights_in"], 16)
            sp.wait_ge(s["dt_w_clear"], 1)
            for dst, src in (
                    (wp_sb[:, :, :], wp), (win_sb[:, :, :], win),
                    (wout01[:, :], wout[0:128, :]), (wout2[0:64, 0, :], wout[128:DI, :]), (wout2[64:128, 1, :], wout[128:DI, :]),
                    (dt_w[96:96 + R, :, 0, :], dtproj[:, :, 0:128]), (dt_w[96:96 + R, :, 1, 0:64], dtproj[:, :, 128:DI]),
                    (dt_w[96:96 + R, :, 2, 64:128], dtproj[:, :, 128:DI])):
                sp.dma_start(dst, src).then_inc(s["late_weights_in"], 16)

            sp.dma_start(x_in[:, :, :], x_pair[0]).then_inc(s["xin_ready"], 16)

            def load_x(i):
                sp.wait_ge(s["xin_ready"], i * 16)
                sp.dma_start(flat(x_in), dram(x_pair, i)).then_inc(s["xin_ready"], 16)

            def spill_z(i):
                sp.wait_ge(s["z_ready"], i * 2 + 2)
                sp.dma_start(dram(z_dram, i), z_out[:, :]).then_inc(s["z_spilled"], 16)

            def spill_xc(i):
                sp.wait_ge(s["xc_ready"], i * 2 + 2)
                sp.dma_start(dram(xc_dram, i), xc_out[:, :]).then_inc(s["xc_spilled"], 16)

            def spill_a(i):
                sp.wait_ge(s["x1_ready"], i + 1)
                sp.wait_ge(s["x1_spilled"], i * 16)
                sp.dma_start(dram(x1_dram, i), flat(x1)).then_inc(s["x1_spilled"], 16)

            sp.wait_ge(s["x1_ready"], 1)
            sp.dma_start(dram(x1_dram, 0), flat(x1)).then_inc(s["x1_spilled"], 16)
            load_x(1)
            spill_a(1)
            spill_z(0)
            with sp.Fori(2, PAIRS) as i:
                load_x(i)
                spill_a(i)
                spill_xc(i - 2)
                spill_z(i - 1)
            spill_xc(PAIRS - 2)
            sp.wait_ge(s["yproj_ready"], PAIRS)
            sp.wait_ge(s["xc_spilled"], 16 * (PAIRS - 1))
            sp.dma_start(xc, dram(xc_dram, 0)).then_inc(s["xc_loaded"], 16)
            spill_z(PAIRS - 1)
            spill_xc(PAIRS - 1)
            sp.dma_start(dram(xc_dram, PAIRS), xc_out[:, :]).then_inc(s["xc_dup"], 16)
            sp.wait_ge(s["xc_dup"], 16)

            sp.wait_ge(s["xc_spilled"], 16 * PAIRS)
            sp.wait_ge(s["z_spilled"], 16 * PAIRS)
            sp.wait_ge(s["x1_spilled"], 16 * PAIRS)

            def fin_loads(i):
                sp.dma_start(xc_fin, dram(xc_dram, i)).then_inc(s["fin_x"], 16)
                sp.dma_start(z_fin, dram(z_dram, i)).then_inc(s["fin_z"], 16)
                sp.dma_start(flat(x1), dram(x1_dram, i)).then_inc(s["fin_x1"], 16)

            def next_x(i):
                sp.wait_ge(s["du_ready"], i * 4 + 4)
                sp.dma_start(xc, dram(xc_dram, i + 1)).then_inc(s["xc_loaded"], 16)

            def store(i):
                sp.wait_ge(s["o_ready"], i * 3 + 3)
                sp.dma_start(dram(out, i), o_sb.rearrange("p a b -> p (a b)")).then_inc(s["out_stored"], 16)

            fin_loads(0)
            next_x(0)
            with sp.Fori(1, PAIRS) as i:
                store(i - 1)
                sp.wait_ge(s["out_stored"], i * 16)
                sp.wait_ge(s["fin_x"], i * 16)
                sp.wait_ge(s["fin_z"], i * 16)
                sp.wait_ge(s["fin_x1"], i * 16)
                fin_loads(i)
                next_x(i)
            store(PAIRS - 1)
            sp.wait_ge(s["out_stored"], 16 * PAIRS)

        @block.gpsimd
        def _(pool):
            pool.memset(dt_w[:, :, :, :], 0.0).then_inc(s["dt_w_clear"], 1)
            pool.memset(ident[:, :], 0.0).then_inc(s["ident0"], 1)
            pool.wait_ge(s["ident0"], 1)
            pool.affine_select(out=ident[:, :], in_=ident[:, :], compare_op=ALU.not_equal, fill=1.0, base=0,
                               pattern=[[-1, 128]], channel_multiplier=1).then_inc(s["ident_ready"], 1)
            g = gavg[:, :, :].rearrange("p k (g i) -> p k g i", i=GN)
            pool.memset(gavg[:, :, :], 1.0 / GN).then_inc(s["gavg_step"], 1)
            pool.wait_ge(s["gavg_step"], 1)
            pool.affine_select(out=g, in_=g, compare_op=ALU.is_ge, fill=0.0, base=0,
                               pattern=[[128, KC], [-GN, C // GN], [0, GN]], channel_multiplier=1
                               ).then_inc(s["gavg_step"], 1)
            pool.wait_ge(s["gavg_step"], 2)
            pool.affine_select(out=g, in_=g, compare_op=ALU.is_ge, fill=0.0, base=GN - 1,
                               pattern=[[-128, KC], [GN, C // GN], [0, GN]], channel_multiplier=-1
                               ).then_inc(s["gavg_step"], 1)
            pool.memset(neg_half[:, :], -0.5).then_inc(s["gavg_step"], 1)
            pool.memset(sel[:, :, :, :], 0.0).then_inc(s["sel_step"], 1)
            step = 1
            for part in range(3):
                for kind, lo, hi, img in ((0, 0, 128, 0), (1, 0, 128, 1), (2, 0, 64, 0), (2, 64, 128, 1)):
                    v = sel[:, :, kind, lo:hi]
                    pool.wait_ge(s["sel_step"], step)
                    pool.affine_select(out=v, in_=v, compare_op=ALU.not_equal, fill=1.0,
                                       base=-(32 * part + N * img), pattern=[[-1, N], [0, hi - lo]],
                                       channel_multiplier=1).then_inc(s["sel_step"], 1)
                    step += 1
            pool.memset(pad01[:, :, :], 0.0).then_inc(s["pad_zero"], 1)
            pool.memset(pad2[:, :, :], 0.0).then_inc(s["pad_zero"], 1)

            pool.wait_ge(s["a_rstd"], 1)

            def norm(t, p, first=False):
                if not first:
                    pool.wait_ge(s["x_ready"], t + 0)
                pool.tensor_tensor(x_tmp[:, :], tok(t), gmean[:, :], ALU.subtract).then_inc(s["xs_tmp"], 1)
                pool.wait_ge(s["xs_tmp"], t + 1)
                if not first:
                    pool.wait_ge(s["xpart_done"], t - 1)
                pool.tensor_tensor(x_cur[:, p, :], x_tmp[:, :], grstd[:, :], ALU.mult).then_inc(s["x_ready"], 1)

            def tok(t):
                return arena[:, bass.ds(t * SEQ, SEQ)] if not isinstance(t, int) else arena[:, t * SEQ:(t + 1) * SEQ]

            def keep(t, p):
                pool.wait_ge(s["h_ready"], t + 2)
                pool.tensor_copy(tok(t), h_t[:, p, :]).then_inc(s["hist_done"], 1)

            norm(0, 0, True)
            pool.wait_ge(s["x_ready"], 1)
            norm(1, 1, True)
            with pool.Fori(0, T // 2 - 1) as i:
                for p in range(2):
                    norm(i * 2 + (p + 2), p)
                    keep(i * 2 + p, p)
            keep(T - 2, 0)
            keep(T - 1, 1)

            pool.wait_ge(s["gavg_step"], 4)

            def rstd_c(i):
                pool.wait_ge(s["gn_step"], i * 8 + 7)
                pool.tensor_tensor(grstd[:, 0:6], gsum[:, 0:6], neg_half[:, 0:6], ALU.pow).then_inc(s["rstd_ready"], 1)

            pool.wait_ge(s["hist_done"], T)
            rstd_c(0)
            with pool.Fori(1, PAIRS) as i:
                rstd_c(i)

            def small_parts(st, b):
                pool.wait_ge(s["xdbl_ready"], 2 * st + 2)
                pool.tensor_tensor(resid[0:96, :], xdbl[0:96, :], bcs[b][0:96, :], ALU.subtract).then_inc(s["resid_ready"], 1)
                pool.wait_ge(s["mid_ready"], 2 * st + 2)
                pool.tensor_tensor(bcs[b][64:96, :], resid[64:96, :], midt[64:96, :], ALU.subtract).then_inc(s["parts_ready"], 1)

            def deltas(st, k, b, first=False):
                pool.wait_ge(s["parts_ready"], st + 1)
                pool.wait_ge(s["soft_step"], 4 * st + 4)
                pool.tensor_tensor(poly, poly, soft, ALU.mult).then_inc(s["series_step"], 1)
                pool.wait_ge(s["series_step"], 2 * st + 1)
                pool.tensor_tensor(poly, poly, lnp, ALU.subtract).then_inc(s["series_step"], 1)
                pool.wait_ge(s["series_step"], 2 * st + 2)
                pool.tensor_tensor(lnp, lnp, relu, ALU.add).then_inc(s["log_ready"], 1)
                pool.wait_ge(s["choice_ready"], st + 1)
                pool.wait_ge(s["log_ready"], st + 1)
                if not first:
                    pool.wait_ge(s["da_ready"], (st - 1) * GRP)
                pool.tensor_tensor(delta[b], lnp, poly, ALU.add).then_inc(s["delta_ready"], 1)
                pool.wait_ge(s["delta_ready"], st + 1)
                if not first:
                    pool.wait_ge(s["m1_done"], (st - 1) * GRP)
                pool.tensor_tensor(du[b], delta[b], xt if k % 2 else xc, ALU.mult).then_inc(s["du_ready"], 1)

            pool.wait_ge(s["xc_loaded"], 16)
            small_parts(0, 0)
            deltas(0, 0, 0, True)

            def pair(i):
                for k in range(K4):
                    st = i * K4 + (k + 1)
                    small_parts(st, (k + 1) % 2)
                    deltas(st, (k + 1) % K4, (k + 1) % 2)

            pair(0)
            with pool.Fori(1, PAIRS) as i:
                pair(i)

        @block.vector
        def _(dve):
            dve.memset(series_bias[:, :], -(3.0 ** 0.5) / 4.0).then_inc(s["const_ready"], 1)
            dve.memset(h_nat[:, :], 0.0).then_inc(s["const_ready"], 1)
            dve.memset(h_t[:, 1, :], 0.0).then_inc(s["h_ready"], 1)
            dve.memset(bc_w[:, :, :, :, :], 0.0).then_inc(s["bcw_step"], 1)
            dve.memset(avg[:, :, :], 0.0).then_inc(s["avg_ready"], 1)
            dve.wait_ge(s["avg_ready"], 1)
            dve.memset(avg[:, 0, :], 1.0 / DI).then_inc(s["avg_ready"], 1)
            dve.memset(avg[0:64, 1, :], 1.0 / DI).then_inc(s["avg_ready"], 1)
            dve.memset(avg[64:128, 2, :], 1.0 / DI).then_inc(s["avg_ready"], 1)
            dve.memset(avg[0:64, 3, 0:64], 1.0 / DI).then_inc(s["avg_ready"], 1)
            dve.memset(avg[64:128, 3, 64:128], 1.0 / DI).then_inc(s["avg_ready"], 1)
            dve.memset(wout2[64:128, 0, :], 0.0).then_inc(s["avg_ready"], 1)
            dve.memset(wout2[0:64, 1, :], 0.0).then_inc(s["avg_ready"], 1)
            dve.memset(avg[:, 4, 0:64], 1.0 / DI).then_inc(s["avg_ready"], 1)
            dve.memset(avg[:, 5, 64:128], 1.0 / DI).then_inc(s["avg_ready"], 1)
            dve.wait_ge(s["params_in"], 16 * PARAM_LOADS)
            dve.wait_ge(s["bcw_step"], 1)
            stage = x1[:, :, :].rearrange("p a b -> p (a b)")
            n56 = K4 * (R + 2 * N)
            for rows, tile, img, col in ((slice(0, 128), 0, 0, 0), (slice(0, 128), 1, 1, 0),
                                         (slice(0, 64), 2, 0, n56), (slice(64, 128), 2, 1, n56)):
                src = stage[rows, col:col + n56].rearrange("p (k m) -> p k m", k=K4)
                rn = rows.stop - rows.start
                for bc in range(2):
                    dst = bc_w[rows, :, bc, tile, 0:96].rearrange("p k (q m) -> p k q m", q=3)[:, :, :, N * img:N * img + N]
                    dve.tensor_copy(dst, src[:, :, R + N * bc:R + N * bc + N].unsqueeze(2).broadcast_to([rn, K4, 3, N])
                                    ).then_inc(s["bcw_step"], 1)
                dve.tensor_copy(bc_w[rows, :, img, tile, 96:96 + R], src[:, :, 0:R]).then_inc(s["bcw_step"], 1)
            for at, from_x, from_h in ((0, 0, None), (CJ, CJ, 0), (2 * CJ, None, CJ), (G3, 2 * CJ, 2 * CJ)):
                dst = gru_bias[:, at:at + CJ]
                if from_h is None:
                    ins = dve.tensor_copy(dst, bias_x[:, from_x:from_x + CJ])
                elif from_x is None:
                    ins = dve.tensor_copy(dst, bias_h[:, from_h:from_h + CJ])
                else:
                    ins = dve.tensor_tensor(dst, bias_x[:, from_x:from_x + CJ], bias_h[:, from_h:from_h + CJ], ALU.add)
                ins.then_inc(s["bias_step"], 1)
            for src, dst, bias in ((par01, a01, abias01), (par2, a2, abias2)):
                src = src[:, P_AL:P_AL + K4 * N]
                dve.tensor_scalar(dst[:, :], src, A_LOG_MAX, None, ALU.min).then_inc(s["a_capped"], 1)
                dve.tensor_scalar(bias[:, :], src, A_LOG_MAX, -1e30, ALU.is_gt, ALU.mult).then_inc(s["a_capped"], 1)
            dve.wait_ge(s["avg_ready"], 10)
            dve.wait_ge(s["ident_ready"], 1)
            dve.tensor_scalar(centring[:, :, :], avg[:, :, :], -1.0, None, ALU.mult).then_inc(s["centre_ready"], 1)
            dve.wait_ge(s["centre_ready"], 1)
            for kind in (0, 3):
                dve.tensor_tensor(centring[:, kind, :], centring[:, kind, :], ident[:, :], ALU.add).then_inc(s["centre_ready"], 1)
            dve.tensor_reduce(dsum01[:, :], par01[:, P_DS:P_DS + K4], mybir.AxisListType.X, ALU.add).then_inc(s["avg_ready"], 1)
            dve.tensor_reduce(dsum2[:, :], par2[:, P_DS:P_DS + K4], mybir.AxisListType.X, ALU.add).then_inc(s["avg_ready"], 1)
            dve.wait_ge(s["a_exp"], 2)
            dve.tensor_scalar(a01[:, :], a01[:, :], -1.0, None, ALU.mult).then_inc(s["a_capped"], 1)
            dve.tensor_scalar(a2[:, :], a2[:, :], -1.0, None, ALU.mult).then_inc(s["a_capped"], 1)
            dve.wait_ge(s["a_capped"], 6)
            for dst, bias in ((a01, abias01), (a2, abias2)):
                dve.scalar_tensor_tensor(dst[:, :], bias[:, :], 0.0, dst[:, :], ALU.is_equal, ALU.mult).then_inc(s["avg_ready"], 1)

            for h in range(2):
                dve.wait_ge(s[f"xload{h}"], 16)
                tokens = seq[:, h * HALF:(h + 1) * HALF, :].rearrange("p t (c u) -> p t c u", u=UNROLL)
                halves = stats[:, :, 2 * h:2 * h + 2, :].rearrange("p (c u) a b -> p c u (a b)", u=UNROLL)
                with dve.Fori(0, SEQ // UNROLL) as c:
                    for u in range(UNROLL):
                        dve.bn_stats(halves[:, bass.ds(c, 1), u, :].rearrange("p c x -> p (c x)"),
                                     tokens[:, :, bass.ds(c, 1), u].rearrange("p t c -> p (t c)")
                                     ).then_inc(s["st_done"], 1)
            dve.wait_ge(s["st_done"], 2 * SEQ)
            dve.tensor_reduce(gsum[:, :], stats[:, :, :, 1], mybir.AxisListType.X, ALU.add).then_inc(s["a_gn"], 1)
            dve.wait_ge(s["a_g1"], 1)
            dve.tensor_scalar(gmean[:, :], ps[:, 2, 0:SEQ], 0.25, None, ALU.mult).then_inc(s["a_gn"], 1)
            dve.wait_ge(s["a_gn"], 2)
            dve.tensor_tensor(dev[:, :, :], stats[:, :, :, 1], gmean[:, :].unsqueeze(2).broadcast_to([128, SEQ, 4]),
                              ALU.subtract).then_inc(s["a_gn"], 1)
            dve.wait_ge(s["a_gn"], 3)
            dve.tensor_tensor(dev[:, :, :], dev[:, :, :], dev[:, :, :], ALU.mult).then_inc(s["a_gn"], 1)
            dve.wait_ge(s["a_gn"], 4)
            dve.scalar_tensor_tensor(dev[:, :, :], dev[:, :, :], float(T // 4), stats[:, :, :, 2], ALU.mult, ALU.add
                                     ).then_inc(s["a_gn"], 1)
            dve.wait_ge(s["a_gn"], 5)
            dve.tensor_reduce(gsum[:, :], dev[:, :, :], mybir.AxisListType.X, ALU.add).then_inc(s["a_gn"], 1)
            dve.wait_ge(s["a_g2"], 1)
            dve.tensor_scalar(gsum[:, :], ps[:, 3, 0:SEQ], 1.0 / T, EPS, ALU.mult, ALU.add).then_inc(s["a_gn"], 1)

            dve.wait_ge(s["a_std"], 1)
            dve.reciprocal(grstd[:, :], gsum[:, :]).then_inc(s["a_rstd"], 1)

            bias_of_n = gru_bias[:, 0:G3].rearrange("p (a c) -> p a c", a=3)[:, 0:3:2, :]

            def step(t, p, first=False):
                dve.wait_ge(s["r_pre_ready"], t + 1)
                dve.tensor_tensor(r_pre[:, :], ps[:, p, CJ:2 * CJ], gru_bias[:, CJ:2 * CJ], ALU.add).then_inc(s["r_biased"], 1)
                dve.tensor_tensor(n_parts[:, :, :], ps[:, p, 0:G3].rearrange("p (a c) -> p a c", a=3)[:, 0:3:2, :], bias_of_n,
                                  ALU.add).then_inc(s["n_biased"], 1)
                dve.wait_ge(s["r_ready"], t + 1)
                dve.wait_ge(s["n_biased"], t + 1)
                dve.tensor_tensor(rh[:, :], r_gate[:, :], n_parts[:, 1, :], ALU.mult).then_inc(s["rh_ready"], 1)
                dve.wait_ge(s["z_pre_ready"], t + 1)
                dve.tensor_tensor(z_pre[:, :], ps[:, Z_BANK + p, 0:CJ], gru_bias[:, G3:4 * CJ], ALU.add).then_inc(s["z_biased"], 1)
                dve.wait_ge(s["rh_ready"], t + 1)
                dve.tensor_tensor(cand_pre[:, :], rh[:, :], n_parts[:, 0, :], ALU.add).then_inc(s["pre_ready"], 1)
                dve.wait_ge(s["z_gate_ready"], t + 1)
                if not first:
                    dve.wait_ge(s["hist_done"], t - 1)
                dve.tensor_tensor(zh[:, :], z_gate[:, :], h_nat[:, :], ALU.mult).then_inc(s["mix_step"], 1)
                dve.wait_ge(s["tanh_ready"], t + 1)
                dve.scalar_tensor_tensor(blend[:, :], z_gate[:, :], -1.0, cand[:, :], ALU.add, ALU.mult).then_inc(s["mix_step"], 1)
                dve.wait_ge(s["mix_step"], t * 2 + 2)
                dve.tensor_tensor(h_nat[:, :], zh[:, :], blend[:, :], ALU.subtract).then_inc(s["hnat_ready"], 1)
                dve.wait_ge(s["hnat_ready"], t + 1)
                dve.transpose(h_t[:, p, :], h_nat[:, :]).then_inc(s["h_ready"], 1)

            dve.wait_ge(s["const_ready"], 2)
            dve.wait_ge(s["bias_step"], 4)
            step(0, 0, True)
            step(1, 1, True)
            with dve.Fori(1, T // 2) as i:
                for p in range(2):
                    step(i * 2 + p, p)

            st6 = stats[:, 0:KC * 2, 0:2, :]
            mean2 = st6[:, :, :, 1]
            dv = dev[:, 0:6, 0:2]

            def add_and_stats(i, first=False):
                dve.wait_ge(s["yproj_ready"], i + 1)
                dve.wait_ge(s["xin_ready"], i * 16 + 16)
                if not first:
                    dve.wait_ge(s["x1_spilled"], i * 16)
                    dve.wait_ge(s["xhat_ready"], i * 6)
                dve.tensor_tensor(x1[:, :, :], x_in[:, :, :], ps[:, 0:3, 0:T2], ALU.add).then_inc(s["x1_ready"], 1)
                dve.wait_ge(s["x1_ready"], i + 1)
                for kc in range(KC):
                    for b in range(2):
                        dve.bn_stats(st6[:, 2 * kc + b, :, :].rearrange("p a b -> p (a b)"),
                                     x1[:, kc, b * T:(b + 1) * T]).then_inc(s["stats_ready"], 1)
                dve.wait_ge(s["stats_ready"], i * 6 + 6)
                dve.tensor_tensor(gsum[:, 0:6], mean2[:, :, 0], mean2[:, :, 1], ALU.add).then_inc(s["gn_step"], 1)

            def deviations(i):
                dve.wait_ge(s["g1_ready"], i + 1)
                dve.tensor_scalar(gmean[:, 0:6], ps[:, 6, 0:6], 0.5, None, ALU.mult).then_inc(s["gn_step"], 1)
                dve.wait_ge(s["gn_step"], i * 8 + 2)
                dve.tensor_tensor(dv, mean2, gmean[:, 0:6].unsqueeze(2).broadcast_to([128, 6, 2]), ALU.subtract
                                  ).then_inc(s["gn_step"], 1)
                dve.wait_ge(s["gn_step"], i * 8 + 3)
                dve.tensor_tensor(dv, dv, dv, ALU.mult).then_inc(s["gn_step"], 1)
                dve.wait_ge(s["gn_step"], i * 8 + 4)
                dve.scalar_tensor_tensor(dv, dv, float(T // 2), st6[:, :, :, 2], ALU.mult, ALU.add).then_inc(s["gn_step"], 1)
                dve.wait_ge(s["gn_step"], i * 8 + 5)
                dve.tensor_tensor(gsum[:, 0:6], dv[:, :, 0], dv[:, :, 1], ALU.add).then_inc(s["gn_step"], 1)

            def variance(i):
                dve.wait_ge(s["g2_ready"], i + 1)
                dve.tensor_scalar(gsum[:, 0:6], ps[:, 7, 0:6], 1.0 / T, EPS, ALU.mult, ALU.add).then_inc(s["gn_step"], 1)

            def shift(i):
                dve.wait_ge(s["rstd_ready"], i + 1)
                dve.scalar_tensor_tensor(gmean[:, 0:6], gmean[:, 0:6], -1.0, grstd[:, 0:6], ALU.mult, ALU.mult
                                         ).then_inc(s["gn_step"], 1)

            def convolve(i, taps, first=False):
                if taps[0] == 0:
                    dve.wait_ge(s["pad_ready"], i * 2 + 2)
                    if not first:
                        dve.wait_ge(s["xc_ready"], i * 2)
                conv_taps(dve, i, taps)

            add_and_stats(0, True)
            deviations(0)
            variance(0)
            shift(0)

            def norm_and_convolve(i, first=False):
                add_and_stats(i)
                if not first:
                    convolve(i - 2, range(4, 6))
                deviations(i)
                if not first:
                    convolve(i - 2, range(6, 9))
                variance(i)
                convolve(i - 1, range(0, 2), first)
                shift(i)
                convolve(i - 1, range(2, 4))

            norm_and_convolve(1, True)
            with dve.Fori(2, PAIRS) as i:
                norm_and_convolve(i)
            convolve(PAIRS - 2, range(4, 9))
            convolve(PAIRS - 1, range(9))

            dve.wait_ge(s["yproj_ready"], PAIRS)
            for q in range(RING):
                for d in range(2):
                    z0 = da[d][q].rearrange("p (r t) -> p r t", t=T)
                    dve.memset(z0[:, :, 0:1] if d == 0 else z0[:, :, T - 1:T], 0.0).then_inc(s["d_zero"], 1)
            dve.wait_ge(s["d_zero"], 2 * RING)

            def m1(i, k, g, G, b, first=False):
                dux, bank, view = group_aps(g)
                q, _ = ring_of(k, g)
                if g == 0:
                    dve.wait_ge(s["du_ready"], i * K4 + (k + 1))
                dve.wait_ge(s["bb_ready"], G + 1)
                if not first:
                    dve.wait_ge(s["red_done"], G - (RING - 1))
                dve.tensor_tensor(view(hb[q]), dux(du[b]), bank(0), ALU.mult).then_inc(s["m1_done"], 1)

            def scan(k, g, G):
                q, dec = ring_of(k, g)
                dve.wait_ge(s["m1_done"], G + 1)
                dve.wait_ge(s["da_ready"], G + 1)
                st = hb[q]
                if k < 2:
                    dve.tensor_tensor_scan(st, dec, st, 0.0, ALU.mult, ALU.add).then_inc(s["scan_done"], 1)
                else:
                    dve.tensor_tensor_scan(st[:, ::-1], dec[:, ::-1], st[:, ::-1], 0.0, ALU.mult, ALU.add
                                           ).then_inc(s["scan_done"], 1)

            def m3(k, g, G):
                _, bank, view = group_aps(g)
                q, _ = ring_of(k, g)
                dve.wait_ge(s["scan_done"], G + 1)
                dve.wait_ge(s["cb_ready"], G + 1)
                dve.tensor_tensor(view(hb[q]), view(hb[q]), bank(2), ALU.mult).then_inc(s["m3_done"], 1)

            def drain(i):
                dve.wait_ge(s["red_done"], (i + 1) * (K4 * GRP))
                dve.wait_ge(s["fin_x"], i * 16 + 16)
                dve.scalar_tensor_tensor(ysb[:, 0:T2], xc_fin[:, 0:T2], dsum01[:, 0:1], ps[:, 4, 0:T2], ALU.mult, ALU.add
                                         ).then_inc(s["y_drained"], 1)
                dve.scalar_tensor_tensor(ysb[:, T2:TC], xc_fin[:, T2:TC], dsum2[:, 0:1], ps[:, 5, 0:T], ALU.mult, ALU.add
                                         ).then_inc(s["y_drained"], 1)

            def gate(i):
                dve.wait_ge(s["rstd2_step"], i * 3 + 3)
                dve.wait_ge(s["fin_z"], i * 16 + 16)
                for lo, hi, table in ((0, T2, par01), (T2, TC, par2)):
                    dve.scalar_tensor_tensor(yc[:, lo:hi], yc[:, lo:hi], table[:, P_G:P_G + 1], ysq[:, lo:hi],
                                             ALU.mult, ALU.mult).then_inc(s["norm_step"], 1)
                dve.wait_ge(s["norm_step"], i * 2 + 2)
                for lo, hi, table in ((0, T2, par01), (T2, TC, par2)):
                    dve.scalar_tensor_tensor(yc[:, lo:hi], yc[:, lo:hi], table[:, P_B:P_B + 1], z_fin[:, lo:hi],
                                             ALU.add, ALU.mult).then_inc(s["gated"], 1)

            def choose(st):
                dve.wait_ge(s["series_step"], 2 * st + 2)
                dve.scalar_tensor_tensor(poly, soft, SMALL, poly, ALU.is_lt, ALU.mult).then_inc(s["choice_ready"], 1)

            def pair(i, head):
                for k in range(K4):
                    for g in range(GRP):
                        G = i * (K4 * GRP) + (k * GRP + g)
                        scan(k, g, G)
                        k2, g2 = (k, g + 1) if g + 1 < GRP else (k + 1, 0)
                        if k2 < K4:
                            m1(i, k2, g2, G + 1, k2 % 2, head and k2 * GRP + g2 < RING)
                        else:
                            m1_next(i, G + 1)
                        m3(k, g, G)
                        if g == (9 if k in (1, 2) else 8):
                            choose(i * K4 + (k + 1))
                        if not head:
                            if (k, g) == (0, 0):
                                drain(i - 1)
                            if (k, g) == (1, 1):
                                gate(i - 1)

            def m1_next(i, G):
                dux, bank, view = group_aps(0)
                dve.wait_ge(s["du_ready"], i * K4 + (K4 + 1))
                dve.wait_ge(s["bb_ready"], G + 1)
                dve.wait_ge(s["red_done"], G - (RING - 1))
                dve.tensor_tensor(view(hb[0]), dux(du[0]), bank(0), ALU.mult).then_inc(s["m1_done"], 1)

            choose(0)
            m1(0, 0, 0, 0, 0, True)
            pair(0, True)
            with dve.Fori(1, PAIRS) as i:
                pair(i, False)
            drain(PAIRS - 1)
            gate(PAIRS - 1)

        @block.scalar
        def _(act):
            act.wait_ge(s["a_capped"], 4)
            act.activation(a01[:, :], a01[:, :], ACT.Exp).then_inc(s["a_exp"], 1)
            act.activation(a2[:, :], a2[:, :], ACT.Exp).then_inc(s["a_exp"], 1)

            act.preload_act_table_set("sqrt_and_others")
            act.wait_ge(s["a_gn"], 7)
            act.activation(gsum[:, :], gsum[:, :], ACT.Sqrt).then_inc(s["a_std"], 1)

            act.preload_act_table_set("sigmoid_and_others")

            def step(t, p):
                act.wait_ge(s["r_biased"], t + 1)
                act.activation(r_gate[:, :], r_pre[:, :], ACT.Sigmoid).then_inc(s["r_ready"], 1)
                act.wait_ge(s["z_biased"], t + 1)
                act.activation(z_gate[:, :], z_pre[:, :], ACT.Sigmoid).then_inc(s["z_gate_ready"], 1)
                act.wait_ge(s["pre_ready"], t + 1)
                act.activation(cand[:, :], cand_pre[:, :], ACT.Tanh).then_inc(s["tanh_ready"], 1)

            with act.Fori(0, T // 2) as i:
                for p in range(2):
                    step(i * 2 + p, p)

            def xh_and_z(i, first=False):
                act.wait_ge(s["inproj_whole"], i + 1)
                if not first:
                    act.wait_ge(s["conv01_step"], i * 9)
                    act.wait_ge(s["conv2_step"], i * 9)
                    act.wait_ge(s["z_spilled"], i * 16)
                act.activation(two_images(pad01[:, 1:2 * H + 3, :])[:, :, :, 1:W + 1],
                               ps[:, 3, 0:T2].rearrange("p (b h w) -> p b h w", b=2, h=H), ACT.Copy
                               ).then_inc(s["pad_ready"], 1)
                act.activation(z_out[:, 0:T2], ps[:, 5, 0:T2], ACT.Silu).then_inc(s["z_ready"], 1)
                act.wait_ge(s["inproj_ready"], i + 1)
                act.activation(pad2[:, 1:H + 1, 1:W + 1],
                               ps[:, 4, 0:T].rearrange("p (h w) -> p h w", h=H), ACT.Copy).then_inc(s["pad_ready"], 1)
                act.activation(z_out[:, T2:TC], ps[:, 4, T:T2], ACT.Silu).then_inc(s["z_ready"], 1)

            def conv_silu(i, first=False):
                if not first:
                    act.wait_ge(s["xc_spilled"], i * 16)
                act.wait_ge(s["conv2_step"], i * 9 + 9)
                act.activation(xc_out[:, T2:TC], conv2_out[:, :, :].rearrange("p h w -> p (h w)"), ACT.Silu).then_inc(s["xc_ready"], 1)
                act.wait_ge(s["conv01_step"], i * 9 + 9)
                act.activation(xc_out[:, 0:T2].rearrange("p (b h w) -> p b h w", b=2, h=H), two_images(conv01_out[:, :, :]), ACT.Silu).then_inc(s["xc_ready"], 1)

            def normalise(i, first=False):
                act.wait_ge(s["gn_step"], i * 8 + 8)
                if not first:
                    act.wait_ge(s["inproj_ready"], i)
                for c in range(6):
                    v = (slice(None), c // 2, slice(c % 2 * T, c % 2 * T + T))
                    act.activation(xhat[v], x1[v], ACT.Identity, scale=grstd[:, c:c + 1], bias=gmean[:, c:c + 1]
                                   ).then_inc(s["xhat_ready"], 1)

            act.wait_ge(s["pad_zero"], 2)
            act.preload_act_table_set("silu_and_others")
            normalise(0, True)
            xh_and_z(0, True)
            normalise(1)
            conv_silu(0, True)
            xh_and_z(1)
            normalise(2)
            with act.Fori(3, PAIRS) as i:
                conv_silu(i - 2)
                xh_and_z(i - 1)
                normalise(i)
            conv_silu(PAIRS - 2)
            xh_and_z(PAIRS - 1)


            def turn(i):
                act.wait_ge(s["xc_loaded"], i * 16 + 16)
                act.activation(xt.rearrange("p (r w h) -> p r h w", r=3, w=W),
                               xc.rearrange("p (r h w) -> p r h w", r=3, h=H), ACT.Copy).then_inc(s["xt_ready"], 1)

            def read_bc(st, b, first=False):
                act.wait_ge(s["bc_ready"], 2 * st + 2)
                if not first:
                    act.wait_ge(s["dt_ready"], 2 * st)
                    act.wait_ge(s["parts_ready"], st + 0)
                    act.wait_ge(s["cb_ready"], (st - 1) * GRP)
                act.activation(xdbl[:, :], ps[:, 6, 0:T2], ACT.Copy).then_inc(s["xdbl_ready"], 1)
                act.activation(bcs[b][0:96, :], ps[0:96, 6, 0:T2], ACT.Copy).then_inc(s["xdbl_ready"], 1)

            def mid_parts(st, b):
                act.wait_ge(s["resid_ready"], st + 1)
                act.activation(bcs[b][32:64, :], resid[32:64, :], ACT.Copy).then_inc(s["mid_ready"], 1)
                act.activation(midt[64:96, :], resid[64:96, :], ACT.Copy).then_inc(s["mid_ready"], 1)

            def softplus(st, k, first=False):
                act.wait_ge(s["dt_ready"], 2 * st + 2)
                if not first:
                    act.wait_ge(s["delta_ready"], st + 0)
                for lo, hi, bank, table in ((0, T2, 7, par01), (T2, TC, 6, par2)):
                    bias = table[:, P_DTB + k:P_DTB + k + 1]
                    act.activation(soft[:, lo:hi], ps[:, bank, 0:hi - lo], ACT.Abs, bias=bias).then_inc(s["dt_read"], 1)
                    act.activation(relu[:, lo:hi], ps[:, bank, 0:hi - lo], ACT.Relu, bias=bias).then_inc(s["dt_read"], 1)

            def series(st):
                act.wait_ge(s["dt_read"], 4 * st + 4)
                act.activation(soft, soft, ACT.Exp, scale=-1.0).then_inc(s["soft_step"], 1)
                act.wait_ge(s["soft_step"], 4 * st + 1)
                act.activation(lnp, soft, ACT.Ln, bias=1.0).then_inc(s["soft_step"], 1)
                act.activation(poly, soft, ACT.Square, scale=3.0 ** -0.5, bias=series_bias[:, 0:1]).then_inc(s["soft_step"], 1)
                act.wait_ge(s["soft_step"], 4 * st + 3)
                act.activation(poly, poly, ACT.Copy, bias=13.0 / 16.0).then_inc(s["soft_step"], 1)

            def decays(i, k, g, G, b, first=False):
                _, dec = ring_of(k, g)
                r = dec.rearrange("p (r t) -> p r t", t=T)
                lo = 1 if k < 2 else 0
                if g == 0:
                    act.wait_ge(s["delta_ready"], i * K4 + (k + 1))
                if not first:
                    act.wait_ge(s["scan_done"], G - (RING - 1))
                if g < 8:
                    src = delta[b][:, 0:T2].rearrange("p (r t) -> p r t", r=2)[:, :, lo:lo + T - 1]
                    for m in range(2):
                        n = 2 * g + m
                        ins = act.activation(r[:, 2 * m:2 * m + 2, lo:lo + T - 1], src, ACT.Exp,
                                             scale=a01[:, k * N + n:k * N + n + 1], bias=abias01[:, k * N + n:k * N + n + 1])
                else:
                    for m in range(4):
                        n = 4 * (g - 8) + m
                        ins = act.activation(r[:, m, lo:lo + T - 1], delta[b][:, T2 + lo:T2 + lo + T - 1], ACT.Exp,
                                             scale=a2[:, k * N + n:k * N + n + 1], bias=abias2[:, k * N + n:k * N + n + 1])
                ins.then_inc(s["da_ready"], 1)

            def square(i):
                act.wait_ge(s["centred"], i * 2 + 2)
                act.activation(yc[:, 0:T2], ps[:, 6, 0:T2], ACT.Copy).then_inc(s["yc_ready"], 1)
                act.activation(yc[:, T2:TC], ps[:, 7, 0:T], ACT.Copy).then_inc(s["yc_ready"], 1)
                act.wait_ge(s["yc_ready"], i * 2 + 2)
                act.activation(ysq, yc, ACT.Square).then_inc(s["ysq_ready"], 1)

            def result(i, oc):
                act.wait_ge(s["oproj_ready"], i * 3 + (oc + 1))
                act.activation(o_sb[:, oc, :], ps[:, 6 + oc % 2, 0:T2], ACT.Copy).then_inc(s["o_ready"], 1)

            def rstd(i):
                act.wait_ge(s["var_ready"], i * 2 + 2)
                act.activation(ysq[:, 0:T2], ps[:, 6, 0:T2], ACT.Ln, bias=EPS
                               ).then_inc(s["rstd2_step"], 1)
                act.activation(ysq[:, T2:TC], ps[:, 7, 0:T], ACT.Ln, bias=EPS).then_inc(s["rstd2_step"], 1)
                act.wait_ge(s["rstd2_step"], i * 3 + 2)
                act.activation(ysq, ysq, ACT.Exp, scale=-0.5).then_inc(s["rstd2_step"], 1)

            RESULTS = ((1, 9), (1, 11), (2, 1))

            def pair(i, head):
                for k in range(K4):
                    st = i * K4 + (k + 1)
                    kn, b = (k + 1) % K4, (k + 1) % 2
                    g0 = 1 if k in (1, 2) else 0
                    for g in range(GRP):
                        decays(i, k, g, i * (K4 * GRP) + (k * GRP + g), k % 2, head and k * GRP + g < RING)
                        if g == g0 + 3:
                            read_bc(st, b)
                        if g == g0 + 4:
                            mid_parts(st, b)
                        if g == g0 + 6:
                            softplus(st, kn)
                        if g == g0 + 7:
                            series(st)
                        if not head:
                            if (k, g) == (0, 10):
                                square(i - 1)
                            if (k, g) == (1, 1):
                                rstd(i - 1)
                            if (k, g) in RESULTS:
                                result(i - 1, RESULTS.index((k, g)))
                        if k == 3 and g == 9:
                            turn(i + 1)

            turn(0)
            read_bc(0, 0, True)
            mid_parts(0, 0)
            softplus(0, 0, True)
            conv_silu(PAIRS - 1)
            act.preload_act_table_set("natural_log_exp_and_others")
            series(0)
            act.wait_ge(s["avg_ready"], 14)
            act.wait_ge(s["d_zero"], 2 * RING)
            pair(0, True)
            with act.Fori(1, PAIRS) as i:
                pair(i, False)
            square(PAIRS - 1)
            rstd(PAIRS - 1)
            for oc in range(KC):
                result(PAIRS - 1, oc)

        @block.tensor
        def _(pe):
            def group_average(src, bank, cols, done):
                for oc in range(KC):
                    ks = [k for k in range(KC) if abs(k - oc) < 2]
                    for k in ks:
                        mm = pe.matmul(ps[:, bank, oc * cols:(oc + 1) * cols], gavg[:, k, oc * 128:(oc + 1) * 128],
                                       src[:, k * cols:(k + 1) * cols], start=(k == ks[0]), stop=(k == ks[-1]))
                mm.then_inc(done, 1)

            pe.wait_ge(s["gavg_step"], 3)
            pe.wait_ge(s["a_gn"], 1)
            group_average(gsum, 2, B, s["a_g1"])
            pe.wait_ge(s["a_gn"], 6)
            group_average(gsum, 3, B, s["a_g2"])

            def x_part(p):
                for bank, lo, hi in ((p, 0, 2 * CJ), (Z_BANK + p, 2 * CJ, G3)):
                    for k in range(KC):
                        for j in range(NJ):
                            mm = pe.matmul(ps[32 * j:32 * j + 32, bank, 0:hi - lo], x_cur[:, p, 32 * k:32 * k + 32],
                                           wx_sb[:, k, j, lo:hi], start=(k == 0), stop=False)
                mm.then_inc(s["xpart_done"], 1)

            def h_part(p):
                def part(bank, at, k, lo, hi):
                    for j in range(NJ):
                        mm = pe.matmul(ps[32 * j:32 * j + 32, bank, at:at + hi - lo], h_t[:, 1 - p, 32 * k:32 * k + 32],
                                       wh_sb[:, k, j, lo:hi], start=False, stop=(k == KC - 1))
                    return mm

                part(p, CJ, 0, 0, CJ)
                part(p, 2 * CJ, 0, CJ, 2 * CJ)
                part(p, CJ, 1, 0, 2 * CJ)
                part(p, CJ, 2, 0, 2 * CJ).then_inc(s["r_pre_ready"], 1)
                part(Z_BANK + p, 0, 0, 2 * CJ, G3)
                part(Z_BANK + p, 0, 1, 2 * CJ, G3)
                part(Z_BANK + p, 0, 2, 2 * CJ, G3).then_inc(s["z_pre_ready"], 1)

            pe.wait_ge(s["gru_weights_in"], 32)
            pe.wait_ge(s["const_ready"], 2)
            pe.wait_ge(s["x_ready"], 1)
            x_part(0)

            def step(t, p, last=False):
                pe.wait_ge(s["h_ready"], t + 1)
                h_part(p)
                if not last:
                    pe.wait_ge(s["x_ready"], t + 2)
                    x_part(1 - p)

            with pe.Fori(0, T // 2 - 1) as i:
                for p in range(2):
                    step(i * 2 + p, p)
            step(T - 2, 0)
            step(T - 1, 1, True)

            def y_proj(i, first=False):
                if not first:
                    pe.wait_ge(s["x1_ready"], i + 0)
                for oc in range(KC):
                    for k in range(KC):
                        col = i * 2 + k * 32
                        rhs = seq[:, :, col:col + 2] if isinstance(i, int) else seq[:, :, bass.ds(col, 2)]
                        mm = pe.matmul(ps[:, oc, 0:T2].rearrange("p (b t) -> p b t", b=2), wp_sb[:, k, oc * 128:(oc + 1) * 128],
                                       rhs.rearrange("p t b -> p b t"), start=(k == 0), stop=(k == KC - 1))
                mm.then_inc(s["yproj_ready"], 1)

            def in_proj_whole(i, first=False):
                pe.wait_ge(s["xhat_ready"], i * 6 + 6)
                if not first:
                    pe.wait_ge(s["z_ready"], i * 2)
                    pe.wait_ge(s["pad_ready"], i * 2)
                for bank, lo in ((3, 0), (5, DI)):
                    for k in range(KC):
                        mm = pe.matmul(ps[:, bank, 0:T2], win_sb[:, k, lo:lo + 128], xhat[:, k, :], start=(k == 0), stop=(k == KC - 1))
                mm.then_inc(s["inproj_whole"], 1)

            def in_proj_halves(i):
                for col, lo in ((0, 128), (T, DI + 128)):
                    for k in range(KC):
                        for b in range(2):
                            mm = pe.matmul(ps[64 * b:64 * b + 64, 4, col:col + T], win_sb[:, k, lo:lo + 64],
                                           xhat[:, k, b * T:(b + 1) * T], start=(k == 0), stop=(k == KC - 1))
                mm.then_inc(s["inproj_ready"], 1)

            def mean_sums(i):
                pe.wait_ge(s["gn_step"], i * 8 + 1)
                group_average(gsum, 6, 2, s["g1_ready"])

            def var_sums(i):
                pe.wait_ge(s["gn_step"], i * 8 + 6)
                group_average(gsum, 7, 2, s["g2_ready"])

            pe.wait_ge(s["hist_done"], T)
            def project(i, first=False):
                y_proj(i)
                in_proj_whole(i - 1, first)
                mean_sums(i)
                in_proj_halves(i - 1)
                var_sums(i)

            pe.wait_ge(s["late_weights_in"], 16 * LATE_LOADS)
            y_proj(0, True)
            mean_sums(0)
            var_sums(0)
            project(1, True)
            with pe.Fori(2, PAIRS) as i:
                project(i)
            in_proj_whole(PAIRS - 1)
            in_proj_halves(PAIRS - 1)

            def bc_proj(i, k, st, bc, first=False):
                x = xt if k % 2 else xc
                if bc == 0:
                    pe.wait_ge(s["xc_loaded"], i * 16 + 16)
                    if k % 2:
                        pe.wait_ge(s["xt_ready"], i + 1)
                    if not first:
                        pe.wait_ge(s["dt_read"], 4 * st)
                for tile in range(3):
                    mm = pe.matmul(ps[:, 6, bc * T:(bc + 1) * T], bc_w[:, k, bc, tile, :], x[:, tile * T:(tile + 1) * T],
                                   start=(tile == 0), stop=(tile == 2))
                mm.then_inc(s["bc_ready"], 1)

            def dt_proj(k, st, part):
                if part == 0:
                    pe.wait_ge(s["xdbl_ready"], 2 * st + 2)
                    pe.matmul(ps[:, 7, 0:T2], dt_w[:, k, 0, :], xdbl[:, :], start=True, stop=True).then_inc(s["dt_ready"], 1)
                else:
                    pe.matmul(ps[:, 6, 0:T], dt_w[:, k, 1, :], xdbl[:, 0:T], start=True, stop=False)
                    pe.matmul(ps[:, 6, 0:T], dt_w[:, k, 2, :], xdbl[:, T:T2], start=False, stop=True).then_inc(s["dt_ready"], 1)

            def spread(g, part, bank, b, done):
                rhs = bcs[b][0:96, part * T:(part + 1) * T]
                for m in range(4):
                    n, kind = (2 * g + m // 2, m % 2) if g < 8 else (4 * (g - 8) + m, 2)
                    mm = pe.matmul(ps[:, bank + m // 2, m % 2 * T:m % 2 * T + T], sel[:, n, kind, :], rhs, start=True, stop=True)
                mm.then_inc(done, 1)

            def reduce(k, g, G, start, stop):
                q, _ = ring_of(k, g)
                runs = 2 if g < 8 else 4
                pe.wait_ge(s["m3_done"], G + 1)
                for m in range(runs):
                    cols = GC // runs
                    bank = 4 if g < 8 else 5
                    src = hb[q][:, m * cols:(m + 1) * cols]
                    dst = ps[:, bank, 0:cols]
                    if k % 2:
                        src = src.rearrange("p (r w h) -> p r h w", w=W, h=H)
                        dst = dst.rearrange("p (r h w) -> p r h w", h=H, w=W)
                    mm = pe.matmul(dst, ident[:, :], src, start=(start and m == 0), stop=(stop and m == runs - 1))
                mm.then_inc(s["red_done"], 1)

            def first_of_pair(k, g):
                return k == 0 and g in (0, 8)

            def last_of_pair(k, g):
                return k == K4 - 1 and g in (7, GRP - 1)

            def over_channels(weights, src, part, done):
                if part == 0:
                    pe.matmul(ps[:, 6, 0:T2], weights[:, 0, :], src[:, 0:T2], start=True, stop=False)
                    pe.matmul(ps[:, 6, 0:T], weights[:, 1, :], src[:, T2:TC], start=False, stop=False)
                    pe.matmul(ps[:, 6, T:T2], weights[:, 2, :], src[:, T2:TC], start=False, stop=True).then_inc(done, 1)
                else:
                    pe.matmul(ps[:, 7, 0:T], weights[:, 3, :], src[:, T2:TC], start=True, stop=False)
                    pe.matmul(ps[:, 7, 0:T], weights[:, 4, :], src[:, 0:T], start=False, stop=False)
                    pe.matmul(ps[:, 7, 0:T], weights[:, 5, :], src[:, T:T2], start=False, stop=True).then_inc(done, 1)

            def centre(i, part, dt_reads):
                if part == 0:
                    pe.wait_ge(s["y_drained"], i * 2 + 2)
                    pe.wait_ge(s["dt_read"], dt_reads)
                over_channels(centring, ysb, part, s["centred"])

            def var(i, part):
                if part == 0:
                    pe.wait_ge(s["ysq_ready"], i + 1)
                over_channels(avg, ysq, part, s["var_ready"])

            def out_proj(i, oc):
                bank = 6 + oc % 2
                pe.wait_ge(s["gated"], i * 2 + 2)
                if oc == 2:
                    pe.wait_ge(s["o_ready"], i * 3 + 1)
                c = slice(oc * 128, (oc + 1) * 128)
                pe.matmul(ps[:, bank, 0:T2], wout01[:, c], yc[:, 0:T2], start=True, stop=False)
                for b in range(2):
                    pe.matmul(ps[:, bank, b * T:(b + 1) * T], wout2[:, b, c], yc[:, T2:TC], start=False, stop=False)

            def residual(i, oc):
                if oc == 0:
                    pe.wait_ge(s["fin_x1"], i * 16 + 16)
                pe.matmul(ps[:, 6 + oc % 2, 0:T2], ident[:, :], x1[:, oc, :], start=False, stop=True).then_inc(s["oproj_ready"], 1)

            def pair(i, head):
                for k in range(K4):
                    st = i * K4 + (k + 1)
                    inext, kn = (i, k + 1) if k + 1 < K4 else (i + 1, 0)
                    g0 = 1 if k in (1, 2) else 0
                    for g in range(GRP):
                        G = i * (K4 * GRP) + (k * GRP + g)
                        if g == GRP - 1:
                            pe.wait_ge(s["parts_ready"], st + 1)
                        pe.wait_ge(s["m1_done"], G + 1)
                        spread((g + 1) % GRP, 0, 0, (k if g < GRP - 1 else k + 1) % 2, s["bb_ready"])
                        if not (head and k == 0 and g == 0):
                            pe.wait_ge(s["m3_done"], G + 0)
                        spread(g, 1, 2, k % 2, s["cb_ready"])
                        if (k, g) != (0, 0):
                            kp, gp = (k, g - 1) if g else (k - 1, GRP - 1)
                            if (kp, gp) == (0, 0) and not head:
                                pe.wait_ge(s["y_drained"], i * 2)
                            reduce(kp, gp, G - 1, first_of_pair(kp, gp), last_of_pair(kp, gp))
                        elif not head:
                            reduce(K4 - 1, GRP - 1, G - 1, False, True)
                        if g in (g0, g0 + 1):
                            if g == g0 and not head:
                                if k == 1:
                                    pe.wait_ge(s["rstd2_step"], i * 3)
                                if k == 2:
                                    pe.wait_ge(s["o_ready"], i * 3)
                            bc_proj(inext, kn, st, g - g0)
                        if g in (g0 + 3, g0 + 4):
                            dt_proj(kn, st, g - g0 - 3)
                        if not head:
                            if k == 0 and g in (5, 6):
                                centre(i - 1, g - 5, 4 * st + 4)
                            if k == 0 and g in (9, 10):
                                var(i - 1, g - 9)
                            if k == 1 and g >= 6:
                                if g == 6:
                                    pe.wait_ge(s["dt_read"], 4 * st + 4)
                                (residual if g % 2 else out_proj)(i - 1, (g - 6) // 2)

            pe.wait_ge(s["bcw_step"], 13)
            pe.wait_ge(s["sel_step"], 13)
            pe.wait_ge(s["ident_ready"], 1)
            pe.wait_ge(s["gn_step"], 8 * PAIRS)
            pe.wait_ge(s["avg_ready"], 14)
            pe.wait_ge(s["centre_ready"], 3)
            for part in range(2):
                bc_proj(0, 0, 0, part, True)
            for part in range(2):
                dt_proj(0, 0, part)
            pe.wait_ge(s["z_ready"], 2 * PAIRS)
            pe.wait_ge(s["pad_ready"], 2 * PAIRS)
            pe.wait_ge(s["parts_ready"], 1)
            spread(0, 0, 0, 0, s["bb_ready"])
            pair(0, True)
            with pe.Fori(1, PAIRS) as i:
                pair(i, False)
            reduce(K4 - 1, GRP - 1, PAIRS * K4 * GRP - 1, False, True)
            for part in range(2):
                centre(PAIRS - 1, part, 4 * (K4 * PAIRS + 1))
            for part in range(2):
                var(PAIRS - 1, part)
            for oc in range(KC):
                if oc == 0:
                    pe.wait_ge(s["rstd2_step"], 3 * PAIRS)
                out_proj(PAIRS - 1, oc)
                residual(PAIRS - 1, oc)


def dram(t, i):
    return t[i] if isinstance(i, int) else t[bass.ds(i, 1), :, :].rearrange("o p c -> (o p) c")


def flat(t):
    return t[:, :, :].rearrange("p a b -> p (a b)")


def kernel(**inputs):
    import numpy as np
    import concourse.bacc as bacc
    from concourse.bass_utils import run_bass_kernel_spmd as run

    a = {k: np.asarray(v) for k, v in inputs.items()}
    x = a["x"]
    lay = {
        "x_seq": x.reshape(B, T, KC, 128).transpose(3, 1, 2, 0).reshape(128, T, SEQ),
        "x_pair": x.reshape(PAIRS, 2, T, KC, 128).transpose(0, 4, 3, 1, 2).reshape(PAIRS, 128, KC * T2),
        "wx": a["L0_conv_Wx"].reshape(3, NJ, CJ, KC, 128)[[2, 1, 0]].transpose(4, 3, 1, 0, 2).reshape(128, KC, NJ, G3),
        "wh": a["L0_conv_Wh"].reshape(3, NJ, CJ, NJ, KC, 32)[[1, 2, 0]].transpose(3, 5, 4, 1, 0, 2).reshape(128, KC, NJ, G3),
        "bx": a["L0_conv_bx"].reshape(3, NJ, CJ)[[2, 1, 0]].transpose(1, 0, 2).reshape(NJ, G3),
        "bh": a["L0_conv_bh"].reshape(3, NJ, CJ)[[1, 2, 0]].transpose(1, 0, 2).reshape(NJ, G3),
        "wp": a["L0_conv_Wp"].reshape(C, NJ, KC, 32).transpose(1, 3, 2, 0).reshape(128, KC, C),
        "win": a["L1_conv_in_proj_w"].reshape(C, KC, 128).transpose(2, 1, 0),
        "par": np.concatenate([
            a["L1_conv_conv_w"].reshape(DI, 9), a["L1_conv_conv_b"].reshape(DI, 1), a["L1_conv_dt_projs_b"].T,
            a["L1_conv_A_logs"].reshape(K4, DI, N).transpose(1, 0, 2).reshape(DI, K4 * N),
            a["L1_conv_Ds"].reshape(K4, DI).T, a["L1_conv_out_norm_g"].reshape(DI, 1),
            a["L1_conv_out_norm_b"].reshape(DI, 1)], axis=1),
        "xproj": a["L1_conv_x_proj_w"].transpose(2, 0, 1).reshape(DI, K4 * (R + 2 * N)),
        "dtproj": a["L1_conv_dt_projs_w"].transpose(2, 0, 1),
        "wout": a["L1_conv_out_proj_w"].T,
    }
    nc = bacc.Bacc("TRN2", target_bir_lowering=False, num_devices=1)
    arrays, args = {}, []
    for name, v in lay.items():
        v = np.ascontiguousarray(v)
        arrays[name] = v
        args.append(nc.dram_tensor(name, v.shape, mybir.dt.from_np(v.dtype), kind="ExternalInput").ap())
    args.append(nc.dram_tensor("out_0", (PAIRS, 128, KC * T2), F32, kind="ExternalOutput").ap())
    build(nc, *args)
    r = run(nc, [arrays], core_ids=[0])
    o = r.results[0]["out_0"].reshape(PAIRS, 128, KC, 2, T)
    return o.transpose(0, 3, 4, 2, 1).reshape(B, H, W, C)
```

```python
from contextlib import ExitStack

import concourse.bass as bass
from concourse import mybir

F32 = mybir.dt.float32
BF16 = mybir.dt.bfloat16
ALU = mybir.AluOpType
ACT = mybir.ActivationFunctionType

B, H, W, C = 32, 14, 14, 384
T = H * W
KC = C // 128
NJ = 4
CJ = C // NJ
SEQ = KC * B
G3 = 3 * CJ
Z_BANK = 4
GN = 12
PAIRS = B // 2
DI = C // 2
N = 16
R = 24
K4 = 4
T2 = 2 * T
TC = 3 * T
GRP = 12
GC = 4 * T
RING = 4
EPS = 1e-5
UNROLL = 32
A_LOG_MAX = 88.72
SMALL = 0.022
P_CW, P_CB, P_DTB, P_AL, P_DS, P_G, P_B = 0, 9, 10, 14, 78, 82, 83
NP = 84


def build(nc, x_seq, x_pair, wx, wh, bx, bh, wp, win, par, xproj, dtproj, wout, out):
    x1_dram = nc.dram_tensor("x1_dram", [PAIRS, 128, KC * T2], F32)
    z_dram = nc.dram_tensor("z_dram", [PAIRS, 128, TC], F32)
    xc_dram = nc.dram_tensor("xc_dram", [PAIRS + 1, 128, TC], F32)

    with ExitStack() as ctx:
        def sb(name, shape, dt=F32):
            return ctx.enter_context(nc.sbuf_tensor(name, shape, dt))

        def sem(name):
            return ctx.enter_context(nc.semaphore(name))

        arena = sb("arena", [128, T * SEQ])
        wx_sb = sb("wx_sb", [128, KC, NJ, G3])
        wh_sb = sb("wh_sb", [128, KC, NJ, G3])
        wp_sb = sb("wp_sb", [128, KC, C])
        win_sb = sb("win_sb", [128, KC, C])
        par01 = sb("par01", [128, NP])
        par2 = sb("par2", [128, NP])
        gavg = sb("gavg", [128, KC, C])
        gru_bias = sb("gru_bias", [128, 4 * CJ])
        bias_x = sb("bias_x", [128, G3])
        bias_h = sb("bias_h", [128, G3])
        ident = sb("ident", [128, 128])
        sel = sb("sel", [96, N, 3, 128], BF16)
        bc_w = sb("bc_w", [128, K4, 2, 3, 128])
        dt_w = sb("dt_w", [128, K4, 3, 128])
        wout01 = sb("wout01", [128, C])
        wout2 = sb("wout2", [128, 2, C])
        avg = sb("avg", [128, 6, 128])
        centring = sb("centring", [128, 6, 128])
        skip01 = sb("skip01", [128, 128])
        skip2 = sb("skip2", [128, 128])
        a01 = sb("a01", [128, K4 * N])
        a2 = sb("a2", [128, K4 * N])
        abias01 = sb("abias01", [128, K4 * N])
        abias2 = sb("abias2", [128, K4 * N])
        dsum01 = sb("dsum01", [128, 1])
        dsum2 = sb("dsum2", [128, 1])
        neg_half = sb("neg_half", [128, SEQ])
        series_bias = sb("series_bias", [128, 1])
        stats = sb("stats", [128, SEQ, 4, 3])
        gsum = sb("gsum", [128, SEQ])
        gmean = sb("gmean", [128, SEQ])
        grstd = sb("grstd", [128, SEQ])
        dev = sb("dev", [128, SEQ, 4])
        x_tmp = sb("x_tmp", [128, SEQ])
        x_cur = sb("x_cur", [128, 2, SEQ])
        h_nat = sb("h_nat", [128, CJ])
        h_t = sb("h_t", [128, 2, CJ])
        z_gate = sb("z_gate", [128, CJ])
        r_gate = sb("r_gate", [128, CJ])
        rh = sb("rh", [128, CJ])
        r_pre = sb("r_pre", [128, CJ])
        z_pre = sb("z_pre", [128, CJ])
        n_parts = sb("n_parts", [128, 2, CJ])
        cand_pre = sb("cand_pre", [128, CJ])
        cand = sb("cand", [128, CJ])
        zh = sb("zh", [128, CJ])
        blend = sb("blend", [128, CJ])
        x_in = sb("x_in", [128, KC, T2])
        x1 = sb("x1", [128, KC, T2])
        xhat = sb("xhat", [128, KC, T2])
        pad01 = sb("pad01", [128, 2 * H + 3, W + 2])
        pad2 = sb("pad2", [128, H + 2, W + 2])
        conv01_out = sb("conv01_out", [128, 2 * H + 2, W])
        conv2_out = sb("conv2_out", [128, H, W])
        xc_out = sb("xc_out", [128, TC])
        z_out = sb("z_out", [128, TC])

        ps = ctx.enter_context(nc.psum_tensor("ps", [128, 8, 512], F32))

        seq = arena[:, :].rearrange("p (t c) -> p t c", c=SEQ)

        used = [0]

        def carve(cols):
            a = arena[:, used[0]:used[0] + cols]
            used[0] += cols
            return a

        wx_cols = wx_sb[:, :, :, :].rearrange("p a b c -> p (a b c)")
        spare = [wx_cols[:, q * GC:(q + 1) * GC] for q in range(3)]
        da = [[carve(GC) for _ in range(RING - 1)] + [spare[d]] for d in range(2)]
        hb = [carve(GC) for _ in range(RING - 1)] + [spare[2]]
        delta = [carve(TC) for _ in range(2)]
        du = [carve(TC) for _ in range(2)]
        xc = carve(TC)
        xt = carve(TC)
        xdbl = carve(T2)
        resid = carve(T2)
        bcs = [carve(T2 // 2).bitcast(BF16) for _ in range(2)]
        midt = carve(T2 // 2).bitcast(BF16)
        soft = carve(TC)
        relu = carve(TC)
        lnp = carve(TC)
        poly = carve(TC)
        xc_fin = carve(TC)
        z_fin = carve(TC)
        ysb = carve(TC)
        yc = carve(TC)
        ysq = carve(TC)
        o_sb = carve(KC * T2).rearrange("p (a b) -> p a b", a=KC)
        assert used[0] <= T * SEQ

        s = {n: sem(n) for n in (
            "params_in", "gru_weights_in", "late_weights_in", "dt_w_clear", "xload0", "xload1",
            "ident0", "ident_ready", "sel_step", "gavg_step", "const_ready", "pad_zero", "d_zero", "setup_step",
            "a_exp", "a_capped", "bias_step", "bcw_step", "centring_step", "skip_step",
            "st_done", "a_gn", "a_g1", "a_g2", "a_std", "a_rstd",
            "xs_tmp", "x_ready", "xpart_done", "h_ready", "r_pre_ready", "z_pre_ready", "r_biased", "n_biased",
            "z_biased", "r_ready", "z_gate_ready", "rh_ready", "pre_ready", "tanh_ready", "mix_step",
            "hnat_ready", "hist_done",
            "xin_ready", "yproj_ready", "x1_ready", "x1_spilled", "stats_ready", "gn_step", "g1_ready",
            "g2_ready", "rstd_ready", "xhat_ready", "inproj_whole", "inproj_ready", "pad_ready", "z_ready",
            "conv01_step", "conv2_step", "xc_ready", "z_spilled", "xc_spilled", "xc_dup",
            "xc_loaded", "xt_ready", "bc_ready", "xdbl_ready", "resid_ready", "mid_ready", "parts_ready",
            "dt_ready", "dt_read", "soft_step", "series_step", "choice_ready", "log_ready", "delta_ready", "du_ready",
            "b_ready", "c_ready", "decay_ready", "drive_ready", "scan_done", "readout_ready", "reduced",
            "y_drained", "centred", "yc_ready", "ysq_ready", "var_ready", "rstd2_step", "norm_step", "gated",
            "oproj_ready", "o_ready", "out_stored", "fin_x", "fin_z", "fin_x1")}

        convs = ((pad01, conv01_out, 2 * H + 1, par01, s["conv01_step"]), (pad2, conv2_out, H, par2, s["conv2_step"]))

        def conv_taps(eng, i, taps):
            for tap in taps:
                for pad, conv, rows, table, step in convs:
                    win_ = pad[:, tap // 3:tap // 3 + rows, tap % 3:tap % 3 + W]
                    dst = conv[:, 0:rows, :]
                    wv = table[:, P_CW + tap:P_CW + tap + 1]
                    if tap == 0:
                        ins = eng.tensor_scalar(dst, win_, wv, table[:, P_CB:P_CB + 1], ALU.mult, ALU.add)
                    else:
                        eng.wait_ge(step, i * 9 + tap)
                        ins = eng.scalar_tensor_tensor(dst, win_, wv, dst, ALU.mult, ALU.add)
                    ins.then_inc(step, 1)

        def two_images(rows):
            return rows.rearrange("p (b r) w -> p b r w", b=2)[:, :, 0:H, :]

        def group_aps(g):
            if g < 8:
                return (lambda a: a[:, 0:T2].unsqueeze(1).broadcast_to([128, 2, T2]),
                        lambda bank: ps[:, bank:bank + 2, 0:T2],
                        lambda a: a.rearrange("p (m c) -> p m c", m=2))
            return (lambda a: a[:, T2:TC].unsqueeze(1).unsqueeze(1).broadcast_to([128, 2, 2, T]),
                    lambda bank: ps[:, bank:bank + 2, 0:T2].rearrange("p m (q t) -> p m q t", q=2),
                    lambda a: a.rearrange("p (m q t) -> p m q t", m=2, q=2))

        def ring_of(k, g):
            return (k * GRP + g) % RING, da[k // 2][(k % 2 * GRP + g) % RING]

        block = ctx.enter_context(nc.Block())

        PARAM_LOADS, LATE_LOADS = 6 + 2 * NJ, 8
        HALF = T // 2

        @block.sync
        def _(sp):
            stage = x1[:, :, :].rearrange("p a b -> p (a b)")
            n56 = K4 * (R + 2 * N)
            for dst, src in (
                    (par01[:, :], par[0:128, :]), (par2[0:64, :], par[128:DI, :]), (par2[64:128, :], par[128:DI, :]),
                    (stage[:, 0:n56], xproj[0:128, :]), (stage[0:64, n56:2 * n56], xproj[128:DI, :]),
                    (stage[64:128, n56:2 * n56], xproj[128:DI, :])):
                sp.dma_start(dst, src).then_inc(s["params_in"], 16)
            for j in range(NJ):
                sp.dma_start(bias_x[32 * j:32 * j + 32, :], bx[j:j + 1, :].broadcast_to([32, G3])
                    ).then_inc(s["params_in"], 16)
                sp.dma_start(bias_h[32 * j:32 * j + 32, :], bh[j:j + 1, :].broadcast_to([32, G3])
                    ).then_inc(s["params_in"], 16)
            for h in range(2):
                sp.dma_start(seq[:, h * HALF:(h + 1) * HALF, :],
                             x_seq[:, h * HALF:(h + 1) * HALF, :]).then_inc(s[f"xload{h}"], 16)
            sp.dma_start(wx_sb[:, :, :, :], wx).then_inc(s["gru_weights_in"], 16)
            sp.dma_start(wh_sb[:, :, :, :], wh).then_inc(s["gru_weights_in"], 16)
            sp.wait_ge(s["dt_w_clear"], 1)
            for dst, src in (
                    (wp_sb[:, :, :], wp), (win_sb[:, :, :], win),
                    (wout01[:, :], wout[0:128, :]), (wout2[0:64, 0, :], wout[128:DI, :]), (wout2[64:128, 1, :], wout[128:DI, :]),
                    (dt_w[96:96 + R, :, 0, :], dtproj[:, :, 0:128]), (dt_w[96:96 + R, :, 1, 0:64], dtproj[:, :, 128:DI]),
                    (dt_w[96:96 + R, :, 2, 64:128], dtproj[:, :, 128:DI])):
                sp.dma_start(dst, src).then_inc(s["late_weights_in"], 16)

            sp.dma_start(x_in[:, :, :], x_pair[0]).then_inc(s["xin_ready"], 16)

            def load_x(i):
                sp.wait_ge(s["xin_ready"], i * 16)
                sp.dma_start(flat(x_in), dram(x_pair, i)).then_inc(s["xin_ready"], 16)

            def spill_z(i):
                sp.wait_ge(s["z_ready"], i * 2 + 2)
                sp.dma_start(dram(z_dram, i), z_out[:, :]).then_inc(s["z_spilled"], 16)

            def spill_xc(i):
                sp.wait_ge(s["xc_ready"], i * 2 + 2)
                sp.dma_start(dram(xc_dram, i), xc_out[:, :]).then_inc(s["xc_spilled"], 16)

            def spill_a(i):
                sp.wait_ge(s["x1_ready"], i + 1)
                sp.wait_ge(s["x1_spilled"], i * 16)
                sp.dma_start(dram(x1_dram, i), flat(x1)).then_inc(s["x1_spilled"], 16)

            sp.wait_ge(s["x1_ready"], 1)
            sp.dma_start(dram(x1_dram, 0), flat(x1)).then_inc(s["x1_spilled"], 16)
            load_x(1)
            spill_a(1)
            spill_z(0)
            with sp.Fori(2, PAIRS) as i:
                load_x(i)
                spill_a(i)
                spill_xc(i - 2)
                spill_z(i - 1)
            spill_xc(PAIRS - 2)
            sp.wait_ge(s["yproj_ready"], PAIRS)
            sp.wait_ge(s["xc_spilled"], 16 * (PAIRS - 1))
            sp.dma_start(xc, dram(xc_dram, 0)).then_inc(s["xc_loaded"], 16)
            spill_z(PAIRS - 1)
            spill_xc(PAIRS - 1)
            sp.dma_start(dram(xc_dram, PAIRS), xc_out[:, :]).then_inc(s["xc_dup"], 16)
            sp.wait_ge(s["xc_dup"], 16)

            sp.wait_ge(s["xc_spilled"], 16 * PAIRS)
            sp.wait_ge(s["z_spilled"], 16 * PAIRS)
            sp.wait_ge(s["x1_spilled"], 16 * PAIRS)

            def fin_loads(i):
                sp.dma_start(xc_fin, dram(xc_dram, i)).then_inc(s["fin_x"], 16)
                sp.dma_start(z_fin, dram(z_dram, i)).then_inc(s["fin_z"], 16)
                sp.dma_start(flat(x1), dram(x1_dram, i)).then_inc(s["fin_x1"], 16)

            def next_x(i):
                sp.wait_ge(s["du_ready"], i * 4 + 4)
                sp.dma_start(xc, dram(xc_dram, i + 1)).then_inc(s["xc_loaded"], 16)

            def store(i):
                sp.wait_ge(s["o_ready"], i * 3 + 3)
                sp.dma_start(dram(out, i), o_sb.rearrange("p a b -> p (a b)")).then_inc(s["out_stored"], 16)

            fin_loads(0)
            next_x(0)
            with sp.Fori(1, PAIRS) as i:
                store(i - 1)
                sp.wait_ge(s["out_stored"], i * 16)
                sp.wait_ge(s["fin_x"], i * 16)
                sp.wait_ge(s["fin_z"], i * 16)
                sp.wait_ge(s["fin_x1"], i * 16)
                fin_loads(i)
                next_x(i)
            store(PAIRS - 1)
            sp.wait_ge(s["out_stored"], 16 * PAIRS)

        @block.gpsimd
        def _(pool):
            pool.memset(dt_w[:, :, :, :], 0.0).then_inc(s["dt_w_clear"], 1)
            pool.memset(ident[:, :], 0.0).then_inc(s["ident0"], 1)
            pool.wait_ge(s["ident0"], 1)
            pool.affine_select(out=ident[:, :], in_=ident[:, :], compare_op=ALU.not_equal, fill=1.0, base=0,
                               pattern=[[-1, 128]], channel_multiplier=1).then_inc(s["ident_ready"], 1)
            g = gavg[:, :, :].rearrange("p k (g i) -> p k g i", i=GN)
            pool.memset(gavg[:, :, :], 1.0 / GN).then_inc(s["gavg_step"], 1)
            pool.wait_ge(s["gavg_step"], 1)
            pool.affine_select(out=g, in_=g, compare_op=ALU.is_ge, fill=0.0, base=0,
                               pattern=[[128, KC], [-GN, C // GN], [0, GN]], channel_multiplier=1
                               ).then_inc(s["gavg_step"], 1)
            pool.wait_ge(s["gavg_step"], 2)
            pool.affine_select(out=g, in_=g, compare_op=ALU.is_ge, fill=0.0, base=GN - 1,
                               pattern=[[-128, KC], [GN, C // GN], [0, GN]], channel_multiplier=-1
                               ).then_inc(s["gavg_step"], 1)
            pool.memset(neg_half[:, :], -0.5).then_inc(s["gavg_step"], 1)
            pool.memset(sel[:, :, :, :], 0.0).then_inc(s["sel_step"], 1)
            step = 1
            for part in range(3):
                for kind, lo, hi, img in ((0, 0, 128, 0), (1, 0, 128, 1), (2, 0, 64, 0), (2, 64, 128, 1)):
                    v = sel[:, :, kind, lo:hi]
                    pool.wait_ge(s["sel_step"], step)
                    pool.affine_select(out=v, in_=v, compare_op=ALU.not_equal, fill=1.0,
                                       base=-(32 * part + N * img), pattern=[[-1, N], [0, hi - lo]],
                                       channel_multiplier=1).then_inc(s["sel_step"], 1)
                    step += 1
            pool.memset(pad01[:, :, :], 0.0).then_inc(s["pad_zero"], 1)
            pool.memset(pad2[:, :, :], 0.0).then_inc(s["pad_zero"], 1)

            pool.wait_ge(s["a_rstd"], 1)

            def norm(t, p, first=False):
                if not first:
                    pool.wait_ge(s["x_ready"], t)
                pool.tensor_tensor(x_tmp[:, :], tok(t), gmean[:, :], ALU.subtract).then_inc(s["xs_tmp"], 1)
                pool.wait_ge(s["xs_tmp"], t + 1)
                if not first:
                    pool.wait_ge(s["xpart_done"], t - 1)
                pool.tensor_tensor(x_cur[:, p, :], x_tmp[:, :], grstd[:, :], ALU.mult).then_inc(s["x_ready"], 1)

            def tok(t):
                return arena[:, bass.ds(t * SEQ, SEQ)] if not isinstance(t, int) else arena[:, t * SEQ:(t + 1) * SEQ]

            def keep(t, p):
                pool.wait_ge(s["h_ready"], t + 2)
                pool.tensor_copy(tok(t), h_t[:, p, :]).then_inc(s["hist_done"], 1)

            norm(0, 0, True)
            pool.wait_ge(s["x_ready"], 1)
            norm(1, 1, True)
            with pool.Fori(0, T // 2 - 1) as i:
                for p in range(2):
                    norm(i * 2 + (p + 2), p)
                    keep(i * 2 + p, p)
            keep(T - 2, 0)
            keep(T - 1, 1)

            pool.wait_ge(s["gavg_step"], 4)

            def rstd_c(i):
                pool.wait_ge(s["gn_step"], i * 8 + 7)
                pool.tensor_tensor(grstd[:, 0:6], gsum[:, 0:6], neg_half[:, 0:6], ALU.pow
                    ).then_inc(s["rstd_ready"], 1)

            pool.wait_ge(s["hist_done"], T)
            rstd_c(0)
            with pool.Fori(1, PAIRS) as i:
                rstd_c(i)

            def small_parts(st, b):
                pool.wait_ge(s["xdbl_ready"], 2 * st + 2)
                pool.tensor_tensor(resid[0:96, :], xdbl[0:96, :], bcs[b][0:96, :], ALU.subtract
                    ).then_inc(s["resid_ready"], 1)
                pool.wait_ge(s["mid_ready"], 2 * st + 2)
                pool.tensor_tensor(bcs[b][64:96, :], resid[64:96, :], midt[64:96, :], ALU.subtract
                    ).then_inc(s["parts_ready"], 1)

            def deltas(st, k, b, early=False):
                pool.wait_ge(s["parts_ready"], st + 1)
                pool.wait_ge(s["soft_step"], 4 * st + 4)
                pool.tensor_tensor(poly, poly, soft, ALU.mult).then_inc(s["series_step"], 1)
                pool.wait_ge(s["series_step"], 2 * st + 1)
                pool.tensor_tensor(poly, poly, lnp, ALU.subtract).then_inc(s["series_step"], 1)
                pool.wait_ge(s["series_step"], 2 * st + 2)
                pool.tensor_tensor(lnp, lnp, relu, ALU.add).then_inc(s["log_ready"], 1)
                pool.wait_ge(s["choice_ready"], st + 1)
                pool.wait_ge(s["log_ready"], st + 1)
                if not early:
                    pool.wait_ge(s["decay_ready"], (st - 1) * GRP)
                pool.tensor_tensor(delta[b], lnp, poly, ALU.add).then_inc(s["delta_ready"], 1)
                pool.wait_ge(s["delta_ready"], st + 1)
                if not early:
                    pool.wait_ge(s["drive_ready"], (st - 1) * GRP)
                pool.tensor_tensor(du[b], delta[b], xt if k % 2 else xc, ALU.mult).then_inc(s["du_ready"], 1)

            pool.wait_ge(s["xc_loaded"], 16)
            small_parts(0, 0)
            deltas(0, 0, 0, True)

            def pair(i, head):
                for k in range(K4):
                    st = i * K4 + (k + 1)
                    small_parts(st, (k + 1) % 2)
                    deltas(st, (k + 1) % K4, (k + 1) % 2, head and k == 0)

            pair(0, True)
            with pool.Fori(1, PAIRS) as i:
                pair(i, False)

        @block.vector
        def _(dve):
            dve.memset(series_bias[:, :], -(3.0 ** 0.5) / 4.0).then_inc(s["const_ready"], 1)
            dve.memset(h_nat[:, :], 0.0).then_inc(s["const_ready"], 1)
            dve.memset(h_t[:, 1, :], 0.0).then_inc(s["h_ready"], 1)
            dve.memset(bc_w[:, :, :, :, :], 0.0).then_inc(s["bcw_step"], 1)
            dve.memset(avg[:, :, :], 0.0).then_inc(s["setup_step"], 1)
            dve.wait_ge(s["setup_step"], 1)
            dve.memset(avg[:, 0, :], 1.0 / DI).then_inc(s["setup_step"], 1)
            dve.memset(avg[0:64, 1, :], 1.0 / DI).then_inc(s["setup_step"], 1)
            dve.memset(avg[64:128, 2, :], 1.0 / DI).then_inc(s["setup_step"], 1)
            dve.memset(avg[0:64, 3, 0:64], 1.0 / DI).then_inc(s["setup_step"], 1)
            dve.memset(avg[64:128, 3, 64:128], 1.0 / DI).then_inc(s["setup_step"], 1)
            dve.memset(wout2[64:128, 0, :], 0.0).then_inc(s["setup_step"], 1)
            dve.memset(wout2[0:64, 1, :], 0.0).then_inc(s["setup_step"], 1)
            dve.memset(avg[:, 4, 0:64], 1.0 / DI).then_inc(s["setup_step"], 1)
            dve.memset(avg[:, 5, 64:128], 1.0 / DI).then_inc(s["setup_step"], 1)
            dve.wait_ge(s["params_in"], 16 * PARAM_LOADS)
            dve.wait_ge(s["bcw_step"], 1)
            stage = x1[:, :, :].rearrange("p a b -> p (a b)")
            n56 = K4 * (R + 2 * N)
            for rows, tile, img, col in ((slice(0, 128), 0, 0, 0), (slice(0, 128), 1, 1, 0),
                                         (slice(0, 64), 2, 0, n56), (slice(64, 128), 2, 1, n56)):
                src = stage[rows, col:col + n56].rearrange("p (k m) -> p k m", k=K4)
                rn = rows.stop - rows.start
                for bc in range(2):
                    dst = bc_w[rows, :, bc, tile, 0:96].rearrange("p k (q m) -> p k q m", q=3)[:, :, :, N * img:N * img + N]
                    dve.tensor_copy(dst, src[:, :, R + N * bc:R + N * bc + N].unsqueeze(2).broadcast_to([rn, K4, 3, N])
                                    ).then_inc(s["bcw_step"], 1)
                dve.tensor_copy(bc_w[rows, :, img, tile, 96:96 + R], src[:, :, 0:R]).then_inc(s["bcw_step"], 1)
            for at, from_x, from_h in ((0, 0, None), (CJ, CJ, 0), (2 * CJ, None, CJ), (G3, 2 * CJ, 2 * CJ)):
                dst = gru_bias[:, at:at + CJ]
                if from_h is None:
                    ins = dve.tensor_copy(dst, bias_x[:, from_x:from_x + CJ])
                elif from_x is None:
                    ins = dve.tensor_copy(dst, bias_h[:, from_h:from_h + CJ])
                else:
                    ins = dve.tensor_tensor(dst, bias_x[:, from_x:from_x + CJ], bias_h[:, from_h:from_h + CJ], ALU.add)
                ins.then_inc(s["bias_step"], 1)
            for src, dst, bias in ((par01, a01, abias01), (par2, a2, abias2)):
                src = src[:, P_AL:P_AL + K4 * N]
                dve.tensor_scalar(dst[:, :], src, A_LOG_MAX, None, ALU.min).then_inc(s["a_capped"], 1)
                dve.tensor_scalar(bias[:, :], src, A_LOG_MAX, -1e30, ALU.is_gt, ALU.mult
                    ).then_inc(s["a_capped"], 1)
            dve.wait_ge(s["setup_step"], 10)
            dve.wait_ge(s["ident_ready"], 1)
            dve.tensor_scalar(centring[:, :, :], avg[:, :, :], -1.0, None, ALU.mult
                ).then_inc(s["centring_step"], 1)
            dve.wait_ge(s["centring_step"], 1)
            for kind in (0, 3):
                dve.tensor_tensor(centring[:, kind, :], centring[:, kind, :], ident[:, :], ALU.add
                    ).then_inc(s["centring_step"], 1)
            dve.tensor_reduce(dsum01[:, :], par01[:, P_DS:P_DS + K4], mybir.AxisListType.X, ALU.add
                ).then_inc(s["setup_step"], 1)
            dve.tensor_reduce(dsum2[:, :], par2[:, P_DS:P_DS + K4], mybir.AxisListType.X, ALU.add
                ).then_inc(s["setup_step"], 1)
            dve.wait_ge(s["setup_step"], 12)
            for dst, dsum in ((skip01, dsum01), (skip2, dsum2)):
                dve.tensor_scalar(dst[:, :], ident[:, :], dsum[:, 0:1], None, ALU.mult).then_inc(s["skip_step"], 1)
            dve.wait_ge(s["a_exp"], 2)
            dve.tensor_scalar(a01[:, :], a01[:, :], -1.0, None, ALU.mult).then_inc(s["a_capped"], 1)
            dve.tensor_scalar(a2[:, :], a2[:, :], -1.0, None, ALU.mult).then_inc(s["a_capped"], 1)
            dve.wait_ge(s["a_capped"], 6)
            for dst, bias in ((a01, abias01), (a2, abias2)):
                dve.scalar_tensor_tensor(dst[:, :], bias[:, :], 0.0, dst[:, :], ALU.is_equal, ALU.mult
                    ).then_inc(s["setup_step"], 1)

            for h in range(2):
                dve.wait_ge(s[f"xload{h}"], 16)
                tokens = seq[:, h * HALF:(h + 1) * HALF, :].rearrange("p t (c u) -> p t c u", u=UNROLL)
                halves = stats[:, :, 2 * h:2 * h + 2, :].rearrange("p (c u) a b -> p c u (a b)", u=UNROLL)
                with dve.Fori(0, SEQ // UNROLL) as c:
                    for u in range(UNROLL):
                        dve.bn_stats(halves[:, bass.ds(c, 1), u, :].rearrange("p c x -> p (c x)"),
                                     tokens[:, :, bass.ds(c, 1), u].rearrange("p t c -> p (t c)")
                                     ).then_inc(s["st_done"], 1)
            dve.wait_ge(s["st_done"], 2 * SEQ)
            dve.tensor_reduce(gsum[:, :], stats[:, :, :, 1], mybir.AxisListType.X, ALU.add
                ).then_inc(s["a_gn"], 1)
            dve.wait_ge(s["a_g1"], 1)
            dve.tensor_scalar(gmean[:, :], ps[:, 2, 0:SEQ], 0.25, None, ALU.mult).then_inc(s["a_gn"], 1)
            dve.wait_ge(s["a_gn"], 2)
            dve.tensor_tensor(dev[:, :, :], stats[:, :, :, 1], gmean[:, :].unsqueeze(2).broadcast_to([128, SEQ, 4]),
                              ALU.subtract).then_inc(s["a_gn"], 1)
            dve.wait_ge(s["a_gn"], 3)
            dve.tensor_tensor(dev[:, :, :], dev[:, :, :], dev[:, :, :], ALU.mult).then_inc(s["a_gn"], 1)
            dve.wait_ge(s["a_gn"], 4)
            dve.scalar_tensor_tensor(dev[:, :, :], dev[:, :, :], float(T // 4), stats[:, :, :, 2], ALU.mult, ALU.add
                                     ).then_inc(s["a_gn"], 1)
            dve.wait_ge(s["a_gn"], 5)
            dve.tensor_reduce(gsum[:, :], dev[:, :, :], mybir.AxisListType.X, ALU.add).then_inc(s["a_gn"], 1)
            dve.wait_ge(s["a_g2"], 1)
            dve.tensor_scalar(gsum[:, :], ps[:, 3, 0:SEQ], 1.0 / T, EPS, ALU.mult, ALU.add
                ).then_inc(s["a_gn"], 1)

            dve.wait_ge(s["a_std"], 1)
            dve.reciprocal(grstd[:, :], gsum[:, :]).then_inc(s["a_rstd"], 1)

            bias_of_n = gru_bias[:, 0:G3].rearrange("p (a c) -> p a c", a=3)[:, 0:3:2, :]

            def step(t, p, first=False):
                dve.wait_ge(s["r_pre_ready"], t + 1)
                dve.tensor_tensor(r_pre[:, :], ps[:, p, CJ:2 * CJ], gru_bias[:, CJ:2 * CJ], ALU.add
                    ).then_inc(s["r_biased"], 1)
                if not first:
                    dve.wait_ge(s["hist_done"], t - 1)
                dve.tensor_tensor(n_parts[:, :, :], ps[:, p, 0:G3].rearrange("p (a c) -> p a c", a=3)[:, 0:3:2, :], bias_of_n,
                                  ALU.add).then_inc(s["n_biased"], 1)
                dve.wait_ge(s["r_ready"], t + 1)
                dve.wait_ge(s["n_biased"], t + 1)
                dve.tensor_tensor(rh[:, :], r_gate[:, :], n_parts[:, 1, :], ALU.mult).then_inc(s["rh_ready"], 1)
                dve.wait_ge(s["z_pre_ready"], t + 1)
                dve.tensor_tensor(z_pre[:, :], ps[:, Z_BANK + p, 0:CJ], gru_bias[:, G3:4 * CJ], ALU.add
                    ).then_inc(s["z_biased"], 1)
                dve.wait_ge(s["rh_ready"], t + 1)
                dve.tensor_tensor(cand_pre[:, :], rh[:, :], n_parts[:, 0, :], ALU.add
                    ).then_inc(s["pre_ready"], 1)
                dve.wait_ge(s["z_gate_ready"], t + 1)
                dve.tensor_tensor(zh[:, :], z_gate[:, :], h_nat[:, :], ALU.mult).then_inc(s["mix_step"], 1)
                dve.wait_ge(s["tanh_ready"], t + 1)
                dve.scalar_tensor_tensor(blend[:, :], z_gate[:, :], -1.0, cand[:, :], ALU.add, ALU.mult
                    ).then_inc(s["mix_step"], 1)
                dve.wait_ge(s["mix_step"], t * 2 + 2)
                dve.tensor_tensor(h_nat[:, :], zh[:, :], blend[:, :], ALU.subtract).then_inc(s["hnat_ready"], 1)
                dve.wait_ge(s["hnat_ready"], t + 1)
                dve.transpose(h_t[:, p, :], h_nat[:, :]).then_inc(s["h_ready"], 1)

            dve.wait_ge(s["const_ready"], 2)
            dve.wait_ge(s["bias_step"], 4)
            step(0, 0, True)
            step(1, 1, True)
            with dve.Fori(1, T // 2) as i:
                for p in range(2):
                    step(i * 2 + p, p)

            st6 = stats[:, 0:KC * 2, 0:2, :]
            mean2 = st6[:, :, :, 1]
            dv = dev[:, 0:6, 0:2]

            def add_and_stats(i, first=False):
                dve.wait_ge(s["yproj_ready"], i + 1)
                dve.wait_ge(s["xin_ready"], i * 16 + 16)
                if not first:
                    dve.wait_ge(s["x1_spilled"], i * 16)
                    dve.wait_ge(s["xhat_ready"], i * 6)
                dve.tensor_tensor(x1[:, :, :], x_in[:, :, :], ps[:, 0:3, 0:T2], ALU.add
                    ).then_inc(s["x1_ready"], 1)
                dve.wait_ge(s["x1_ready"], i + 1)
                for kc in range(KC):
                    for b in range(2):
                        dve.bn_stats(st6[:, 2 * kc + b, :, :].rearrange("p a b -> p (a b)"),
                                     x1[:, kc, b * T:(b + 1) * T]).then_inc(s["stats_ready"], 1)
                dve.wait_ge(s["stats_ready"], i * 6 + 6)
                dve.tensor_tensor(gsum[:, 0:6], mean2[:, :, 0], mean2[:, :, 1], ALU.add
                    ).then_inc(s["gn_step"], 1)

            def deviations(i):
                dve.wait_ge(s["g1_ready"], i + 1)
                dve.tensor_scalar(gmean[:, 0:6], ps[:, 6, 0:6], 0.5, None, ALU.mult).then_inc(s["gn_step"], 1)
                dve.wait_ge(s["gn_step"], i * 8 + 2)
                dve.tensor_tensor(dv, mean2, gmean[:, 0:6].unsqueeze(2).broadcast_to([128, 6, 2]), ALU.subtract
                                  ).then_inc(s["gn_step"], 1)
                dve.wait_ge(s["gn_step"], i * 8 + 3)
                dve.tensor_tensor(dv, dv, dv, ALU.mult).then_inc(s["gn_step"], 1)
                dve.wait_ge(s["gn_step"], i * 8 + 4)
                dve.scalar_tensor_tensor(dv, dv, float(T // 2), st6[:, :, :, 2], ALU.mult, ALU.add
                    ).then_inc(s["gn_step"], 1)
                dve.wait_ge(s["gn_step"], i * 8 + 5)
                dve.tensor_tensor(gsum[:, 0:6], dv[:, :, 0], dv[:, :, 1], ALU.add).then_inc(s["gn_step"], 1)

            def variance(i):
                dve.wait_ge(s["g2_ready"], i + 1)
                dve.tensor_scalar(gsum[:, 0:6], ps[:, 7, 0:6], 1.0 / T, EPS, ALU.mult, ALU.add
                    ).then_inc(s["gn_step"], 1)

            def shift(i):
                dve.wait_ge(s["rstd_ready"], i + 1)
                dve.scalar_tensor_tensor(gmean[:, 0:6], gmean[:, 0:6], -1.0, grstd[:, 0:6], ALU.mult, ALU.mult
                                         ).then_inc(s["gn_step"], 1)

            def convolve(i, taps, first=False):
                if taps[0] == 0:
                    dve.wait_ge(s["pad_ready"], i * 2 + 2)
                    if not first:
                        dve.wait_ge(s["xc_ready"], i * 2)
                conv_taps(dve, i, taps)

            add_and_stats(0, True)
            deviations(0)
            variance(0)
            shift(0)

            def norm_and_convolve(i, first=False):
                add_and_stats(i)
                if not first:
                    convolve(i - 2, range(4, 6))
                deviations(i)
                if not first:
                    convolve(i - 2, range(6, 9))
                variance(i)
                convolve(i - 1, range(0, 2), first)
                shift(i)
                convolve(i - 1, range(2, 4))

            norm_and_convolve(1, True)
            with dve.Fori(2, PAIRS) as i:
                norm_and_convolve(i)
            convolve(PAIRS - 2, range(4, 9))
            convolve(PAIRS - 1, range(9))

            dve.wait_ge(s["yproj_ready"], PAIRS)
            for q in range(RING):
                for d in range(2):
                    z0 = da[d][q].rearrange("p (r t) -> p r t", t=T)
                    dve.memset(z0[:, :, 0:1] if d == 0 else z0[:, :, T - 1:T], 0.0).then_inc(s["d_zero"], 1)
            dve.wait_ge(s["d_zero"], 2 * RING)

            def drive(i, k, g, G, b, first=False):
                dux, bank, view = group_aps(g)
                q, _ = ring_of(k, g)
                if g == 0:
                    dve.wait_ge(s["du_ready"], i * K4 + (k + 1))
                dve.wait_ge(s["b_ready"], G + 1)
                if not first:
                    dve.wait_ge(s["reduced"], G - (RING - 1))
                dve.tensor_tensor(view(hb[q]), dux(du[b]), bank(0), ALU.mult).then_inc(s["drive_ready"], 1)

            def scan(k, g, G):
                q, dec = ring_of(k, g)
                dve.wait_ge(s["drive_ready"], G + 1)
                dve.wait_ge(s["decay_ready"], G + 1)
                st = hb[q]
                if k < 2:
                    dve.tensor_tensor_scan(st, dec, st, 0.0, ALU.mult, ALU.add).then_inc(s["scan_done"], 1)
                else:
                    dve.tensor_tensor_scan(st[:, ::-1], dec[:, ::-1], st[:, ::-1], 0.0, ALU.mult, ALU.add
                                           ).then_inc(s["scan_done"], 1)

            def read_out(k, g, G):
                _, bank, view = group_aps(g)
                q, _ = ring_of(k, g)
                dve.wait_ge(s["scan_done"], G + 1)
                dve.wait_ge(s["c_ready"], G + 1)
                dve.tensor_tensor(view(hb[q]), view(hb[q]), bank(2), ALU.mult).then_inc(s["readout_ready"], 1)

            def gate(i):
                dve.wait_ge(s["rstd2_step"], i * 3 + 3)
                dve.wait_ge(s["fin_z"], i * 16 + 16)
                for lo, hi, table in ((0, T2, par01), (T2, TC, par2)):
                    dve.scalar_tensor_tensor(yc[:, lo:hi], yc[:, lo:hi], table[:, P_G:P_G + 1], ysq[:, lo:hi],
                                             ALU.mult, ALU.mult).then_inc(s["norm_step"], 1)
                dve.wait_ge(s["norm_step"], i * 2 + 2)
                for lo, hi, table in ((0, T2, par01), (T2, TC, par2)):
                    dve.scalar_tensor_tensor(yc[:, lo:hi], yc[:, lo:hi], table[:, P_B:P_B + 1], z_fin[:, lo:hi],
                                             ALU.add, ALU.mult).then_inc(s["gated"], 1)

            def choose(st):
                dve.wait_ge(s["series_step"], 2 * st + 2)
                dve.scalar_tensor_tensor(poly, soft, SMALL, poly, ALU.is_lt, ALU.mult
                    ).then_inc(s["choice_ready"], 1)

            def pair(i, head):
                for k in range(K4):
                    for g in range(GRP):
                        G = i * (K4 * GRP) + (k * GRP + g)
                        scan(k, g, G)
                        k2, g2 = (k, g + 1) if g + 1 < GRP else (k + 1, 0)
                        if k2 < K4:
                            drive(i, k2, g2, G + 1, k2 % 2, head and k2 * GRP + g2 < RING)
                        else:
                            drive_next(i, G + 1)
                        read_out(k, g, G)
                        if g == (9 if k in (1, 2) else 8):
                            choose(i * K4 + (k + 1))
                        if not head:
                            if (k, g) == (1, 1):
                                gate(i - 1)

            def drive_next(i, G):
                dux, bank, view = group_aps(0)
                dve.wait_ge(s["du_ready"], i * K4 + (K4 + 1))
                dve.wait_ge(s["b_ready"], G + 1)
                dve.wait_ge(s["reduced"], G - (RING - 1))
                dve.tensor_tensor(view(hb[0]), dux(du[0]), bank(0), ALU.mult).then_inc(s["drive_ready"], 1)

            choose(0)
            drive(0, 0, 0, 0, 0, True)
            pair(0, True)
            with dve.Fori(1, PAIRS) as i:
                pair(i, False)
            gate(PAIRS - 1)

        @block.scalar
        def _(act):
            act.wait_ge(s["a_capped"], 4)
            act.activation(a01[:, :], a01[:, :], ACT.Exp).then_inc(s["a_exp"], 1)
            act.activation(a2[:, :], a2[:, :], ACT.Exp).then_inc(s["a_exp"], 1)

            act.preload_act_table_set("sqrt_and_others")
            act.wait_ge(s["a_gn"], 7)
            act.activation(gsum[:, :], gsum[:, :], ACT.Sqrt).then_inc(s["a_std"], 1)

            act.preload_act_table_set("sigmoid_and_others")

            def step(t, p):
                act.wait_ge(s["r_biased"], t + 1)
                act.activation(r_gate[:, :], r_pre[:, :], ACT.Sigmoid).then_inc(s["r_ready"], 1)
                act.wait_ge(s["z_biased"], t + 1)
                act.activation(z_gate[:, :], z_pre[:, :], ACT.Sigmoid).then_inc(s["z_gate_ready"], 1)
                act.wait_ge(s["pre_ready"], t + 1)
                act.activation(cand[:, :], cand_pre[:, :], ACT.Tanh).then_inc(s["tanh_ready"], 1)

            with act.Fori(0, T // 2) as i:
                for p in range(2):
                    step(i * 2 + p, p)

            def xh_and_z(i, first=False):
                act.wait_ge(s["inproj_whole"], i + 1)
                if not first:
                    act.wait_ge(s["conv01_step"], i * 9)
                    act.wait_ge(s["conv2_step"], i * 9)
                    act.wait_ge(s["z_spilled"], i * 16)
                act.activation(two_images(pad01[:, 1:2 * H + 3, :])[:, :, :, 1:W + 1],
                               ps[:, 3, 0:T2].rearrange("p (b h w) -> p b h w", b=2, h=H), ACT.Copy
                               ).then_inc(s["pad_ready"], 1)
                act.activation(z_out[:, 0:T2], ps[:, 5, 0:T2], ACT.Silu).then_inc(s["z_ready"], 1)
                act.wait_ge(s["inproj_ready"], i + 1)
                act.activation(pad2[:, 1:H + 1, 1:W + 1],
                               ps[:, 4, 0:T].rearrange("p (h w) -> p h w", h=H), ACT.Copy
                                   ).then_inc(s["pad_ready"], 1)
                act.activation(z_out[:, T2:TC], ps[:, 4, T:T2], ACT.Silu).then_inc(s["z_ready"], 1)

            def conv_silu(i, first=False):
                if not first:
                    act.wait_ge(s["xc_spilled"], i * 16)
                act.wait_ge(s["conv2_step"], i * 9 + 9)
                act.activation(xc_out[:, T2:TC], conv2_out[:, :, :].rearrange("p h w -> p (h w)"), ACT.Silu
                    ).then_inc(s["xc_ready"], 1)
                act.wait_ge(s["conv01_step"], i * 9 + 9)
                act.activation(xc_out[:, 0:T2].rearrange("p (b h w) -> p b h w", b=2, h=H), two_images(conv01_out[:, :, :]), ACT.Silu
                    ).then_inc(s["xc_ready"], 1)

            def normalise(i, first=False):
                act.wait_ge(s["gn_step"], i * 8 + 8)
                if not first:
                    act.wait_ge(s["inproj_ready"], i)
                for c in range(6):
                    v = (slice(None), c // 2, slice(c % 2 * T, c % 2 * T + T))
                    act.activation(xhat[v], x1[v], ACT.Identity, scale=grstd[:, c:c + 1], bias=gmean[:, c:c + 1]
                                   ).then_inc(s["xhat_ready"], 1)

            act.wait_ge(s["pad_zero"], 2)
            act.preload_act_table_set("silu_and_others")
            normalise(0, True)
            xh_and_z(0, True)
            normalise(1)
            conv_silu(0, True)
            xh_and_z(1)
            normalise(2)
            with act.Fori(3, PAIRS) as i:
                conv_silu(i - 2)
                xh_and_z(i - 1)
                normalise(i)
            conv_silu(PAIRS - 2)
            xh_and_z(PAIRS - 1)


            def turn(i):
                act.wait_ge(s["xc_loaded"], i * 16 + 16)
                act.activation(xt.rearrange("p (r w h) -> p r h w", r=3, w=W),
                               xc.rearrange("p (r h w) -> p r h w", r=3, h=H), ACT.Copy
                                   ).then_inc(s["xt_ready"], 1)

            def read_bc(st, b, first=False, second=False):
                act.wait_ge(s["bc_ready"], 2 * st + 2)
                if not first:
                    act.wait_ge(s["dt_ready"], 2 * st)
                    act.wait_ge(s["parts_ready"], st)
                if not first and not second:
                    act.wait_ge(s["c_ready"], (st - 1) * GRP)
                act.activation(xdbl[:, :], ps[:, 6, 0:T2], ACT.Copy).then_inc(s["xdbl_ready"], 1)
                act.activation(bcs[b][0:96, :], ps[0:96, 6, 0:T2], ACT.Copy).then_inc(s["xdbl_ready"], 1)

            def mid_parts(st, b):
                act.wait_ge(s["resid_ready"], st + 1)
                act.activation(bcs[b][32:64, :], resid[32:64, :], ACT.Copy).then_inc(s["mid_ready"], 1)
                act.activation(midt[64:96, :], resid[64:96, :], ACT.Copy).then_inc(s["mid_ready"], 1)

            def softplus(st, k, first=False):
                act.wait_ge(s["dt_ready"], 2 * st + 2)
                if not first:
                    act.wait_ge(s["delta_ready"], st)
                for lo, hi, bank, table in ((0, T2, 7, par01), (T2, TC, 6, par2)):
                    bias = table[:, P_DTB + k:P_DTB + k + 1]
                    act.activation(soft[:, lo:hi], ps[:, bank, 0:hi - lo], ACT.Abs, bias=bias
                        ).then_inc(s["dt_read"], 1)
                    act.activation(relu[:, lo:hi], ps[:, bank, 0:hi - lo], ACT.Relu, bias=bias
                        ).then_inc(s["dt_read"], 1)

            def series(st):
                act.wait_ge(s["dt_read"], 4 * st + 4)
                act.activation(soft, soft, ACT.Exp, scale=-1.0).then_inc(s["soft_step"], 1)
                act.wait_ge(s["soft_step"], 4 * st + 1)
                act.activation(lnp, soft, ACT.Ln, bias=1.0).then_inc(s["soft_step"], 1)
                act.activation(poly, soft, ACT.Square, scale=3.0 ** -0.5, bias=series_bias[:, 0:1]
                    ).then_inc(s["soft_step"], 1)
                act.wait_ge(s["soft_step"], 4 * st + 3)
                act.activation(poly, poly, ACT.Copy, bias=13.0 / 16.0).then_inc(s["soft_step"], 1)

            def decays(i, k, g, G, b, first=False):
                _, dec = ring_of(k, g)
                r = dec.rearrange("p (r t) -> p r t", t=T)
                lo = 1 if k < 2 else 0
                if g == 0:
                    act.wait_ge(s["delta_ready"], i * K4 + (k + 1))
                if not first:
                    act.wait_ge(s["scan_done"], G - (RING - 1))
                if g < 8:
                    src = delta[b][:, 0:T2].rearrange("p (r t) -> p r t", r=2)[:, :, lo:lo + T - 1]
                    for m in range(2):
                        n = 2 * g + m
                        ins = act.activation(r[:, 2 * m:2 * m + 2, lo:lo + T - 1], src, ACT.Exp,
                                             scale=a01[:, k * N + n:k * N + n + 1], bias=abias01[:, k * N + n:k * N + n + 1])
                else:
                    for m in range(4):
                        n = 4 * (g - 8) + m
                        ins = act.activation(r[:, m, lo:lo + T - 1], delta[b][:, T2 + lo:T2 + lo + T - 1], ACT.Exp,
                                             scale=a2[:, k * N + n:k * N + n + 1], bias=abias2[:, k * N + n:k * N + n + 1])
                ins.then_inc(s["decay_ready"], 1)

            def drain(i):
                act.wait_ge(s["reduced"], (i + 1) * (K4 * GRP))
                act.activation(ysb[:, 0:T2], ps[:, 4, 0:T2], ACT.Copy).then_inc(s["y_drained"], 1)
                act.activation(ysb[:, T2:TC], ps[:, 5, 0:T], ACT.Copy).then_inc(s["y_drained"], 1)

            def square(i):
                act.wait_ge(s["centred"], i * 2 + 2)
                act.activation(yc[:, 0:T2], ps[:, 6, 0:T2], ACT.Copy).then_inc(s["yc_ready"], 1)
                act.activation(yc[:, T2:TC], ps[:, 7, 0:T], ACT.Copy).then_inc(s["yc_ready"], 1)
                act.wait_ge(s["yc_ready"], i * 2 + 2)
                act.activation(ysq, yc, ACT.Square).then_inc(s["ysq_ready"], 1)

            def result(i, oc):
                act.wait_ge(s["oproj_ready"], i * 3 + (oc + 1))
                act.activation(o_sb[:, oc, :], ps[:, 6 + oc % 2, 0:T2], ACT.Copy).then_inc(s["o_ready"], 1)

            def rstd(i):
                act.wait_ge(s["var_ready"], i * 2 + 2)
                act.activation(ysq[:, 0:T2], ps[:, 6, 0:T2], ACT.Ln, bias=EPS
                               ).then_inc(s["rstd2_step"], 1)
                act.activation(ysq[:, T2:TC], ps[:, 7, 0:T], ACT.Ln, bias=EPS).then_inc(s["rstd2_step"], 1)
                act.wait_ge(s["rstd2_step"], i * 3 + 2)
                act.activation(ysq, ysq, ACT.Exp, scale=-0.5).then_inc(s["rstd2_step"], 1)

            RESULTS = ((1, 9), (1, 11), (2, 1))

            def pair(i, head):
                for k in range(K4):
                    st = i * K4 + (k + 1)
                    kn, b = (k + 1) % K4, (k + 1) % 2
                    g0 = 1 if k in (1, 2) else 0
                    for g in range(GRP):
                        decays(i, k, g, i * (K4 * GRP) + (k * GRP + g), k % 2, head and k * GRP + g < RING)
                        if g == g0 + 3:
                            read_bc(st, b, second=head and k == 0)
                        if g == g0 + 4:
                            mid_parts(st, b)
                        if g == g0 + 6:
                            softplus(st, kn)
                        if g == g0 + 7:
                            series(st)
                        if not head:
                            if (k, g) == (0, 2):
                                drain(i - 1)
                            if (k, g) == (0, 10):
                                square(i - 1)
                            if (k, g) == (1, 1):
                                rstd(i - 1)
                            if (k, g) in RESULTS:
                                result(i - 1, RESULTS.index((k, g)))
                        if k == 3 and g == 9:
                            turn(i + 1)

            turn(0)
            read_bc(0, 0, True)
            mid_parts(0, 0)
            softplus(0, 0, True)
            conv_silu(PAIRS - 1)
            act.preload_act_table_set("natural_log_exp_and_others")
            series(0)
            act.wait_ge(s["setup_step"], 14)
            act.wait_ge(s["d_zero"], 2 * RING)
            pair(0, True)
            with act.Fori(1, PAIRS) as i:
                pair(i, False)
            drain(PAIRS - 1)
            square(PAIRS - 1)
            rstd(PAIRS - 1)
            for oc in range(KC):
                result(PAIRS - 1, oc)

        @block.tensor
        def _(pe):
            def group_average(src, bank, cols, done):
                for oc in range(KC):
                    ks = [k for k in range(KC) if abs(k - oc) < 2]
                    for k in ks:
                        mm = pe.matmul(ps[:, bank, oc * cols:(oc + 1) * cols], gavg[:, k, oc * 128:(oc + 1) * 128],
                                       src[:, k * cols:(k + 1) * cols], start=(k == ks[0]), stop=(k == ks[-1]))
                mm.then_inc(done, 1)

            pe.wait_ge(s["gavg_step"], 3)
            pe.wait_ge(s["a_gn"], 1)
            group_average(gsum, 2, B, s["a_g1"])
            pe.wait_ge(s["a_gn"], 6)
            group_average(gsum, 3, B, s["a_g2"])

            def x_part(p):
                for bank, lo, hi in ((p, 0, 2 * CJ), (Z_BANK + p, 2 * CJ, G3)):
                    for k in range(KC):
                        for j in range(NJ):
                            mm = pe.matmul(ps[32 * j:32 * j + 32, bank, 0:hi - lo], x_cur[:, p, 32 * k:32 * k + 32],
                                           wx_sb[:, k, j, lo:hi], start=(k == 0), stop=False)
                mm.then_inc(s["xpart_done"], 1)

            def h_part(p):
                def part(bank, at, k, lo, hi):
                    for j in range(NJ):
                        mm = pe.matmul(ps[32 * j:32 * j + 32, bank, at:at + hi - lo], h_t[:, 1 - p, 32 * k:32 * k + 32],
                                       wh_sb[:, k, j, lo:hi], start=False, stop=(k == KC - 1))
                    return mm

                part(p, CJ, 0, 0, CJ)
                part(p, 2 * CJ, 0, CJ, 2 * CJ)
                part(p, CJ, 1, 0, 2 * CJ)
                part(p, CJ, 2, 0, 2 * CJ).then_inc(s["r_pre_ready"], 1)
                part(Z_BANK + p, 0, 0, 2 * CJ, G3)
                part(Z_BANK + p, 0, 1, 2 * CJ, G3)
                part(Z_BANK + p, 0, 2, 2 * CJ, G3).then_inc(s["z_pre_ready"], 1)

            pe.wait_ge(s["gru_weights_in"], 32)
            pe.wait_ge(s["const_ready"], 2)
            pe.wait_ge(s["x_ready"], 1)
            x_part(0)

            def step(t, p, last=False):
                pe.wait_ge(s["h_ready"], t + 1)
                h_part(p)
                if not last:
                    pe.wait_ge(s["x_ready"], t + 2)
                    x_part(1 - p)

            with pe.Fori(0, T // 2 - 1) as i:
                for p in range(2):
                    step(i * 2 + p, p)
            step(T - 2, 0)
            step(T - 1, 1, True)

            def y_proj(i, first=False):
                if not first:
                    pe.wait_ge(s["x1_ready"], i)
                for oc in range(KC):
                    for k in range(KC):
                        col = i * 2 + k * 32
                        rhs = seq[:, :, col:col + 2] if isinstance(i, int) else seq[:, :, bass.ds(col, 2)]
                        mm = pe.matmul(ps[:, oc, 0:T2].rearrange("p (b t) -> p b t", b=2), wp_sb[:, k, oc * 128:(oc + 1) * 128],
                                       rhs.rearrange("p t b -> p b t"), start=(k == 0), stop=(k == KC - 1))
                mm.then_inc(s["yproj_ready"], 1)

            def in_proj_whole(i, first=False):
                pe.wait_ge(s["xhat_ready"], i * 6 + 6)
                if not first:
                    pe.wait_ge(s["z_ready"], i * 2)
                    pe.wait_ge(s["pad_ready"], i * 2)
                for bank, lo in ((3, 0), (5, DI)):
                    for k in range(KC):
                        mm = pe.matmul(ps[:, bank, 0:T2], win_sb[:, k, lo:lo + 128], xhat[:, k, :], start=(k == 0), stop=(k == KC - 1))
                mm.then_inc(s["inproj_whole"], 1)

            def in_proj_halves(i):
                for col, lo in ((0, 128), (T, DI + 128)):
                    for k in range(KC):
                        for b in range(2):
                            mm = pe.matmul(ps[64 * b:64 * b + 64, 4, col:col + T], win_sb[:, k, lo:lo + 64],
                                           xhat[:, k, b * T:(b + 1) * T], start=(k == 0), stop=(k == KC - 1))
                mm.then_inc(s["inproj_ready"], 1)

            def mean_sums(i):
                pe.wait_ge(s["gn_step"], i * 8 + 1)
                group_average(gsum, 6, 2, s["g1_ready"])

            def var_sums(i):
                pe.wait_ge(s["gn_step"], i * 8 + 6)
                group_average(gsum, 7, 2, s["g2_ready"])

            pe.wait_ge(s["hist_done"], T)
            def project(i, first=False):
                y_proj(i)
                in_proj_whole(i - 1, first)
                mean_sums(i)
                in_proj_halves(i - 1)
                var_sums(i)

            pe.wait_ge(s["late_weights_in"], 16 * LATE_LOADS)
            y_proj(0, True)
            mean_sums(0)
            var_sums(0)
            project(1, True)
            with pe.Fori(2, PAIRS) as i:
                project(i)
            in_proj_whole(PAIRS - 1)
            in_proj_halves(PAIRS - 1)

            def bc_proj(i, k, st, bc, first=False):
                x = xt if k % 2 else xc
                if bc == 0:
                    pe.wait_ge(s["xc_loaded"], i * 16 + 16)
                    if k % 2:
                        pe.wait_ge(s["xt_ready"], i + 1)
                    if not first:
                        pe.wait_ge(s["dt_read"], 4 * st)
                for tile in range(3):
                    mm = pe.matmul(ps[:, 6, bc * T:(bc + 1) * T], bc_w[:, k, bc, tile, :], x[:, tile * T:(tile + 1) * T],
                                   start=(tile == 0), stop=(tile == 2))
                mm.then_inc(s["bc_ready"], 1)

            def dt_proj(k, st, part):
                if part == 0:
                    pe.wait_ge(s["xdbl_ready"], 2 * st + 2)
                    pe.matmul(ps[:, 7, 0:T2], dt_w[:, k, 0, :], xdbl[:, :], start=True, stop=True
                        ).then_inc(s["dt_ready"], 1)
                else:
                    pe.matmul(ps[:, 6, 0:T], dt_w[:, k, 1, :], xdbl[:, 0:T], start=True, stop=False)
                    pe.matmul(ps[:, 6, 0:T], dt_w[:, k, 2, :], xdbl[:, T:T2], start=False, stop=True
                        ).then_inc(s["dt_ready"], 1)

            def spread(g, part, bank, b, done):
                rhs = bcs[b][0:96, part * T:(part + 1) * T]
                for m in range(4):
                    n, kind = (2 * g + m // 2, m % 2) if g < 8 else (4 * (g - 8) + m, 2)
                    mm = pe.matmul(ps[:, bank + m // 2, m % 2 * T:m % 2 * T + T], sel[:, n, kind, :], rhs, start=True, stop=True)
                mm.then_inc(done, 1)

            def reduce(k, g, G, start, stop):
                q, _ = ring_of(k, g)
                runs = 2 if g < 8 else 4
                pe.wait_ge(s["readout_ready"], G + 1)
                for m in range(runs):
                    cols = GC // runs
                    bank = 4 if g < 8 else 5
                    src = hb[q][:, m * cols:(m + 1) * cols]
                    dst = ps[:, bank, 0:cols]
                    if k % 2:
                        src = src.rearrange("p (r w h) -> p r h w", w=W, h=H)
                        dst = dst.rearrange("p (r h w) -> p r h w", h=H, w=W)
                    mm = pe.matmul(dst, ident[:, :], src, start=(start and m == 0), stop=(stop and m == runs - 1))
                mm.then_inc(s["reduced"], 1)

            def skip(i):
                pe.wait_ge(s["fin_x"], i * 16 + 16)
                pe.matmul(ps[:, 4, 0:T2], skip01[:, :], xc_fin[:, 0:T2], start=False, stop=True)
                pe.matmul(ps[:, 5, 0:T], skip2[:, :], xc_fin[:, T2:TC], start=False, stop=False)

            def first_of_pair(k, g):
                return k == 0 and g in (0, 8)

            def over_channels(weights, src, part, done):
                if part == 0:
                    pe.matmul(ps[:, 6, 0:T2], weights[:, 0, :], src[:, 0:T2], start=True, stop=False)
                    pe.matmul(ps[:, 6, 0:T], weights[:, 1, :], src[:, T2:TC], start=False, stop=False)
                    pe.matmul(ps[:, 6, T:T2], weights[:, 2, :], src[:, T2:TC], start=False, stop=True
                        ).then_inc(done, 1)
                else:
                    pe.matmul(ps[:, 7, 0:T], weights[:, 3, :], src[:, T2:TC], start=True, stop=False)
                    pe.matmul(ps[:, 7, 0:T], weights[:, 4, :], src[:, 0:T], start=False, stop=False)
                    pe.matmul(ps[:, 7, 0:T], weights[:, 5, :], src[:, T:T2], start=False, stop=True
                        ).then_inc(done, 1)

            def centre(i, part, dt_reads):
                if part == 0:
                    pe.wait_ge(s["y_drained"], i * 2 + 2)
                    pe.wait_ge(s["dt_read"], dt_reads)
                over_channels(centring, ysb, part, s["centred"])

            def var(i, part):
                if part == 0:
                    pe.wait_ge(s["ysq_ready"], i + 1)
                over_channels(avg, ysq, part, s["var_ready"])

            def out_proj(i, oc):
                bank = 6 + oc % 2
                pe.wait_ge(s["gated"], i * 2 + 2)
                if oc == 2:
                    pe.wait_ge(s["o_ready"], i * 3 + 1)
                c = slice(oc * 128, (oc + 1) * 128)
                pe.matmul(ps[:, bank, 0:T2], wout01[:, c], yc[:, 0:T2], start=True, stop=False)
                for b in range(2):
                    pe.matmul(ps[:, bank, b * T:(b + 1) * T], wout2[:, b, c], yc[:, T2:TC], start=False, stop=False)

            def residual(i, oc):
                if oc == 0:
                    pe.wait_ge(s["fin_x1"], i * 16 + 16)
                pe.matmul(ps[:, 6 + oc % 2, 0:T2], ident[:, :], x1[:, oc, :], start=False, stop=True
                    ).then_inc(s["oproj_ready"], 1)

            def pair(i, head):
                for k in range(K4):
                    st = i * K4 + (k + 1)
                    inext, kn = (i, k + 1) if k + 1 < K4 else (i + 1, 0)
                    g0 = 1 if k in (1, 2) else 0
                    for g in range(GRP):
                        G = i * (K4 * GRP) + (k * GRP + g)
                        if g == GRP - 1:
                            pe.wait_ge(s["parts_ready"], st + 1)
                        pe.wait_ge(s["drive_ready"], G + 1)
                        spread((g + 1) % GRP, 0, 0, (k if g < GRP - 1 else k + 1) % 2, s["b_ready"])
                        if not (head and k == 0 and g == 0):
                            pe.wait_ge(s["readout_ready"], G)
                        spread(g, 1, 2, k % 2, s["c_ready"])
                        if (k, g) != (0, 0):
                            kp, gp = (k, g - 1) if g else (k - 1, GRP - 1)
                            if (kp, gp) == (0, 0) and not head:
                                pe.wait_ge(s["y_drained"], i * 2)
                            reduce(kp, gp, G - 1, first_of_pair(kp, gp), False)
                        elif not head:
                            reduce(K4 - 1, GRP - 1, G - 1, False, True)
                        if g in (g0, g0 + 1):
                            if g == g0 and not head:
                                if k == 1:
                                    pe.wait_ge(s["rstd2_step"], i * 3)
                                if k == 2:
                                    pe.wait_ge(s["o_ready"], i * 3)
                            bc_proj(inext, kn, st, g - g0)
                        if g in (g0 + 3, g0 + 4):
                            dt_proj(kn, st, g - g0 - 3)
                        if (k, g) == (3, 9):
                            skip(i)
                        if not head:
                            if k == 0 and g in (5, 6):
                                centre(i - 1, g - 5, 4 * st + 4)
                            if k == 0 and g in (9, 10):
                                var(i - 1, g - 9)
                            if k == 1 and g >= 6:
                                if g == 6:
                                    pe.wait_ge(s["dt_read"], 4 * st + 4)
                                (residual if g % 2 else out_proj)(i - 1, (g - 6) // 2)

            pe.wait_ge(s["bcw_step"], 13)
            pe.wait_ge(s["sel_step"], 13)
            pe.wait_ge(s["ident_ready"], 1)
            pe.wait_ge(s["gn_step"], 8 * PAIRS)
            pe.wait_ge(s["setup_step"], 14)
            pe.wait_ge(s["centring_step"], 3)
            pe.wait_ge(s["skip_step"], 2)
            for part in range(2):
                bc_proj(0, 0, 0, part, True)
            for part in range(2):
                dt_proj(0, 0, part)
            pe.wait_ge(s["z_ready"], 2 * PAIRS)
            pe.wait_ge(s["pad_ready"], 2 * PAIRS)
            pe.wait_ge(s["parts_ready"], 1)
            spread(0, 0, 0, 0, s["b_ready"])
            pair(0, True)
            with pe.Fori(1, PAIRS) as i:
                pair(i, False)
            reduce(K4 - 1, GRP - 1, PAIRS * K4 * GRP - 1, False, True)
            for part in range(2):
                centre(PAIRS - 1, part, 4 * (K4 * PAIRS + 1))
            for part in range(2):
                var(PAIRS - 1, part)
            for oc in range(KC):
                if oc == 0:
                    pe.wait_ge(s["rstd2_step"], 3 * PAIRS)
                out_proj(PAIRS - 1, oc)
                residual(PAIRS - 1, oc)


def dram(t, i):
    return t[i] if isinstance(i, int) else t[bass.ds(i, 1), :, :].rearrange("o p c -> (o p) c")


def flat(t):
    return t[:, :, :].rearrange("p a b -> p (a b)")


def kernel(**inputs):
    import numpy as np
    import concourse.bacc as bacc
    from concourse.bass_utils import run_bass_kernel_spmd as run

    a = {k: np.asarray(v) for k, v in inputs.items()}
    x = a["x"]
    lay = {
        "x_seq": x.reshape(B, T, KC, 128).transpose(3, 1, 2, 0).reshape(128, T, SEQ),
        "x_pair": x.reshape(PAIRS, 2, T, KC, 128).transpose(0, 4, 3, 1, 2).reshape(PAIRS, 128, KC * T2),
        "wx": a["L0_conv_Wx"].reshape(3, NJ, CJ, KC, 128)[[2, 1, 0]].transpose(4, 3, 1, 0, 2).reshape(128, KC, NJ, G3),
        "wh": a["L0_conv_Wh"].reshape(3, NJ, CJ, NJ, KC, 32)[[1, 2, 0]].transpose(3, 5, 4, 1, 0, 2).reshape(128, KC, NJ, G3),
        "bx": a["L0_conv_bx"].reshape(3, NJ, CJ)[[2, 1, 0]].transpose(1, 0, 2).reshape(NJ, G3),
        "bh": a["L0_conv_bh"].reshape(3, NJ, CJ)[[1, 2, 0]].transpose(1, 0, 2).reshape(NJ, G3),
        "wp": a["L0_conv_Wp"].reshape(C, NJ, KC, 32).transpose(1, 3, 2, 0).reshape(128, KC, C),
        "win": a["L1_conv_in_proj_w"].reshape(C, KC, 128).transpose(2, 1, 0),
        "par": np.concatenate([
            a["L1_conv_conv_w"].reshape(DI, 9), a["L1_conv_conv_b"].reshape(DI, 1), a["L1_conv_dt_projs_b"].T,
            a["L1_conv_A_logs"].reshape(K4, DI, N).transpose(1, 0, 2).reshape(DI, K4 * N),
            a["L1_conv_Ds"].reshape(K4, DI).T, a["L1_conv_out_norm_g"].reshape(DI, 1),
            a["L1_conv_out_norm_b"].reshape(DI, 1)], axis=1),
        "xproj": a["L1_conv_x_proj_w"].transpose(2, 0, 1).reshape(DI, K4 * (R + 2 * N)),
        "dtproj": a["L1_conv_dt_projs_w"].transpose(2, 0, 1),
        "wout": a["L1_conv_out_proj_w"].T,
    }
    nc = bacc.Bacc("TRN2", target_bir_lowering=False, num_devices=1)
    arrays, args = {}, []
    for name, v in lay.items():
        v = np.ascontiguousarray(v)
        arrays[name] = v
        args.append(nc.dram_tensor(name, v.shape, mybir.dt.from_np(v.dtype), kind="ExternalInput").ap())
    args.append(nc.dram_tensor("out_0", (PAIRS, 128, KC * T2), F32, kind="ExternalOutput").ap())
    build(nc, *args)
    r = run(nc, [arrays], core_ids=[0])
    o = r.results[0]["out_0"].reshape(PAIRS, 128, KC, 2, T)
    return o.transpose(0, 3, 4, 2, 1).reshape(B, H, W, C)
```
